# Optimizing a Trainium2 kernel written in Bass

```python
import numpy as np
import jax
import jax.numpy as jnp

def _softmax(x, axis=-1):
    return jax.nn.softmax(x, axis=axis)

def _gelu(x):
    return jax.nn.gelu(x, approximate=True)

def _silu(x):
    return jax.nn.silu(x)

def _sigmoid(x):
    return jax.nn.sigmoid(x)

def _layernorm(x, axis=-1, eps=1e-05):
    m = jnp.mean(x, axis=axis, keepdims=True)
    v = jnp.var(x, axis=axis, keepdims=True)
    return (x - m) / jnp.sqrt(v + eps)

def _scatter_add(tgt, idx, src, axis=0):
    return tgt.at[idx].add(src)

def _segment_sum(src, seg, n):
    return jax.ops.segment_sum(src, seg, n)
kernel_name = 'mk_sandwich_d1_jaxref_r2_9c4913'

def setup_inputs(seed: int=0):
    np.random.seed(seed)
    _w = jnp.asarray

    def _L0_attn_setup():
        import jax, jax.numpy as jnp
        import numpy as np
        B, L, D_IN, D_OUT, H = (4, 1024, 512, 512, 16)
        DH = D_OUT // H
        EPS = 1e-06

        def _rmsnorm(x, w):
            var = jnp.mean(jnp.square(x), axis=-1, keepdims=True)
            return x * jax.lax.rsqrt(var + EPS) * w
        key = jax.random.key(seed)
        ks = jax.random.split(key, 12)
        s_in = 1.0 / np.sqrt(D_IN)
        s_out = 1.0 / np.sqrt(D_OUT)
        return {'x': jax.random.normal(ks[0], (B, L, D_IN), jnp.float32), 'Wq': jax.random.normal(ks[1], (D_OUT, D_IN), jnp.float32) * s_in, 'Wk': jax.random.normal(ks[2], (D_OUT, D_IN), jnp.float32) * s_in, 'Wv': jax.random.normal(ks[3], (D_OUT, D_IN), jnp.float32) * s_in, 'Wg': jax.random.normal(ks[4], (D_OUT, D_IN), jnp.float32) * s_in, 'Wb': jax.random.normal(ks[5], (D_OUT, D_IN), jnp.float32) * s_in, 'Wa': jax.random.normal(ks[6], (H, D_IN), jnp.float32) * s_in, 'dt_bias': jnp.ones((H,), jnp.float32), 'A_log': jnp.log(jax.random.uniform(ks[7], (H,), jnp.float32, 0.001, 16.0)), 'norm_w': jnp.ones((DH,), jnp.float32), 'Wo': jax.random.normal(ks[8], (D_OUT, D_OUT), jnp.float32) * s_out, 'bo': jnp.zeros((D_OUT,), jnp.float32)}
    _L0_attn_in = _L0_attn_setup()

    def _L0_ffn_setup():
        import jax, jax.numpy as jnp
        import numpy as np
        NUM_COLUMNS = 16
        INPUT_DIM = 512
        NUM_NEURONS = 128
        SPARSITY = 0.05
        B, S = (4, 1024)

        def _l2norm(v, axis=-1, eps=1e-12):
            n = jnp.sqrt(jnp.sum(v * v, axis=axis, keepdims=True))
            return v / jnp.maximum(n, eps)
        key = jax.random.key(seed)
        ks = jax.random.split(key, 12)
        D, C, N = (INPUT_DIM, NUM_COLUMNS, NUM_NEURONS)
        inp = {'x': jax.random.normal(ks[0], (B, S, D), dtype=jnp.float32), 'col_emb': jax.random.normal(ks[1], (C, D), dtype=jnp.float32) * 0.02, 'gate_w1': jax.random.normal(ks[2], (D, D // 2), dtype=jnp.float32) / np.sqrt(D), 'gate_b1': jnp.zeros((D // 2,), dtype=jnp.float32), 'gate_w2': jax.random.normal(ks[3], (D // 2, C), dtype=jnp.float32) / np.sqrt(D // 2), 'gate_b2': jnp.zeros((C,), dtype=jnp.float32), 'W_cols': jax.random.normal(ks[4], (C, D, N), dtype=jnp.float32) / np.sqrt(D), 'b_cols': jnp.zeros((C, N), dtype=jnp.float32), 'proj_w': jax.random.normal(ks[5], (C * N, D), dtype=jnp.float32) / np.sqrt(C * N), 'proj_b': jnp.zeros((D,), dtype=jnp.float32), 'ln_g': jnp.ones((D,), dtype=jnp.float32), 'ln_b': jnp.zeros((D,), dtype=jnp.float32)}
        return inp
    _L0_ffn_in = _L0_ffn_setup()
    _d = {'L0_attn_x': _L0_attn_in['x'], 'L0_attn_Wq': _L0_attn_in['Wq'], 'L0_attn_Wk': _L0_attn_in['Wk'], 'L0_attn_Wv': _L0_attn_in['Wv'], 'L0_attn_Wg': _L0_attn_in['Wg'], 'L0_attn_Wb': _L0_attn_in['Wb'], 'L0_attn_Wa': _L0_attn_in['Wa'], 'L0_attn_dt_bias': _L0_attn_in['dt_bias'], 'L0_attn_A_log': _L0_attn_in['A_log'], 'L0_attn_norm_w': _L0_attn_in['norm_w'], 'L0_attn_Wo': _L0_attn_in['Wo'], 'L0_attn_bo': _L0_attn_in['bo'], 'L0_ffn_col_emb': _L0_ffn_in['col_emb'], 'L0_ffn_gate_w1': _L0_ffn_in['gate_w1'], 'L0_ffn_gate_b1': _L0_ffn_in['gate_b1'], 'L0_ffn_gate_w2': _L0_ffn_in['gate_w2'], 'L0_ffn_gate_b2': _L0_ffn_in['gate_b2'], 'L0_ffn_W_cols': _L0_ffn_in['W_cols'], 'L0_ffn_b_cols': _L0_ffn_in['b_cols'], 'L0_ffn_proj_w': _L0_ffn_in['proj_w'], 'L0_ffn_proj_b': _L0_ffn_in['proj_b'], 'L0_ffn_ln_g': _L0_ffn_in['ln_g'], 'L0_ffn_ln_b': _L0_ffn_in['ln_b']}
    _x0 = _d['L0_attn_x']
    _d['L0_attn_x'] = jax.random.normal(jax.random.fold_in(jax.random.key(seed), 1), (4, 2048, 512), dtype=_x0.dtype)
    del _x0
    return _d

def reference(L0_attn_x, L0_attn_Wq, L0_attn_Wk, L0_attn_Wv, L0_attn_Wg, L0_attn_Wb, L0_attn_Wa, L0_attn_dt_bias, L0_attn_A_log, L0_attn_norm_w, L0_attn_Wo, L0_attn_bo, L0_ffn_col_emb, L0_ffn_gate_w1, L0_ffn_gate_b1, L0_ffn_gate_w2, L0_ffn_gate_b2, L0_ffn_W_cols, L0_ffn_b_cols, L0_ffn_proj_w, L0_ffn_proj_b, L0_ffn_ln_g, L0_ffn_ln_b):

    def _L0_attn_ref(x, Wq, Wk, Wv, Wg, Wb, Wa, dt_bias, A_log, norm_w, Wo, bo):
        import jax, jax.numpy as jnp
        import numpy as np
        B, L, D_IN, D_OUT, H = (4, 1024, 512, 512, 16)
        DH = D_OUT // H
        EPS = 1e-06

        def _rmsnorm(x, w):
            var = jnp.mean(jnp.square(x), axis=-1, keepdims=True)
            return x * jax.lax.rsqrt(var + EPS) * w
        b, l, _ = x.shape
        q = (x @ Wq.T).reshape(b, l, H, DH)
        k = (x @ Wk.T).reshape(b, l, H, DH)
        v = (x @ Wv.T).reshape(b, l, H, DH)
        gate = (x @ Wg.T).reshape(b, l, H, DH)
        beta = jax.nn.sigmoid(x @ Wb.T).reshape(b, l, H, DH)
        alpha = jnp.exp(-jnp.exp(A_log)[None, None, :] * jax.nn.softplus(x @ Wa.T + dt_bias))
        q = q / jnp.linalg.norm(q, axis=-1, keepdims=True) / np.sqrt(DH)
        k = k / jnp.linalg.norm(k, axis=-1, keepdims=True)

        def step(S, inp):
            k_t, q_t, v_t, beta_t, a_t = inp
            S = S * a_t[..., None, None]
            kv_mem = jnp.einsum('bhd,bhde->bhe', k_t, S)
            delta = (v_t - kv_mem) * beta_t
            S = S + k_t[..., :, None] * delta[..., None, :]
            y_t = jnp.einsum('bhd,bhde->bhe', q_t, S)
            return (S, y_t)
        tfirst = lambda a: jnp.moveaxis(a, 1, 0)
        S0 = jnp.zeros((b, H, DH, DH), x.dtype)
        _, ys = jax.lax.scan(step, S0, (tfirst(k), tfirst(q), tfirst(v), tfirst(beta), tfirst(alpha)))
        ys = jnp.moveaxis(ys, 0, 1)
        ctx = _rmsnorm(ys, norm_w) * jax.nn.silu(gate)
        ctx = ctx.reshape(b, l, D_OUT)
        return ctx @ Wo.T + bo

    def _L0_ffn_ref(x, col_emb, gate_w1, gate_b1, gate_w2, gate_b2, W_cols, b_cols, proj_w, proj_b, ln_g, ln_b):
        import jax, jax.numpy as jnp
        import numpy as np
        NUM_COLUMNS = 16
        INPUT_DIM = 512
        NUM_NEURONS = 128
        SPARSITY = 0.05
        B, S = (4, 1024)

        def _l2norm(v, axis=-1, eps=1e-12):
            n = jnp.sqrt(jnp.sum(v * v, axis=axis, keepdims=True))
            return v / jnp.maximum(n, eps)
        Bq, Sq, D = x.shape
        C = col_emb.shape[0]
        similarity = jnp.einsum('bsd,cd->bsc', _l2norm(x), _l2norm(col_emb))
        h = jax.nn.gelu(x @ gate_w1 + gate_b1, approximate=False)
        gate_values = jax.nn.sigmoid(h @ gate_w2 + gate_b2)
        logits = similarity + gate_values
        k = max(1, int(C * SPARSITY))
        _, top_idx = jax.lax.top_k(logits, k)
        mask = jnp.sum(jax.nn.one_hot(top_idx, C, dtype=logits.dtype), axis=-2)
        weights = mask * jax.nn.softmax(logits, axis=-1)
        cols = jax.nn.gelu(jnp.einsum('bsd,cdn->bscn', x, W_cols) + b_cols, approximate=False)
        cols = cols * weights[..., None]
        combined = cols.reshape(Bq, Sq, -1)
        y = combined @ proj_w + proj_b + x
        mu = jnp.mean(y, axis=-1, keepdims=True)
        var = jnp.mean((y - mu) ** 2, axis=-1, keepdims=True)
        out = (y - mu) * jax.lax.rsqrt(var + 1e-05) * ln_g + ln_b
        return out
    x = L0_attn_x
    x = x + _layernorm(_L0_attn_ref(_layernorm(x, axis=-1), L0_attn_Wq, L0_attn_Wk, L0_attn_Wv, L0_attn_Wg, L0_attn_Wb, L0_attn_Wa, L0_attn_dt_bias, L0_attn_A_log, L0_attn_norm_w, L0_attn_Wo, L0_attn_bo), axis=-1)
    x = x + _layernorm(_L0_ffn_ref(_layernorm(x, axis=-1), L0_ffn_col_emb, L0_ffn_gate_w1, L0_ffn_gate_b1, L0_ffn_gate_w2, L0_ffn_gate_b2, L0_ffn_W_cols, L0_ffn_b_cols, L0_ffn_proj_w, L0_ffn_proj_b, L0_ffn_ln_g, L0_ffn_ln_b), axis=-1)
    return x

_drawn_inputs = setup_inputs


def setup_inputs(seed=0):
    import zlib

    import numpy as np

    out = dict(_drawn_inputs(seed))
    spreads = {'L0_attn_dt_bias': (1.0, 0.6),
     'L0_attn_norm_w': (1.0, 0.2),
     'L0_attn_bo': (0.0, 0.1),
     'L0_ffn_gate_b1': (0.0, 0.8),
     'L0_ffn_gate_b2': (0.0, 0.8),
     'L0_ffn_b_cols': (0.0, 0.8),
     'L0_ffn_proj_b': (0.0, 0.268),
     'L0_ffn_ln_g': (1.0, 0.2),
     'L0_ffn_ln_b': (0.0, 0.1)}
    factors = {'L0_ffn_col_emb': 8.0,
     'L0_ffn_gate_w1': 8.0,
     'L0_ffn_gate_w2': 8.0,
     'L0_ffn_W_cols': 8.0,
     'L0_ffn_proj_w': 8.0}
    for name, (base, spread) in spreads.items():
        noise = np.random.default_rng([zlib.crc32(name.encode()), seed]).standard_normal(out[name].shape)
        drawn = base * np.exp(spread * noise) if base else spread * noise
        out[name] = jnp.asarray(drawn.astype(out[name].dtype))
    for name, factor in factors.items():
        out[name] = (out[name] * factor).astype(out[name].dtype)
    return out
```

```python
import math
from contextlib import ExitStack

import concourse.bass as bass
from concourse import mybir

F32 = mybir.dt.float32
I32 = mybir.dt.int32
U32 = mybir.dt.uint32
ALU = mybir.AluOpType
ACT = mybir.ActivationFunctionType
AX = mybir.AxisListType

B, L, D = 4, 2048, 512
H, DH = 16, 32
P = 128
KD = D // P
HP = P // DH
T = 128
NT = L // T
C = DH
NC = T // C
CS = C // 2
G = KD * B
NP = 5
E, N = 16, 128
HID = 256
ROWS = B * L
XSW = D + 4
SHARE = ROWS + 2 * P
PADROW = E // 2 * SHARE
NM = ROWS // P + E - 1
NEG = -1.0e30

WID = [CS - 1 - s for s in range(CS - 1)]
OFF = [G * sum(WID[:s]) for s in range(CS - 1)]
PACKS = [(0, 1), (2, 3), (4, 5, 6), (7, 8, 9, 10, 11), (12, 13, 14)]
NPAIR = G * sum(WID)


class Chain:

    def __init__(self, eng, sem):
        self.eng, self.sem, self.n = eng, sem, 0

    def __call__(self, ins):
        self.n += 1
        ins.then_inc(self.sem, 1)
        self.eng.wait_ge(self.sem, self.n)

    def restart(self):
        self.eng.sem_inc(self.sem, -self.n)
        self.n = 0


def sandwich_kernel(nc, x, w_in, wa, dt_bias, a_log, norm_w, wo, bo, col_emb, gw1, gb1, gw2, gb2,
                    w_cols, b_cols, proj_w, proj_b, ln_g, ln_b,
                    c_sq, c_sel, c_mask, c_iota, c_pad, c_tok, c_row, c_col, out, xs_dram):
    with ExitStack() as ctx:
        def sb(name, shape, dt=F32):
            return ctx.enter_context(nc.sbuf_tensor(name, shape, dt))

        def ps(name, shape):
            return ctx.enter_context(nc.psum_tensor(name, shape, F32))

        def sem(name):
            return ctx.enter_context(nc.semaphore(name))

        squares = sb("squares", [P, 5, P])
        ident, blk1, ucum, ustrict, ones = (squares[:, i, :] for i in range(5))
        sel = sb("sel", [P, C, P])
        mask = sb("mask", [P, C])
        iota = sb("iota", [P, E])
        w_sb = sb("w_sb", [P, KD, NP * D])
        wa_sb = sb("wa_sb", [P, KD, H])
        dtb = sb("dtb", [P, H])
        neg_a = sb("neg_a", [P, H])
        nw = sb("nw", [P, 1])
        wo_sb = sb("wo_sb", [P, KD, D])
        bo_sb = sb("bo_sb", [P, D])
        gw1_sb = sb("gw1_sb", [P, KD, HID])
        gb1_sb = sb("gb1_sb", [P, HID // P])
        gw2_sb = sb("gw2_sb", [P, HID // P, E])
        gb2_sb = sb("gb2_sb", [P, E])
        ceT = sb("ceT", [P, KD, E])
        ce_s = sb("ce_s", [E, 4])
        eps5 = sb("eps5", [P, 1])
        eps6 = sb("eps6", [P, 1])
        lnq = sb("lnq", [P, 1])
        ln3 = sb("ln3", [P, 1])

        xt = sb("xt", [P, B, D])
        xn = sb("xn", [P, B, D])
        xT = sb("xT", [P, KD, B * T])
        stats = sb("stats", [P, B, 6])
        mv = sb("mv", [P, B, 2])
        ve = sb("ve", [P, B])
        rstd = sb("rstd", [P, B])
        nt1 = sb("nt1", [P, B])
        nmr = sb("nmr", [P, B])
        la = sb("la", [P, B, H])
        eg = sb("eg", [P, G, T])
        dec = sb("dec", [P, G, T])
        qraw = sb("qraw", [P, B * T])
        qsq = sb("qsq", [P, B * T])
        qr = sb("qr", [P, B * T])
        kq = sb("kq", [P, G, NC, 2, C])
        kqd = sb("kqd", [P, G, NC, 2, C])
        vT = sb("vT", [P, G, T])
        beta = sb("beta", [P, G, T])
        silu = sb("silu", [P, G, T])
        A = sb("A", [P, G, 2, C])
        kd = sb("kd", [P, G, C])
        kt = sb("kt", [P, G, C])
        pairs = [sb(f"pairs{j}", [P, NPAIR]) for j in range(2)]
        S = sb("S", [P, G, DH])
        ssq = sb("ssq", [P, B])
        lt = sb("lt", [P, 6, B, E])
        l1 = sb("l1", [P, 4, B])
        oh = sb("oh", [P, B, E])
        base = sb("base", [P, E])
        slotf = sb("slotf", [P, B])
        slot = sb("slot", [P, B], I32)
        tok0 = sb("tok0", [P, B])
        tokf = sb("tokf", [P, B])
        kq_flat = kq[:].rearrange("p g c a t -> p (g c a t)")
        kqd_flat = kqd[:].rearrange("p g c a t -> p (g c a t)")
        xn_flat = xn[:].rearrange("p b d -> p (b d)")
        Sd, U, delT = (xn_flat[:, n * G * C:(n + 1) * G * C].rearrange("p (g t) -> p g t", g=G) for n in range(3))
        Ut = xn_flat[:, 3 * G * C:3 * G * C + G * CS].rearrange("p (g t) -> p g t", g=G)
        tabf = A[:].rearrange("p g a t -> p (g a t)")[:, 0:6 * P].rearrange("p (n m) -> p n m", n=6)
        oT = xT[:].rearrange("p k (b t) -> p (k b) t", b=B)
        ctxT = xn[:].rearrange("p b (k t) -> p (b k) t", t=T)
        y = kq_flat[:, 0:B * D].rearrange("p (b d) -> p b d", b=B)
        hT = kq_flat[:, B * D:B * D + HID // P * B * T].rearrange("p (n t) -> p n t", n=HID // P)
        xfw = kqd_flat[:, 0:B * XSW].rearrange("p (b d) -> p b d", b=B)
        xfT = vT[:].rearrange("p (k b) t -> p k (b t)", k=KD)
        x1 = dec[:].rearrange("p (b k) t -> p b (k t)", b=B)
        gsb, gT, sg = qsq, qraw, qraw
        lax = kq_flat[:, 0:B * H * DH].rearrange("p (b h e) -> p b h e", b=B, h=H)
        ce = qsq[0:E, :]
        alog = qr[:, 0:4 * B * H].rearrange("p (n h) -> p n h", n=4)
        junk = qraw
        tb2 = kq_flat[:, 0:E * P].rearrange("p (e m) -> p e m", e=E)
        tb3 = kq_flat[:, E * P:2 * E * P].rearrange("p (e m) -> p e m", e=E)
        w_flat = w_sb[:].rearrange("p k n -> p (k n)")
        wc = w_flat[:, 0:D].rearrange("p (k n) -> p k n", k=KD)
        pw = w_flat[:, D:2 * D]
        xsT = w_flat[:, 2 * D:3 * D].rearrange("p (k t) -> p k t", k=KD)
        ya, z = w_flat[:, 3 * D:4 * D], w_flat[:, 4 * D:5 * D]
        pb_sb, lg_sb, lb_sb = (w_flat[:, n * D:(n + 1) * D] for n in (5, 6, 7))
        xs = w_flat[:, 8 * D:8 * D + XSW]
        pad = w_flat[:, 10 * D:10 * D + XSW]
        hm = w_flat[:, 12 * D:12 * D + P]
        tb = sb("tb", [P, 10, E])
        krow = sb("krow", [P, P])
        col = sb("col", [P, 5, E])
        tab = sb("tab", [P, 2, P], I32)
        cnt = sb("cnt", [P, E], I32)
        toki = sb("toki", [P, 1], I32)
        bc = sb("bc", [P, 1])
        mst = sb("mst", [P, 6])
        mmv = sb("mmv", [P, 2])
        ms = sb("ms", [P, 4])

        work = [ps(f"work{i}", [P, 512]) for i in range(2)]
        kkq = ps("kkq", [P, G, 2, C])
        uo = ps("uo", [P, G, 2, C])
        su = ps("su", [P, G, DH])
        bcast = ps("bcast", [P, 512])

        loaded = sem("loaded")
        dve_step, act_step, pool_step = sem("dve_step"), sem("act_step"), sem("pool_step")
        names = """x_loaded xt_free xres_loaded dec_free var_ready rstd_raw norm_ready xn_ready
            work_full_a work_full_v z_ready la_e_ready la_l_ready la_ready lax_ready g_copied gT_ready diff_ready
            dec_ready eg_ready q_sq_ready q_r_ready kq_ready_v kq_ready_g kq_ready_p qraw_free beta_ready gate_ready v_ready sil_ready
            kkq_full kkq_free A_ready kt_ready kd_ready kd_free bc_full bc_free pr_copied pr_ready pairs_free
            uo_full uo_free corr_full delT_ready S_ready su_full Sd_ready
            o_full o_sq_ready o_copied o_r_ready ctx_raw ctx_ready y_ready zn_ready x1_ready xf_ready
            h_ready ss_ready lg_ready sig_ready d_ready e_ready oh_ready rank_full slot_ready scat_done store_done x1_free
            ce_sq ce_r ce_n ce_T base_ready setup_v setup_a setup_p table_ready
            m_xs m_wc m_t m_xsT m_h m_hm m_y m_v m_r m_z m_free m_wfree m_add m_pad m_s S_used dec_seen
            silu_free v_free
            """.split()
        s = {n: sem(n) for n in names}
        work_free = [sem(f"work{i}_free") for i in range(2)]

        block = ctx.enter_context(nc.Block())
        x_v = x.rearrange("b (i t) d -> i t b d", t=T)
        out_v = out.rearrange("b (i t) d -> i t b d", t=T)
        out_rows = out.rearrange("b l d -> (b l) d")

        loads = [
            (squares[:], c_sq), (sel[:], c_sel), (mask[:], c_mask), (iota[:], c_iota), (tok0[:], c_tok), (krow[:], c_row), (col[:], c_col),
            (w_sb[:], w_in.rearrange("(k p) n -> p k n", p=P)),
            (wa_sb[:], wa.rearrange("(k p) n -> p k n", p=P)),
            (dtb[:], dt_bias.partition_broadcast(P)), (neg_a[:], a_log.partition_broadcast(P)),
            (wo_sb[:], wo.rearrange("(k p) n -> p k n", p=P)), (bo_sb[:], bo.partition_broadcast(P)),
            (gw1_sb[:], gw1.rearrange("(k p) n -> p k n", p=P)),
            (gb1_sb[:], gb1),
            (gw2_sb[:], gw2.rearrange("(k p) n -> p k n", p=P)), (gb2_sb[:], gb2.partition_broadcast(P)),
            (ce, col_emb),
        ] + [(nw[DH * h:DH * h + DH, :], norm_w.rearrange("(p o) -> p o", o=1)) for h in range(HP)]
        ALL = 16 * len(loads)

        @block.sync
        def _(sp):
            for dst, src in loads:
                sp.dma_start(dst, src).then_inc(loaded, 16)
            with sp.Fori(0, NT) as i:
                sp.wait_ge(s["xt_free"], 1)
                sp.sem_inc(s["xt_free"], -1)
                sp.dma_start(xt[:], x_v[bass.ds(i, 1)].rearrange("i t b d -> (i t) b d")).then_inc(s["x_loaded"], 16)
                sp.wait_ge(s["x1_free"], 1)
                sp.sem_inc(s["x1_free"], -1)
                sp.dma_start(x1, x_v[bass.ds(i, 1)].rearrange("i t b d -> (i t) b d")).then_inc(s["xres_loaded"], 16)
                sp.wait_ge(s["x1_ready"], 1)
                sp.sem_inc(s["x1_ready"], -1)
                sp.dma_start(out_v[bass.ds(i, 1)].rearrange("i t b d -> (i t) b d"), x1).then_inc(s["store_done"], 16)
                sp.wait_ge(s["store_done"], 16)
                sp.sem_inc(s["store_done"], -16)
                sp.sem_inc(s["dec_free"], 1)
            sp.wait_ge(s["table_ready"], 1)
            sp.sem_inc(s["table_ready"], -1)
            for dst, src in ((pad, c_pad), (pb_sb, proj_b.partition_broadcast(P)), (lg_sb, ln_g.partition_broadcast(P)),
                             (lb_sb, ln_b.partition_broadcast(P))):
                sp.dma_start(dst, src).then_inc(s["m_pad"], 16)
            sp.wait_ge(s["m_pad"], 64)
            sp.sem_inc(s["m_pad"], -64)
            for e in range(E):
                behind = nc.sync.value_load(cnt[0:1, e:e + 1], min_val=0, max_val=PADROW)
                sp.dma_start(xs_dram[bass.ds(behind, P)], pad).then_inc(s["m_pad"], 16)
            sp.dma_start(xs_dram[PADROW:PADROW + P], pad).then_inc(s["m_pad"], 16)
            sp.wait_ge(s["m_pad"], 16 * (E + 1))
            sp.sem_inc(s["m_pad"], -(16 * (E + 1)))
            sp.wait_ge(s["scat_done"], 16 * B * NT)
            with sp.Fori(0, NM) as m:
                e_m = nc.sync.value_load(tab[0:1, 0, bass.ds(m, 1)], min_val=0, max_val=E - 1)
                r_m = nc.sync.value_load(tab[0:1, 1, bass.ds(m, 1)], min_val=0, max_val=PADROW)
                sp.wait_ge(s["m_wfree"], 1)
                sp.sem_inc(s["m_wfree"], -1)
                sp.dma_start(wc, w_cols[bass.ds(e_m, 1)].rearrange("e (k p) n -> p (e k) n", p=P)).then_inc(s["m_wc"], 16)
                sp.dma_start(bc[:], b_cols[bass.ds(e_m, 1)].rearrange("e n o -> (e n) o")).then_inc(s["m_wc"], 16)
                sp.dma_start(pw, proj_w[bass.ds(e_m, 1)].rearrange("e n d -> (e n) d")).then_inc(s["m_wc"], 16)
                sp.wait_ge(s["m_free"], 1)
                sp.sem_inc(s["m_free"], -1)
                sp.dma_start(xs, xs_dram[bass.ds(r_m, P)]).then_inc(s["m_xs"], 16)

        @block.tensor
        def _(pe):
            def into_work(k):
                pe.wait_ge(work_free[k % 2], 1)
                pe.sem_inc(work_free[k % 2], -1)
                return work[k % 2]

            pe.wait_ge(loaded, ALL)
            pe.wait_ge(s["ce_n"], 1)
            pe.sem_inc(s["ce_n"], -1)
            for k in range(KD):
                mm = pe.transpose(work[0][:, k * E:(k + 1) * E], ce[:, k * P:(k + 1) * P], ident[0:E, 0:E])
            mm.then_inc(s["ce_T"], 1)
            with pe.Fori(0, NT):
                k = 0
                pe.wait_ge(s["xn_ready"], B)
                pe.sem_inc(s["xn_ready"], -B)
                pe.sem_inc(s["xt_free"], 1)
                for f in range(KD):
                    w = into_work(k)
                    for b in range(B):
                        mm = pe.transpose(w[:, b * T:(b + 1) * T], xn[:, b, f * P:(f + 1) * P], ident)
                    mm.then_inc(s["work_full_v"], 1)
                    k += 1
                pe.wait_ge(s["z_ready"], KD)
                pe.sem_inc(s["z_ready"], -KD)
                w = into_work(k)
                for b in range(B):
                    for f in range(KD):
                        mm = pe.matmul(w[:, b * H:(b + 1) * H], xT[:, f, b * T:(b + 1) * T], wa_sb[:, f, :],
                                       start=(f == 0), stop=(f == KD - 1))
                mm.then_inc(s["work_full_v"], 1)
                k += 1

                def project(j, hg):
                    w = into_work(k)
                    for f in range(KD):
                        mm = pe.matmul(w[:], w_sb[:, f, j * D + hg * P:j * D + (hg + 1) * P], xT[:, f, :],
                                       start=(f == 0), stop=(f == KD - 1))
                    mm.then_inc(s["work_full_a"], 1)

                for j in (2,):
                    for hg in range(KD):
                        project(j, hg)
                        k += 1
                pe.wait_ge(s["lax_ready"], 1)
                pe.sem_inc(s["lax_ready"], -1)
                for hg in range(KD):
                    w = into_work(k)
                    for b in range(B):
                        mm = pe.matmul(w[:, b * T:(b + 1) * T],
                                       lax[:, b, hg * HP:(hg + 1) * HP, :].rearrange("p h e -> p (h e)"), ucum,
                                       start=True, stop=True)
                    mm.then_inc(s["work_full_a"], 1)
                    k += 1
                for j in range(2):
                    for hg in range(KD):
                        project(j, hg)
                        k += 1
                        pe.wait_ge(s["q_sq_ready"], 1)
                        pe.sem_inc(s["q_sq_ready"], -1)
                        w = into_work(k)
                        pe.matmul(w[:], blk1, qsq[:], start=True, stop=True).then_inc(s["work_full_a"], 1)
                        k += 1
                for j in (3, 4):
                    for hg in range(KD):
                        project(j, hg)
                        k += 1
                pe.wait_ge(s["kq_ready_v"], 2 * KD)
                pe.sem_inc(s["kq_ready_v"], -(2 * KD))
                pe.wait_ge(s["kq_ready_p"], 2 * KD)
                pe.sem_inc(s["kq_ready_p"], -(2 * KD))
                for c in range(NC):
                    pe.wait_ge(s["kkq_free"], 1)
                    pe.sem_inc(s["kkq_free"], -1)
                    for g in range(G):
                        for h in range(HP):
                            q = slice(DH * h, DH * h + DH)
                            mm = pe.matmul(kkq[q, g], kq[q, g, c, 0, :], kq[q, g, c].rearrange("p a t -> p (a t)"),
                                           start=True, stop=True)
                    mm.then_inc(s["kkq_full"], 1)
                    pe.wait_ge(s["S_ready"], 1)
                    pe.sem_inc(s["S_ready"], -1)
                    pe.wait_ge(s["uo_free"], 1)
                    pe.sem_inc(s["uo_free"], -1)
                    for g in range(G):
                        for h in range(HP):
                            q = slice(DH * h, DH * h + DH)
                            mm = pe.matmul(uo[q, g], S[q, g, :], kqd[q, g, c].rearrange("p a t -> p (a t)"),
                                           start=(g % 8 == 0), stop=True, skip_group_check=True)
                    mm.then_inc(s["uo_full"], 1)
                    pe.wait_ge(s["A_ready"], 1)
                    pe.sem_inc(s["A_ready"], -1)
                    for j in range(2):
                        for pack in PACKS:
                            pe.wait_ge(s["bc_free"], 1)
                            pe.sem_inc(s["bc_free"], -1)
                            o = 0
                            for t0 in pack:
                                n = G * WID[t0]
                                mm = pe.matmul(bcast[:, o:o + n], sel[:, j * CS + t0, :],
                                               A[:, :, 0, j * CS + t0 + 1:(j + 1) * CS],
                                               start=(o == 0), stop=True, skip_group_check=True)
                                o += n
                            mm.then_inc(s["bc_full"], 1)
                    pe.wait_ge(s["delT_ready"], 1)
                    pe.sem_inc(s["delT_ready"], -1)
                    for g in range(G):
                        for h in range(HP):
                            q = slice(DH * h, DH * h + CS)
                            mm = pe.matmul(uo[DH * h:DH * h + DH, g, 0, CS:C], delT[q, g, :], A[q, g, 0, CS:C],
                                           start=False, stop=True, skip_group_check=True)
                    mm.then_inc(s["corr_full"], 1)
                    pe.wait_ge(s["delT_ready"], 1)
                    pe.sem_inc(s["delT_ready"], -1)
                    pe.wait_ge(s["kd_ready"], 1)
                    pe.sem_inc(s["kd_ready"], -1)
                    for g in range(G):
                        for h in range(HP):
                            q = slice(DH * h, DH * h + DH)
                            mm = pe.matmul(su[q, g, :], kd[q, g, :], delT[q, g, :], start=True, stop=True)
                    mm.then_inc(s["su_full"], 1)
                    for g in range(G):
                        for h in range(HP):
                            q = slice(DH * h, DH * h + DH)
                            mm = pe.matmul(uo[q, g, 1, :], delT[q, g, :], A[q, g, 1, :],
                                           start=False, stop=True, skip_group_check=True)
                    mm.then_inc(s["o_full"], 1)
                for hg in range(KD):
                    pe.wait_ge(s["o_sq_ready"], 1)
                    pe.sem_inc(s["o_sq_ready"], -1)
                    w = into_work(k)
                    pe.matmul(w[:], blk1, qsq[:], start=True, stop=True).then_inc(s["work_full_a"], 1)
                    k += 1
                pe.wait_ge(s["ctx_ready"], KD)
                pe.sem_inc(s["ctx_ready"], -KD)
                for b in range(B):
                    w = into_work(k)
                    for hg in range(KD):
                        mm = pe.matmul(w[:], ctxT[:, hg * B + b, :], wo_sb[:, hg, :],
                                       start=(hg == 0), stop=(hg == KD - 1))
                    mm.then_inc(s["work_full_v"], 1)
                    k += 1
                pe.wait_ge(s["xf_ready"], B)
                pe.sem_inc(s["xf_ready"], -B)
                for f in range(KD):
                    w = into_work(k)
                    for b in range(B):
                        mm = pe.transpose(w[:, b * T:(b + 1) * T], xfw[:, b, f * P:(f + 1) * P], ident)
                    mm.then_inc(s["work_full_v"], 1)
                    k += 1
                pe.wait_ge(s["z_ready"], KD)
                pe.sem_inc(s["z_ready"], -KD)
                for n in range(HID // P):
                    w = into_work(k)
                    for f in range(KD):
                        mm = pe.matmul(w[:], gw1_sb[:, f, n * P:(n + 1) * P], xfT[:, f, :],
                                       start=(f == 0), stop=(f == KD - 1))
                    mm.then_inc(s["work_full_a"], 1)
                    k += 1
                pe.wait_ge(s["h_ready"], HID // P)
                pe.sem_inc(s["h_ready"], -(HID // P))
                w = into_work(k)
                for b in range(B):
                    for f in range(KD):
                        pe.matmul(w[:, b * 2 * E:b * 2 * E + E], xfT[:, f, b * T:(b + 1) * T], ceT[:, f, :],
                                  start=(f == 0), stop=(f == KD - 1))
                    for n in range(HID // P):
                        mm = pe.matmul(w[:, b * 2 * E + E:(b + 1) * 2 * E], hT[:, n, b * T:(b + 1) * T], gw2_sb[:, n, :],
                                       start=(n == 0), stop=(n == HID // P - 1))
                mm.then_inc(s["work_full_v"], 1)
                k += 1
                pe.wait_ge(s["oh_ready"], 1)
                pe.sem_inc(s["oh_ready"], -1)
                w = into_work(k)
                pe.matmul(w[:, 0:B * E], ustrict, oh[:].rearrange("p b e -> p (b e)"), start=True, stop=False,
                          skip_group_check=True)
                for n in range(1, B):
                    pe.matmul(w[:, n * E:B * E], ones, oh[:, 0:B - n, :].rearrange("p b e -> p (b e)"),
                              start=False, stop=False, skip_group_check=True)
                for b in range(B):
                    mm = pe.matmul(w[:, B * E:(B + 1) * E], ones, oh[:, b, :], start=False, stop=(b == B - 1),
                                   skip_group_check=True)
                mm.then_inc(s["work_full_v"], 1)
                k += 1
            with pe.Fori(0, NM):
                pe.wait_ge(s["m_xs"], 16)
                pe.sem_inc(s["m_xs"], -16)
                pe.wait_ge(work_free[0], 1)
                pe.sem_inc(work_free[0], -1)
                for f in range(KD):
                    mm = pe.transpose(work[0][:, f * P:(f + 1) * P], xs[:, f * P:(f + 1) * P], ident)
                mm.then_inc(s["m_t"], 1)
                pe.wait_ge(s["m_xsT"], 1)
                pe.sem_inc(s["m_xsT"], -1)
                pe.wait_ge(s["m_wc"], 48)
                pe.sem_inc(s["m_wc"], -48)
                pe.wait_ge(work_free[1], 1)
                pe.sem_inc(work_free[1], -1)
                for f in range(KD):
                    mm = pe.matmul(work[1][:, 0:P], wc[:, f, :], xsT[:, f, :], start=(f == 0), stop=(f == KD - 1))
                mm.then_inc(s["m_h"], 1)
                pe.wait_ge(s["m_hm"], 1)
                pe.sem_inc(s["m_hm"], -1)
                pe.wait_ge(s["bc_free"], 1)
                pe.sem_inc(s["bc_free"], -1)
                pe.matmul(bcast[:], hm, pw, start=True, stop=True).then_inc(s["m_y"], 1)

        @block.scalar
        def _(act):
            link = Chain(act, act_step)

            def rsqrt(dst, src, scale=1.0, bias=None, out_bias=None):
                link(nc.scalar.activation(dst, src, ACT.Ln, scale=scale, **({} if bias is None else {"bias": bias})))
                return nc.scalar.activation(dst, dst, ACT.Exp, scale=-0.5,
                                            **({} if out_bias is None else {"bias": out_bias}))

            act.wait_ge(loaded, ALL)
            act.wait_ge(s["setup_v"], 1)
            act.sem_inc(s["setup_v"], -1)
            link(nc.scalar.activation(neg_a[:], neg_a[:], ACT.Exp))
            act.sem_inc(s["setup_a"], 1)
            link(nc.scalar.activation(junk[0:E, :], ce, ACT.Square, accum_out=ce_s[:, 0:1]))
            act.sem_inc(s["ce_sq"], 1)
            act.wait_ge(s["ce_r"], 1)
            act.sem_inc(s["ce_r"], -1)
            rsqrt(ce_s[:, 2:3], ce_s[:, 1:2], scale=1e6, out_bias=ln3[0:E, :]).then_inc(s["ce_sq"], 1)
            link.restart()
            with act.Fori(0, NT):
                k = 0

                def norm_tokens(dst, src, width):
                    act.wait_ge(s["var_ready"], 1)
                    act.sem_inc(s["var_ready"], -1)
                    rsqrt(rstd[:], ve[:]).then_inc(s["rstd_raw"], 1)
                    act.wait_ge(s["norm_ready"], 1)
                    act.sem_inc(s["norm_ready"], -1)
                    for b in range(B):
                        yield nc.scalar.activation(dst[:, b, 0:D], src[:, b, :], ACT.Identity,
                                                   scale=rstd[:, b:b + 1], bias=nmr[:, b:b + 1])

                for ins in norm_tokens(xn, xt, D):
                    ins.then_inc(s["xn_ready"], 1)
                act.wait_ge(s["la_e_ready"], 1)
                act.sem_inc(s["la_e_ready"], -1)
                link(nc.scalar.activation(alog[:, 2, :], alog[:, 1, :], ACT.Exp, scale=-1.0))
                nc.scalar.activation(alog[:, 3, :], alog[:, 2, :], ACT.Ln, bias=1.0).then_inc(s["la_l_ready"], 1)
                k = KD + 1
                for hg in range(KD):
                    act.wait_ge(s["work_full_a"], 1)
                    act.sem_inc(s["work_full_a"], -1)
                    nc.scalar.activation(vT[:, hg * B:(hg + 1) * B, :].rearrange("p g t -> p (g t)"), work[k % 2][:],
                                         ACT.Copy).then_inc(work_free[k % 2], 1)
                    k += 1
                for hg in range(KD):
                    gs = slice(hg * B, (hg + 1) * B)
                    act.wait_ge(s["work_full_a"], 1)
                    act.sem_inc(s["work_full_a"], -1)
                    if hg:
                        act.wait_ge(s["diff_ready"], 1)
                        act.sem_inc(s["diff_ready"], -1)
                        nc.scalar.activation(dec[:, gs.start - B:gs.stop - B, :], dec[:, gs.start - B:gs.stop - B, :], ACT.Exp)
                    link(nc.scalar.activation(gsb[:], work[k % 2][:], ACT.Copy))
                    act.sem_inc(s["g_copied"], 1)
                    link(nc.scalar.activation(eg[:, gs, :].rearrange("p g t -> p (g t)"), work[k % 2][:], ACT.Exp))
                    act.sem_inc(work_free[k % 2], 1)
                    act.sem_inc(s["eg_ready"], 1)
                    k += 1
                act.wait_ge(s["diff_ready"], 1)
                act.sem_inc(s["diff_ready"], -1)
                link(nc.scalar.activation(dec[:, G - B:G, :], dec[:, G - B:G, :], ACT.Exp))
                act.sem_inc(s["dec_ready"], 1)
                for j in range(2):
                    for hg in range(KD):
                        w = work[k % 2]
                        act.wait_ge(s["work_full_a"], 1)
                        act.sem_inc(s["work_full_a"], -1)
                        if hg or j:
                            act.wait_ge(s["qraw_free"], 1)
                            act.sem_inc(s["qraw_free"], -1)
                        link(nc.scalar.activation(qraw[:], w[:], ACT.Copy))
                        link(nc.scalar.activation(qsq[:], w[:], ACT.Square))
                        act.sem_inc(work_free[k % 2], 1)
                        act.sem_inc(s["q_sq_ready"], 1)
                        k += 1
                        w = work[k % 2]
                        act.wait_ge(s["work_full_a"], 1)
                        act.sem_inc(s["work_full_a"], -1)
                        link(nc.scalar.activation(qr[:], w[:], ACT.Ln))
                        act.sem_inc(work_free[k % 2], 1)
                        nc.scalar.activation(qr[:], qr[:], ACT.Exp, scale=-0.5,
                                             **({"bias": lnq[:]} if j == 0 else {})).then_inc(s["q_r_ready"], 1)
                        k += 1
                act.wait_ge(s["qraw_free"], 1)
                act.sem_inc(s["qraw_free"], -1)
                for hg in range(KD):
                    act.wait_ge(s["work_full_a"], 1)
                    act.sem_inc(s["work_full_a"], -1)
                    nc.scalar.activation(beta[:, hg * B:(hg + 1) * B, :].rearrange("p g t -> p (g t)"), work[k % 2][:],
                                         ACT.Sigmoid).then_inc(work_free[k % 2], 1)
                    k += 1
                for hg in range(KD):
                    act.wait_ge(s["work_full_a"], 1)
                    act.sem_inc(s["work_full_a"], -1)
                    if hg:
                        act.wait_ge(s["silu_free"], 1)
                        act.sem_inc(s["silu_free"], -1)
                    nc.scalar.activation(sg[:], work[k % 2][:], ACT.Sigmoid).then_inc(s["gate_ready"], 1)
                    k += 1
                act.wait_ge(s["silu_free"], 1)
                act.sem_inc(s["silu_free"], -1)
                for c in range(NC):
                    for j in range(2):
                        act.wait_ge(s["pairs_free"], 1)
                        act.sem_inc(s["pairs_free"], -1)
                        for pack in PACKS:
                            n = sum(G * WID[t0] for t0 in pack)
                            act.wait_ge(s["bc_full"], 1)
                            act.sem_inc(s["bc_full"], -1)
                            link(nc.scalar.activation(pairs[j][:, OFF[pack[0]]:OFF[pack[0]] + n], bcast[:, 0:n], ACT.Copy))
                            act.sem_inc(s["bc_free"], 1)
                        act.sem_inc(s["pr_copied"], 1)
                    act.wait_ge(s["o_full"], 1)
                    act.sem_inc(s["o_full"], -1)
                    link(nc.scalar.activation(oT[:, :, c * C:(c + 1) * C], uo[:, :, 1, :], ACT.Copy))
                    act.sem_inc(s["uo_free"], 1)
                for hg in range(KD):
                    gs = slice(hg * B, (hg + 1) * B)
                    nc.scalar.activation(qsq[:], oT[:, gs, :].rearrange("p g t -> p (g t)"), ACT.Square)\
                        .then_inc(s["o_sq_ready"], 1)
                    act.wait_ge(s["work_full_a"], 1)
                    act.sem_inc(s["work_full_a"], -1)
                    if hg:
                        act.wait_ge(s["ctx_raw"], 1)
                        act.sem_inc(s["ctx_raw"], -1)
                    link(nc.scalar.activation(qr[:], work[k % 2][:], ACT.Ln, scale=1.0 / DH, bias=eps6[:]))
                    act.sem_inc(work_free[k % 2], 1)
                    nc.scalar.activation(qr[:], qr[:], ACT.Exp, scale=-0.5).then_inc(s["o_r_ready"], 1)
                    k += 1
                act.wait_ge(s["ctx_raw"], 1)
                act.sem_inc(s["ctx_raw"], -1)
                for ins in norm_tokens(y, y, D):
                    ins.then_inc(s["zn_ready"], 1)
                for b, ins in enumerate(norm_tokens(xfw, x1, D)):
                    link(ins)
                    act.sem_inc(s["xf_ready"], 1)
                k += B + KD
                for b in range(B):
                    link(nc.scalar.activation(junk[:], xfw[:, b, 0:D], ACT.Square, accum_out=ssq[:, b:b + 1]))
                act.sem_inc(s["ss_ready"], 1)
                act.wait_ge(s["var_ready"], 1)
                act.sem_inc(s["var_ready"], -1)
                rsqrt(rstd[:], ve[:], scale=1e6, out_bias=ln3[:]).then_inc(s["rstd_raw"], 1)
                for n in range(HID // P):
                    act.wait_ge(s["work_full_a"], 1)
                    act.sem_inc(s["work_full_a"], -1)
                    link(nc.scalar.activation(hT[:, n, :], work[k % 2][:], ACT.Gelu, bias=gb1_sb[:, n:n + 1]))
                    act.sem_inc(work_free[k % 2], 1)
                    act.sem_inc(s["h_ready"], 1)
                    k += 1
                act.wait_ge(s["lg_ready"], 1)
                act.sem_inc(s["lg_ready"], -1)
                nc.scalar.activation(lt[:, 1], lt[:, 1], ACT.Sigmoid).then_inc(s["sig_ready"], 1)
                act.wait_ge(s["d_ready"], 1)
                act.sem_inc(s["d_ready"], -1)
                nc.scalar.activation(lt[:, 3], lt[:, 2], ACT.Exp).then_inc(s["e_ready"], 1)
                link.restart()
            with act.Fori(0, NM):
                act.wait_ge(s["m_t"], 1)
                act.sem_inc(s["m_t"], -1)
                link(nc.scalar.activation(xsT.rearrange("p k t -> p (k t)"), work[0][:], ACT.Copy))
                act.sem_inc(work_free[0], 1)
                act.sem_inc(s["m_xsT"], 1)
                act.wait_ge(s["m_h"], 1)
                act.sem_inc(s["m_h"], -1)
                link(nc.scalar.activation(hm, work[1][:, 0:P], ACT.Gelu, bias=bc[:]))
                act.sem_inc(work_free[1], 1)
                act.sem_inc(s["m_hm"], 1)
                for _ in range(2):
                    act.wait_ge(s["m_v"], 1)
                    act.sem_inc(s["m_v"], -1)
                    rsqrt(ms[:, 1:2], ms[:, 0:1]).then_inc(s["m_r"], 1)
                link.restart()

        @block.gpsimd
        def _(pool):
            link = Chain(pool, pool_step)
            pool.wait_ge(loaded, ALL)
            link(nc.gpsimd.memset(S[:], 0.0))
            pool.sem_inc(s["S_ready"], 1)
            link(nc.gpsimd.memset(base[:], 0.0))
            pool.sem_inc(s["base_ready"], 1)
            for n in ("xt_free", "kkq_free", "uo_free", "bc_free", "dec_free"):
                pool.sem_inc(s[n], 1)
            for f in work_free:
                pool.sem_inc(f, 1)
            pool.sem_inc(s["pairs_free"], 2)
            link.restart()
            with pool.Fori(0, NT) as i:
                pool.wait_ge(s["la_ready"], 1)
                pool.sem_inc(s["la_ready"], -1)
                nc.gpsimd.tensor_copy(lax, la[:].unsqueeze(3).to_broadcast([P, B, H, DH])).then_inc(s["lax_ready"], 1)
                pool.wait_ge(s["dec_free"], 1)
                pool.sem_inc(s["dec_free"], -1)
                for hg in range(KD):
                    gs = slice(hg * B, (hg + 1) * B)
                    pool.wait_ge(s["gT_ready"], 1)
                    pool.sem_inc(s["gT_ready"], -1)
                    link(nc.gpsimd.tensor_tensor(dec[:, gs, :].rearrange("p g t -> p (g t)"), gsb[:], gT[:], ALU.subtract))
                    link(nc.gpsimd.tensor_tensor(dec[:, gs, :].rearrange("p g (c t) -> p (g c) t", t=C),
                                                 dec[:, gs, :].rearrange("p g (c t) -> p (g c) t", t=C),
                                                 mask[:].unsqueeze(1).to_broadcast([P, B * NC, C]), ALU.add))
                    pool.sem_inc(s["diff_ready"], 1)
                pool.wait_ge(s["eg_ready"], KD)
                pool.sem_inc(s["eg_ready"], -KD)
                pool.wait_ge(s["kq_ready_g"], 2 * KD)
                pool.sem_inc(s["kq_ready_g"], -(2 * KD))
                for hg in range(KD):
                    gs = slice(hg * B, (hg + 1) * B)
                    for a in range(2):
                        nc.gpsimd.tensor_tensor(kqd[:, gs, :, a, :], kq[:, gs, :, a, :],
                                                eg[:, gs, :].rearrange("p g (c t) -> p g c t", t=C),
                                                ALU.mult).then_inc(s["kq_ready_p"], 1)
                pool.wait_ge(s["dec_ready"], 1)
                pool.sem_inc(s["dec_ready"], -1)
                pool.sem_inc(s["dec_seen"], 1)
                for c in range(NC):
                    pool.wait_ge(s["kt_ready"], 1)
                    pool.sem_inc(s["kt_ready"], -1)
                    nc.gpsimd.tensor_tensor(kd[:], kt[:], dec[:, :, c * C + C - 1:c * C + C].to_broadcast([P, G, C]),
                                            ALU.mult).then_inc(s["kd_ready"], 1)
                    for j in range(2):
                        pool.wait_ge(s["pr_copied"], 1)
                        pool.sem_inc(s["pr_copied"], -1)
                        for t0 in range(CS - 1):
                            a = pairs[j][:, OFF[t0]:OFF[t0] + G * WID[t0]].rearrange("p (g t) -> p g t", g=G)
                            t = c * C + j * CS + t0 + 1
                            ins = nc.gpsimd.tensor_tensor(a, a, beta[:, :, t:t + WID[t0]], ALU.mult)
                        ins.then_inc(s["pr_ready"], 1)
                    pool.wait_ge(s["S_used"], 1)
                    pool.sem_inc(s["S_used"], -1)
                    nc.gpsimd.tensor_tensor(Sd, S[:], eg[:, :, c * C + C - 1:c * C + C].to_broadcast([P, G, DH]),
                                            ALU.mult).then_inc(s["Sd_ready"], 1)
                for hg in range(KD):
                    gs = slice(hg * B, (hg + 1) * B)
                    pool.wait_ge(s["o_copied"], 1)
                    pool.sem_inc(s["o_copied"], -1)
                    nc.gpsimd.tensor_tensor(ctxT[:, gs, :], ctxT[:, gs, :], silu[:, gs, :], ALU.mult)\
                        .then_inc(s["ctx_ready"], 1)
                pool.wait_ge(s["xres_loaded"], 16)
                pool.sem_inc(s["xres_loaded"], -16)
                for b in range(B):
                    pool.wait_ge(s["zn_ready"], 1)
                    pool.sem_inc(s["zn_ready"], -1)
                    link(nc.gpsimd.tensor_tensor(x1[:, b, :], x1[:, b, :], y[:, b, :], ALU.add))
                pool.sem_inc(s["y_ready"], 1)
                pool.sem_inc(s["x1_ready"], 1)
                pool.wait_ge(s["slot_ready"], 1)
                pool.sem_inc(s["slot_ready"], -1)
                for b in range(B):
                    nc.gpsimd.indirect_dma_start(
                        xs_dram, bass.IndirectOffsetOnAxis(ap=slot[:, b:b + 1].bitcast(U32), axis=0),
                        xfw[:, b, :], None).then_inc(s["scat_done"], 16)
                pool.wait_ge(s["scat_done"], i * (16 * B) + 16 * B)
                link.restart()
            with pool.Fori(0, NM) as m:
                pool.wait_ge(s["m_z"], 1)
                pool.sem_inc(s["m_z"], -1)
                nc.gpsimd.indirect_dma_start(
                    out_rows, bass.IndirectOffsetOnAxis(ap=toki[:].bitcast(U32), axis=0), z, None,
                    bounds_check=ROWS - 1, oob_is_err=False, compute_op=ALU.add).then_inc(s["m_add"], 16)
                pool.wait_ge(s["m_add"], m * 16 + 16)
                pool.sem_inc(s["m_s"], 1)

        @block.vector
        def _(dve):
            link = Chain(dve, dve_step)
            v = nc.vector

            def refine(r, var, t):
                link(v.tensor_tensor(t, r, r, ALU.mult))
                link(v.tensor_tensor(t, t, var, ALU.mult))
                link(v.tensor_scalar(t, t, -0.5, 1.5, ALU.mult, ALU.add))
                link(v.tensor_tensor(r, r, t, ALU.mult))

            def token_stats(src, b):
                link(v.bn_stats(stats[:, b, :], src[:, b, :]))
                link(v.bn_aggr(mv[:, b, :], stats[:, b, :]))

            def token_norm():
                link(v.tensor_scalar(ve[:], mv[:, :, 1], 1e-5, None, ALU.add))
                dve.sem_inc(s["var_ready"], 1)
                dve.wait_ge(s["rstd_raw"], 1)
                dve.sem_inc(s["rstd_raw"], -1)
                refine(rstd[:], ve[:], nt1[:])
                link(v.scalar_tensor_tensor(nmr[:], mv[:, :, 0], -1.0, rstd[:], ALU.mult, ALU.mult))
                dve.sem_inc(s["norm_ready"], 1)

            dve.wait_ge(loaded, ALL)
            link(v.memset(eps5[:], 1e-5))
            link(v.memset(eps6[:], 1e-6))
            link(v.memset(lnq[:], -0.5 * math.log(DH)))
            link(v.memset(ln3[:], math.log(1e3)))
            dve.sem_inc(s["setup_v"], 1)
            dve.wait_ge(s["setup_a"], 1)
            dve.sem_inc(s["setup_a"], -1)
            link(v.tensor_scalar(neg_a[:], neg_a[:], -1.0, None, ALU.mult))
            dve.wait_ge(s["ce_sq"], 1)
            dve.sem_inc(s["ce_sq"], -1)
            link(v.tensor_scalar(ce_s[:, 1:2], ce_s[:, 0:1], 1e-24, None, ALU.max))
            dve.sem_inc(s["ce_r"], 1)
            dve.wait_ge(s["ce_sq"], 1)
            dve.sem_inc(s["ce_sq"], -1)
            refine(ce_s[:, 2:3], ce_s[:, 1:2], ce_s[:, 3:4])
            link(v.tensor_scalar(ce, ce, ce_s[:, 2:3], None, ALU.mult))
            dve.sem_inc(s["ce_n"], 1)
            dve.wait_ge(s["ce_T"], 1)
            dve.sem_inc(s["ce_T"], -1)
            link(v.tensor_copy(ceT[:].rearrange("p k e -> p (k e)"), work[0][:, 0:KD * E]))
            dve.wait_ge(s["base_ready"], 1)
            dve.sem_inc(s["base_ready"], -1)
            link(v.tensor_copy(tokf[:], tok0[:]))
            link.restart()
            with dve.Fori(0, NT):
                k = 0
                dve.wait_ge(s["x_loaded"], 16)
                dve.sem_inc(s["x_loaded"], -16)
                for b in range(B):
                    token_stats(xt, b)
                token_norm()
                for f in range(KD):
                    dve.wait_ge(s["work_full_v"], 1)
                    dve.sem_inc(s["work_full_v"], -1)
                    link(v.tensor_copy(xT[:, f, :], work[k % 2][:]))
                    dve.sem_inc(work_free[k % 2], 1)
                    dve.sem_inc(s["z_ready"], 1)
                    k += 1
                dve.wait_ge(s["work_full_v"], 1)
                dve.sem_inc(s["work_full_v"], -1)
                link(v.tensor_tensor(alog[:, 0, :].rearrange("p (b h) -> p b h", b=B),
                                     work[k % 2][:, 0:B * H].rearrange("p (b h) -> p b h", b=B),
                                     dtb[:].unsqueeze(1).to_broadcast([P, B, H]), ALU.add))
                dve.sem_inc(work_free[k % 2], 1)
                k += 1
                link(v.scalar_tensor_tensor(alog[:, 1, :], alog[:, 0, :], -1.0, alog[:, 0, :], ALU.mult, ALU.max))
                dve.sem_inc(s["la_e_ready"], 1)
                dve.wait_ge(s["la_l_ready"], 1)
                dve.sem_inc(s["la_l_ready"], -1)
                link(v.scalar_tensor_tensor(alog[:, 1, :], alog[:, 0, :], 0.0, alog[:, 3, :], ALU.max, ALU.add))
                link(v.tensor_tensor(la[:], alog[:, 1, :].rearrange("p (b h) -> p b h", b=B),
                                     neg_a[:].unsqueeze(1).to_broadcast([P, B, H]), ALU.mult))
                dve.sem_inc(s["la_ready"], 1)
                k += KD
                for hg in range(KD):
                    dve.wait_ge(s["g_copied"], 1)
                    dve.sem_inc(s["g_copied"], -1)
                    link(v.transpose(gT[:], gsb[:]))
                    dve.sem_inc(s["gT_ready"], 1)
                k += KD
                for j in range(2):
                    for hg in range(KD):
                        dve.wait_ge(s["q_r_ready"], 1)
                        dve.sem_inc(s["q_r_ready"], -1)
                        link(v.tensor_tensor(kq[:, hg * B:(hg + 1) * B, :, 1 - j, :],
                                             qraw[:].rearrange("p (b c t) -> p b c t", b=B, c=NC),
                                             qr[:].rearrange("p (b c t) -> p b c t", b=B, c=NC), ALU.mult))
                        dve.sem_inc(s["qraw_free"], 1)
                        dve.sem_inc(s["kq_ready_v"], 1)
                        dve.sem_inc(s["kq_ready_g"], 1)
                k += 4 * KD + KD
                for hg in range(KD):
                    dve.wait_ge(s["gate_ready"], 1)
                    dve.sem_inc(s["gate_ready"], -1)
                    link(v.tensor_tensor(silu[:, hg * B:(hg + 1) * B, :].rearrange("p g t -> p (g t)"), work[k % 2][:],
                                         sg[:], ALU.mult))
                    dve.sem_inc(work_free[k % 2], 1)
                    dve.sem_inc(s["silu_free"], 1)
                    k += 1
                dve.wait_ge(s["dec_seen"], 1)
                dve.sem_inc(s["dec_seen"], -1)
                for c in range(NC):
                    tc = slice(c * C, (c + 1) * C)
                    link(v.transpose(kt[:], kq[:, :, c, 0, :]))
                    dve.sem_inc(s["kt_ready"], 1)
                    dve.wait_ge(s["kkq_full"], 1)
                    dve.sem_inc(s["kkq_full"], -1)
                    link(v.tensor_tensor(A[:], kkq[:], dec[:, :, tc].unsqueeze(2).to_broadcast([P, G, 2, C]), ALU.mult))
                    dve.sem_inc(s["kkq_free"], 1)
                    dve.sem_inc(s["A_ready"], 1)
                    dve.wait_ge(s["uo_full"], 1)
                    dve.sem_inc(s["uo_full"], -1)
                    dve.sem_inc(s["S_used"], 1)
                    for j in range(2):
                        h = slice(j * CS, (j + 1) * CS)
                        th = slice(c * C + j * CS, c * C + (j + 1) * CS)
                        if j:
                            dve.wait_ge(s["corr_full"], 1)
                            dve.sem_inc(s["corr_full"], -1)
                        link(v.tensor_tensor(Ut, vT[:, :, th], uo[:, :, 0, h], ALU.subtract))
                        link(v.tensor_tensor(U[:, :, h], Ut, beta[:, :, th], ALU.mult))
                        dve.wait_ge(s["pr_ready"], 1)
                        dve.sem_inc(s["pr_ready"], -1)
                        for t0 in range(CS - 1):
                            n, at = WID[t0], j * CS + t0
                            pr = pairs[j][:, OFF[t0]:OFF[t0] + G * n].rearrange("p (g t) -> p g t", g=G)
                            link(v.tensor_tensor(Ut[:, :, 0:n], pr, U[:, :, at:at + 1].to_broadcast([P, G, n]), ALU.mult))
                            link(v.tensor_tensor(U[:, :, at + 1:at + 1 + n], U[:, :, at + 1:at + 1 + n], Ut[:, :, 0:n],
                                                 ALU.subtract))
                        dve.sem_inc(s["pairs_free"], 1)
                        link(v.transpose(delT, U))
                        dve.sem_inc(s["delT_ready"], 1)
                    dve.wait_ge(s["su_full"], 1)
                    dve.sem_inc(s["su_full"], -1)
                    dve.wait_ge(s["Sd_ready"], 1)
                    dve.sem_inc(s["Sd_ready"], -1)
                    link(v.tensor_tensor(S[:], Sd, su[:], ALU.add))
                    dve.sem_inc(s["S_ready"], 1)
                dve.sem_inc(s["x1_free"], 1)
                for hg in range(KD):
                    gs = slice(hg * B, (hg + 1) * B)
                    dve.wait_ge(s["o_r_ready"], 1)
                    dve.sem_inc(s["o_r_ready"], -1)
                    link(v.scalar_tensor_tensor(ctxT[:, gs, :].rearrange("p g t -> p (g t)"),
                                                oT[:, gs, :].rearrange("p g t -> p (g t)"), nw[:], qr[:],
                                                ALU.mult, ALU.mult))
                    dve.sem_inc(s["ctx_raw"], 1)
                    dve.sem_inc(s["o_copied"], 1)
                    k += 1
                for b in range(B):
                    dve.wait_ge(s["work_full_v"], 1)
                    dve.sem_inc(s["work_full_v"], -1)
                    link(v.tensor_tensor(y[:, b, :], work[k % 2][:], bo_sb[:], ALU.add))
                    dve.sem_inc(work_free[k % 2], 1)
                    token_stats(y, b)
                    k += 1
                token_norm()
                dve.wait_ge(s["y_ready"], 1)
                dve.sem_inc(s["y_ready"], -1)
                for b in range(B):
                    token_stats(x1, b)
                token_norm()
                for f in range(KD):
                    dve.wait_ge(s["work_full_v"], 1)
                    dve.sem_inc(s["work_full_v"], -1)
                    link(v.tensor_copy(xfT[:, f, :], work[k % 2][:]))
                    dve.sem_inc(work_free[k % 2], 1)
                    dve.sem_inc(s["z_ready"], 1)
                    k += 1
                dve.wait_ge(s["ss_ready"], 1)
                dve.sem_inc(s["ss_ready"], -1)
                link(v.tensor_scalar(ve[:], ssq[:], 1e-24, None, ALU.max))
                dve.sem_inc(s["var_ready"], 1)
                dve.wait_ge(s["rstd_raw"], 1)
                dve.sem_inc(s["rstd_raw"], -1)
                refine(rstd[:], ve[:], nt1[:])
                k += HID // P
                dve.wait_ge(s["work_full_v"], 1)
                dve.sem_inc(s["work_full_v"], -1)
                lw = work[k % 2][:, 0:2 * B * E].rearrange("p (b a e) -> p b a e", b=B, a=2)
                link(v.tensor_tensor(lt[:, 1], lw[:, :, 1, :], gb2_sb[:].unsqueeze(1).to_broadcast([P, B, E]), ALU.add))
                dve.sem_inc(s["lg_ready"], 1)
                link(v.tensor_tensor(lt[:, 0], lw[:, :, 0, :], rstd[:].unsqueeze(2).to_broadcast([P, B, E]), ALU.mult))
                dve.sem_inc(work_free[k % 2], 1)
                k += 1
                dve.wait_ge(s["sig_ready"], 1)
                dve.sem_inc(s["sig_ready"], -1)
                link(v.tensor_tensor(lt[:, 0], lt[:, 0], lt[:, 1], ALU.add))
                link(v.tensor_reduce(l1[:, 0, :], lt[:, 0], AX.X, ALU.max))
                link(v.tensor_tensor(lt[:, 2], lt[:, 0], l1[:, 0, :].unsqueeze(2).to_broadcast([P, B, E]), ALU.subtract))
                dve.sem_inc(s["d_ready"], 1)
                link(v.tensor_scalar(lt[:, 4], lt[:, 2], 0.0, -float(E), ALU.is_ge, ALU.mult))
                link(v.tensor_tensor(lt[:, 4], lt[:, 4], iota[:].unsqueeze(1).to_broadcast([P, B, E]), ALU.add))
                link(v.tensor_reduce(l1[:, 1, :], lt[:, 4], AX.X, ALU.min))
                link(v.tensor_tensor(oh[:], lt[:, 4], l1[:, 1, :].unsqueeze(2).to_broadcast([P, B, E]), ALU.is_equal))
                dve.sem_inc(s["oh_ready"], 1)
                dve.wait_ge(s["e_ready"], 1)
                dve.sem_inc(s["e_ready"], -1)
                link(v.tensor_reduce(l1[:, 2, :], lt[:, 3], AX.X, ALU.add))
                link(v.reciprocal(xfw[:, :, D], l1[:, 2, :]))
                link(v.tensor_copy(xfw[:, :, D + 1], tokf[:]))
                link(v.tensor_scalar(tokf[:], tokf[:], float(T), None, ALU.add))
                link(v.memset(xfw[:, :, D + 2:XSW], 0.0))
                dve.wait_ge(s["work_full_v"], 1)
                dve.sem_inc(s["work_full_v"], -1)
                w = work[k % 2]
                link(v.tensor_tensor(lt[:, 5], w[:, 0:B * E].rearrange("p (b e) -> p b e", b=B),
                                     base[:].unsqueeze(1).to_broadcast([P, B, E]), ALU.add))
                link(v.tensor_tensor(base[:], base[:], w[:, B * E:(B + 1) * E], ALU.add))
                dve.sem_inc(work_free[k % 2], 1)
                k += 1
                link(v.tensor_tensor(lt[:, 5], lt[:, 5], col[:, 1, :].unsqueeze(1).to_broadcast([P, B, E]), ALU.mult))
                link(v.tensor_tensor(lt[:, 5], lt[:, 5], col[:, 0, :].unsqueeze(1).to_broadcast([P, B, E]), ALU.add))
                link(v.tensor_tensor(lt[:, 5], lt[:, 5], oh[:], ALU.mult))
                link(v.tensor_reduce(slotf[:], lt[:, 5], AX.X, ALU.add))
                link(v.tensor_copy(slot[:], slotf[:]))
                dve.sem_inc(s["slot_ready"], 1)
                link.restart()
            link(v.tensor_tensor(tb[:, 2, :], base[:], col[:, 1, :], ALU.mult))
            link(v.tensor_tensor(cnt[:], tb[:, 2, :], col[:, 2, :], ALU.add))
            link(v.tensor_scalar(tabf[:, 0, :], krow[:], float(P), None, ALU.mult))
            link(v.tensor_tensor(tb2[:], base[:].unsqueeze(2).to_broadcast([P, E, P]),
                                 tabf[:, 0, :].unsqueeze(1).to_broadcast([P, E, P]), ALU.is_gt))
            link(v.tensor_reduce(tb[:, 0, :], tb2[:], AX.X, ALU.add))
            link(v.tensor_copy(tb[:, 1, :], tb[:, 0, :]))
            for e in range(1, E):
                link(v.tensor_tensor(tb[:, 1, e:e + 1], tb[:, 1, e:e + 1], tb[:, 1, e - 1:e], ALU.add))
            link(v.tensor_tensor(tb2[:], tb[:, 1, :].unsqueeze(2).to_broadcast([P, E, P]),
                                 krow[:].unsqueeze(1).to_broadcast([P, E, P]), ALU.is_le))
            link(v.tensor_reduce(tabf[:, 1, :], tb2[:].rearrange("p e m -> p m e"), AX.X, ALU.add))
            for n, step in ((2, tb[:, 0, :]), (3, col[:, 3, :]), (4, col[:, 4, :])):
                link(v.tensor_tensor(tb3[:], tb2[:], step.unsqueeze(2).to_broadcast([P, E, P]), ALU.mult))
                link(v.tensor_reduce(tabf[:, n, :], tb3[:].rearrange("p e m -> p m e"), AX.X, ALU.add))
            link(v.tensor_tensor(tabf[:, 2, :], krow[:], tabf[:, 2, :], ALU.subtract))
            link(v.tensor_scalar(tabf[:, 4, :], tabf[:, 4, :], 1.0, float(P), ALU.add, ALU.mult))
            link(v.tensor_tensor(tabf[:, 4, :], tabf[:, 4, :], tabf[:, 2, :], ALU.mult))
            link(v.tensor_tensor(tab[:, 1, :], tabf[:, 3, :], tabf[:, 4, :], ALU.add))
            link(v.tensor_scalar(tab[:, 0, :], tabf[:, 1, :], float(E - 1), None, ALU.min))
            dve.sem_inc(s["table_ready"], 1)
            for n in ("m_free", "m_wfree", "m_s"):
                dve.sem_inc(s[n], 1)
            link.restart()
            with dve.Fori(0, NM):
                def row_norm(dst):
                    link(v.bn_stats(mst[:], ya))
                    link(v.bn_aggr(mmv[:], mst[:]))
                    link(v.tensor_scalar(ms[:, 0:1], mmv[:, 1:2], 1e-5, None, ALU.add))
                    dve.sem_inc(s["m_v"], 1)
                    dve.wait_ge(s["m_r"], 1)
                    dve.sem_inc(s["m_r"], -1)
                    refine(ms[:, 1:2], ms[:, 0:1], ms[:, 2:3])
                    link(v.tensor_scalar(dst, ya, mmv[:, 0:1], ms[:, 1:2], ALU.subtract, ALU.mult))

                dve.wait_ge(s["m_y"], 1)
                dve.sem_inc(s["m_y"], -1)
                dve.sem_inc(s["m_wfree"], 1)
                link(v.scalar_tensor_tensor(ya, bcast[:], xs[:, D:D + 1], xs[:, 0:D], ALU.mult, ALU.add))
                dve.sem_inc(s["bc_free"], 1)
                dve.wait_ge(s["m_s"], 1)
                dve.sem_inc(s["m_s"], -1)
                link(v.tensor_copy(toki[:], xs[:, D + 1:D + 2]))
                dve.sem_inc(s["m_free"], 1)
                link(v.tensor_tensor(ya, ya, pb_sb, ALU.add))
                row_norm(ya)
                link(v.tensor_tensor(ya, ya, lg_sb, ALU.mult))
                link(v.tensor_tensor(ya, ya, lb_sb, ALU.add))
                row_norm(z)
                dve.sem_inc(s["m_z"], 1)
                link.restart()


def column_rows():
    import numpy as np
    e = np.arange(E)
    front, sign = e // 2 * SHARE, 1 - 2 * (e % 2)
    first = np.where(e % 2, front + SHARE - 1, front)
    behind = np.where(e % 2, first + 1 - P, first)
    return np.stack([first, sign, behind, np.diff(behind, append=PADROW), np.diff(sign, append=0)])


def constants():
    import numpy as np
    p = np.arange(P)
    same = (p[:, None] // DH) == (p[None, :] // DH)
    squares = np.stack([np.eye(P), same, same & (p[:, None] <= p[None, :]), p[:, None] < p[None, :],
                        np.ones((P, P))], axis=1)
    sel = same[:, None, :] & ((p % DH)[:, None] == np.arange(C)[None, :])[:, :, None]
    mask = np.where(np.arange(C)[None, :] >= (p % DH)[:, None], 0.0, NEG)
    iota = np.broadcast_to(np.arange(E), (P, E))
    pad = np.zeros((P, XSW))
    pad[:, D + 1] = 2 * ROWS
    tok = p[:, None] + L * np.arange(B)[None, :]
    row = np.broadcast_to(p, (P, P))
    col = np.broadcast_to(column_rows(), (P, 5, E))
    return {n: np.ascontiguousarray(a, dtype=np.float32) for n, a in
            dict(c_sq=squares, c_sel=sel, c_mask=mask, c_iota=iota, c_pad=pad, c_tok=tok, c_row=row, c_col=col).items()}


def kernel(**inputs):
    import numpy as np
    import concourse.bacc as bacc
    from concourse.bass_utils import run_bass_kernel_spmd as run

    a = {n[3:]: np.asarray(v) for n, v in inputs.items()}
    laid = {
        "x": a["attn_x"],
        "w_in": np.concatenate([a[f"attn_W{n}"].T for n in "qkvbg"], axis=1),
        "wa": a["attn_Wa"].T, "dt_bias": a["attn_dt_bias"], "a_log": a["attn_A_log"], "norm_w": a["attn_norm_w"],
        "wo": a["attn_Wo"].T, "bo": a["attn_bo"], "col_emb": a["ffn_col_emb"],
        "gw1": a["ffn_gate_w1"], "gb1": a["ffn_gate_b1"].reshape(HID // P, P).T, "gw2": a["ffn_gate_w2"], "gb2": a["ffn_gate_b2"],
        "w_cols": a["ffn_W_cols"], "b_cols": a["ffn_b_cols"][:, :, None], "proj_w": a["ffn_proj_w"].reshape(E, N, D),
        "proj_b": a["ffn_proj_b"], "ln_g": a["ffn_ln_g"], "ln_b": a["ffn_ln_b"], **constants(),
    }
    nc = bacc.Bacc("TRN2", target_bir_lowering=False, num_devices=1)
    arrays, args = {}, {}
    for name, v in laid.items():
        arrays[f"in_{name}"] = v = np.ascontiguousarray(v)
        args[name] = nc.dram_tensor(f"in_{name}", v.shape, mybir.dt.from_np(v.dtype), kind="ExternalInput").ap()
    out = nc.dram_tensor("out", (B, L, D), F32, kind="ExternalOutput").ap()
    xs_dram = nc.dram_tensor("xs_rows", (PADROW + P, XSW), F32, kind="Internal").ap()
    sandwich_kernel(nc, out=out, xs_dram=xs_dram, **args)
    return run(nc, [arrays], core_ids=[0]).results[0]["out"]
```

```python
import math
from contextlib import ExitStack

import concourse.bass as bass
from concourse import mybir

F32 = mybir.dt.float32
I32 = mybir.dt.int32
U32 = mybir.dt.uint32
ALU = mybir.AluOpType
ACT = mybir.ActivationFunctionType
AX = mybir.AxisListType

B, L, D = 4, 2048, 512
H, DH = 16, 32
P = 128
KD = D // P
HP = P // DH
T = 64
NT = L // T
BL = P // T
TB = B // BL
BT = B * T
C = DH
NC = T // C
CS = C // 2
G = KD * B
NP = 5
E, N = 16, 128
HID = 256
ROWS = B * L
XSW = D + 4
SHARE = ROWS + 2 * P
PADROW = E // 2 * SHARE
MQ = 4
NM = -(-(ROWS // P + E - 1) // MQ) * MQ
RSQRT_GUESS = float(0x5f3759df)
NEG = -1.0e30

WID = [CS - 1 - s for s in range(CS - 1)]
PACKS = [(0, 1, 14), (2, 3, 10), (4, 5, 6), (7, 8, 9, 11, 12, 13)]
ORDER = [s for pack in PACKS for s in pack]
OFF = [G * sum(WID[s] for s in ORDER[:ORDER.index(t)]) for t in range(CS - 1)]
NPAIR = G * sum(WID)
GU = G // 2
NW = 3

TURNS = [("pair", 0, 1, i) for i in range(len(PACKS))] + [
    ("xT", 0), ("xT", 1), ("rms", 0), ("rms", 1), ("qk", 0), ("alpha",), ("qk", 1), ("ss", 0)] + [
    ("pair", 1, 0, i) for i in range(len(PACKS))] + [
    ("wo", 0), ("wo", 1), ("qk", 2), ("ss", 1), ("G", 0), ("G", 1), ("qk", 3)] + [
    ("pair", 1, 1, i) for i in range(len(PACKS))] + [
    ("ss", 2), ("gate", 0), ("ss", 3), ("gate", 1), ("beta", 0), ("xfT", 0), ("xfT", 1), ("beta", 1), ("hid",)] + [
    ("pair", 0, 0, i) for i in range(len(PACKS))] + [
    ("v", 0), ("logits",), ("v", 1), ("rank",)]
BANK = {use: n % NW for n, use in enumerate(TURNS)}


class Chain:

    def __init__(self, eng, sem):
        self.eng, self.sem, self.n = eng, sem, 0

    def __call__(self, ins, behind=0):
        self.n += 1
        ins.then_inc(self.sem, 1)
        self.eng.wait_ge(self.sem, self.n - behind)

    def restart(self):
        self.eng.sem_inc(self.sem, -self.n)
        self.n = 0


def sandwich_kernel(nc, x, w_in, wa, dt_bias, a_log, norm_w, wo, bo, col_emb, gw1, gb1, gw2, gb2,
                    w_cols, b_cols, proj_w, proj_b, ln_g, ln_b,
                    c_sq, c_sel, c_mask, c_iota, c_pad, c_tok, c_row, c_col, out, xs_dram):
    with ExitStack() as ctx:
        def sb(name, shape, dt=F32):
            return ctx.enter_context(nc.sbuf_tensor(name, shape, dt))

        def ps(name, shape):
            return ctx.enter_context(nc.psum_tensor(name, shape, F32))

        def sem(name):
            return ctx.enter_context(nc.semaphore(name))

        squares = sb("squares", [P, 5, P])
        ident, blk1, ucum, ustrict, ones = (squares[:, i, :] for i in range(5))
        sel = sb("sel", [P, C, P])
        mask = sb("mask", [P, C])
        iota = sb("iota", [P, E])
        w_sb = sb("w_sb", [P, KD, NP * D])
        wa_sb = sb("wa_sb", [P, KD, H])
        dtb = sb("dtb", [P, H])
        neg_a = sb("neg_a", [P, H])
        nw = sb("nw", [P, 1])
        wo_sb = sb("wo_sb", [P, KD, D])
        bo_sb = sb("bo_sb", [P, D])
        gw1_sb = sb("gw1_sb", [P, KD, HID])
        gb1_sb = sb("gb1_sb", [P, HID // P])
        gw2_sb = sb("gw2_sb", [P, HID // P, E])
        gb2_sb = sb("gb2_sb", [P, E])
        ceT = sb("ceT", [P, KD, E])
        ce_s = sb("ce_s", [E, 4])
        eps6 = sb("eps6", [P, 1])
        lnq = sb("lnq", [P, 1])

        xt = sb("xt", [P, TB, D])
        xn = sb("xn", [P, TB, D])
        xT = sb("xT", [P, KD, BT])
        stats = sb("stats", [P, TB, 6])
        mv = sb("mv", [P, TB, 2])
        ve = sb("ve", [P, TB])
        rstd = sb("rstd", [P, TB])
        nt1 = sb("nt1", [P, TB])
        nmr = sb("nmr", [P, TB])
        alog = sb("alog", [P, 4, TB * H])
        la = sb("la", [P, TB, H])
        eg = sb("eg", [P, G, T])
        eg_end = [sb(f"eg_end{p}", [P, G, NC]) for p in range(2)]
        dec = sb("dec", [P, G, T])
        qraw = [sb(f"qraw{n}", [P, GU * T]) for n in range(2)]
        qsq = [sb(f"qsq{n}", [P, GU * T]) for n in range(2)]
        qr = [sb(f"qr{n}", [P, GU * T]) for n in range(2)]
        sg = sb("sg", [P, GU * T])
        kq = sb("kq", [P, G, NC, 2, C])
        vT = sb("vT", [P, G, T])
        beta = sb("beta", [P, G, T])
        silu = [sb(f"silu{p}", [P, G, T]) for p in range(2)]
        A = [sb(f"A{c}", [P, G, 2, C]) for c in range(NC)]
        kqd = [sb(f"kqd{c}", [P, G, 2, C]) for c in range(NC)]
        kd = [sb(f"kd{c}", [P, G, C]) for c in range(NC)]
        delT = [sb(f"delT{c}", [P, G, C]) for c in range(NC)]
        pairs = [sb(f"pairs{j}", [P, NPAIR]) for j in range(2)]
        S = sb("S", [P, G, DH])
        Sd = sb("Sd", [P, G, DH])
        U = sb("U", [P, G, C])
        Ut = sb("Ut", [P, G, CS])
        oT = sb("oT", [P, G, T])
        ctxT = sb("ctxT", [P, G, T])
        y = sb("y", [P, TB, D])
        x1 = sb("x1", [P, TB, D])
        xfw = sb("xfw", [P, TB, XSW])
        ssq = sb("ssq", [P, TB])
        lt = sb("lt", [P, 6, TB, E])
        l1 = sb("l1", [P, 4, TB])
        oh = sb("oh", [P, TB, E])
        base = sb("base", [P, E])
        slotf = sb("slotf", [P, TB])
        slot = sb("slot", [P, TB], I32)
        tok0 = sb("tok0", [P, TB])
        tokf = sb("tokf", [P, TB])
        ctx_flat = ctxT[:].rearrange("p g t -> p (g t)")
        gsb = qsq[1][:], ctx_flat[:, 0:GU * T]
        gT = qraw[1][:], ctx_flat[:, GU * T:2 * GU * T]
        lax = xt[:].rearrange("p b (h e) -> p b h e", h=H)
        xfT = xn[:].rearrange("p b d -> p (b d)").rearrange("p (k t) -> p k t", k=KD)
        hT = ctx_flat[:, 0:HID // P * BT].rearrange("p (n t) -> p n t", n=HID // P)
        junk = y
        ce = qsq[0][0:E, :]
        tabf = A[0][:].rearrange("p g a t -> p (g a t)")[:, 0:6 * P].rearrange("p (n m) -> p n m", n=6)
        vT_flat, beta_flat, eg_flat, dec_flat = (a[:].rearrange("p g t -> p (g t)") for a in (vT, beta, eg, dec))
        kq_flat = kq[:].rearrange("p g c a t -> p (g c a t)")
        sel_flat = sel[:].rearrange("p s l -> p (s l)")
        w_flat = w_sb[:].rearrange("p k n -> p (k n)")

        def side_by_side(flat, at, n, width):
            return [flat[:, at + i * width:at + (i + 1) * width] for i in range(n)]

        wc = [a.rearrange("p (k n) -> p k n", k=KD) for a in side_by_side(w_flat, 0, MQ, D)]
        pw = side_by_side(w_flat, MQ * D, MQ, D)
        pb_sb, lg_sb, lb_sb = side_by_side(w_flat, 2 * MQ * D, 3, D)
        xs = side_by_side(w_flat, (2 * MQ + 3) * D, MQ, XSW)
        pad = w_flat[:, (2 * MQ + 3) * D + MQ * XSW:(2 * MQ + 3) * D + (MQ + 1) * XSW]
        xsb = [a[:, n * D:(n + 1) * D] for a in (vT_flat, beta_flat) for n in range(2)]
        ya = [a[:, n * D:(n + 1) * D] for a in (eg_flat, dec_flat) for n in range(2)]
        z = side_by_side(sel_flat, 0, MQ, D)
        xsT = [a.rearrange("p (k t) -> p k t", k=KD) for a in side_by_side(kq_flat, 0, 2, D)]
        hm = side_by_side(kq_flat, 2 * D, 2, P)
        tb2, tb3 = (a.rearrange("p (e m) -> p e m", e=E) for a in side_by_side(sel_flat, 0, 2, E * P))
        tb = sb("tb", [P, 10, E])
        krow = sb("krow", [P, P])
        col = sb("col", [P, 5, E])
        tab = sb("tab", [P, 2, P], I32)
        cnt = sb("cnt", [P, E], I32)
        toki = sb("toki", [P, MQ], I32)
        bc = sb("bc", [P, MQ])
        mst = sb("mst", [P, 2, 6])
        mmv = sb("mmv", [P, 2, 2])
        ms = sb("ms", [P, 2, MQ, 2])
        mt = sb("mt", [P, 3, 2])

        work = [ps(f"work{i}", [P, 512]) for i in range(NW)]
        kkq = ps("kkq", [P, G, 2, C])
        uk = ps("uk", [P, G, C])
        uq = ps("uq", [P, G, C])
        su = ps("su", [P, G, DH])
        kkq_flat = kkq[:].rearrange("p g a t -> p (g a t)")
        m_tp = [w[:] for w in work[0:2]]
        m_hp = [a[:].rearrange("p g t -> p (g t)")[:, 0:P] for a in (uk, uq)]
        m_yp = [kkq_flat[:, n * D:(n + 1) * D] for n in range(2)]

        loaded = sem("loaded")
        dve_step, act_step, pool_step = sem("dve_step"), sem("act_step"), sem("pool_step")
        names = """x_loaded xt_free xres_loaded x1_free x1_ready store_done
            norm_ready xn_ready xT_full xT_ready alpha_full la_e_ready la_l_ready la_ready lax_ready
            G_full g_copied gT_ready diff_ready dec_ready eg_ready
            qk_full q_sq_ready ss_full q_r_ready qraw_free kq_free kq_ready_pe kq_ready_p
            v_full beta_full gate_full vb_ready beta_ready vb_free gate_ready sg_free
            pair_full pr_copied pr_ready pairs_free kkq_full kkq_free A_ready kt_ready kd_ready kqd_ready
            uk_full uq_free corr_full delT_ready S_ready S_ready_p su_full Sd_ready o_full
            o_sq_ready rms_full o_r_ready ctx_raw o_copied ctx_ready wo_full zn_ready y_ready
            xf_ready xfT_full xfT_ready ss_ready hid_full h_ready logits_full lg_ready sig_ready d_ready e_ready
            oh_ready rank_full slot_ready scat_done
            ce_sq ce_n ce_T base_ready setup_v setup_a table_ready
            m_xs_p m_xsb m_t m_t_free m_xsT m_h m_h_free m_hm m_y m_y_free m_n m_free m_wfree m_add m_pad
            """.split()
        s = {n: sem(n) for n in names}
        m_xs, m_wc = ([sem(f"{n}{u}") for u in range(MQ)] for n in ("m_xs", "m_wc"))
        work_free = [sem(f"work{i}_free") for i in range(NW)]

        def bank(*use):
            return work[BANK[use]][:]

        def bank_free(*use):
            return work_free[BANK[use]]

        def unit(a, hp):
            return a[:, hp * GU:(hp + 1) * GU]

        def flat(a):
            return a.rearrange("p g t -> p (g t)")

        def per_chunk(a):
            return a.rearrange("p (g c t) -> p g c t", g=GU, c=NC)

        block = ctx.enter_context(nc.Block())
        x_v = x.rearrange("(bh bl) (i t) d -> bl i t bh d", bl=BL, t=T)
        out_v = out.rearrange("(bh bl) (i t) d -> bl i t bh d", bl=BL, t=T)
        out_rows = out.rearrange("b l d -> (b l) d")

        loads = [
            (squares[:], c_sq), (sel[:], c_sel), (mask[:], c_mask), (iota[:], c_iota), (tok0[:], c_tok), (krow[:], c_row), (col[:], c_col),
            (w_sb[:], w_in.rearrange("(k p) n -> p k n", p=P)),
            (wa_sb[:], wa.rearrange("(k p) n -> p k n", p=P)),
            (dtb[:], dt_bias.partition_broadcast(P)), (neg_a[:], a_log.partition_broadcast(P)),
            (wo_sb[:], wo.rearrange("(k p) n -> p k n", p=P)), (bo_sb[:], bo.partition_broadcast(P)),
            (gw1_sb[:], gw1.rearrange("(k p) n -> p k n", p=P)),
            (gb1_sb[:], gb1),
            (gw2_sb[:], gw2.rearrange("(k p) n -> p k n", p=P)), (gb2_sb[:], gb2.partition_broadcast(P)),
            (ce, col_emb),
        ] + [(nw[DH * h:DH * h + DH, :], norm_w.rearrange("(p o) -> p o", o=1)) for h in range(HP)]
        ALL = 16 * len(loads)

        @block.sync
        def _(sp):
            for dst, src in loads:
                sp.dma_start(dst, src).then_inc(loaded, 16)
            def load_tokens(i):
                sp.wait_ge(s["xt_free"], 1)
                sp.sem_inc(s["xt_free"], -1)
                for bl in range(BL):
                    sp.dma_start(xt[bl * T:(bl + 1) * T], x_v[bl, bass.ds(i, 1)].rearrange("i t b d -> (i t) b d"))\
                        .then_inc(s["x_loaded"], 16)

            def add_and_store(i):
                sp.wait_ge(s["x1_free"], 1)
                sp.sem_inc(s["x1_free"], -1)
                for bl in range(BL):
                    sp.dma_start(x1[bl * T:(bl + 1) * T], x_v[bl, bass.ds(i, 1)].rearrange("i t b d -> (i t) b d"))\
                        .then_inc(s["xres_loaded"], 16)
                sp.wait_ge(s["x1_ready"], 1)
                sp.sem_inc(s["x1_ready"], -1)
                for bl in range(BL):
                    sp.dma_start(out_v[bl, bass.ds(i, 1)].rearrange("i t b d -> (i t) b d"), x1[bl * T:(bl + 1) * T])\
                        .then_inc(s["store_done"], 16)
                sp.wait_ge(s["store_done"], 16 * BL)
                sp.sem_inc(s["store_done"], -(16 * BL))

            load_tokens(0)
            load_tokens(1)
            with sp.Fori(0, NT - 2) as i:
                load_tokens(i + 2)
                add_and_store(i)
            add_and_store(NT - 2)
            add_and_store(NT - 1)
            sp.wait_ge(s["table_ready"], 1)
            sp.sem_inc(s["table_ready"], -1)
            for dst, src in ((pad, c_pad), (pb_sb, proj_b.partition_broadcast(P)), (lg_sb, ln_g.partition_broadcast(P)),
                             (lb_sb, ln_b.partition_broadcast(P))):
                sp.dma_start(dst, src).then_inc(s["m_pad"], 16)
            sp.wait_ge(s["m_pad"], 64)
            sp.sem_inc(s["m_pad"], -64)
            for e in range(E):
                behind = nc.sync.value_load(cnt[0:1, e:e + 1], min_val=0, max_val=PADROW)
                sp.dma_start(xs_dram[bass.ds(behind, P)], pad).then_inc(s["m_pad"], 16)
            sp.dma_start(xs_dram[PADROW:PADROW + P], pad).then_inc(s["m_pad"], 16)
            sp.wait_ge(s["m_pad"], 16 * (E + 1))
            sp.sem_inc(s["m_pad"], -(16 * (E + 1)))
            sp.wait_ge(s["scat_done"], 16 * TB * NT)
            with sp.Fori(0, NM // MQ) as q:
                for u in range(MQ):
                    e_m = nc.sync.value_load(tab[0:1, 0, bass.ds(q * MQ + u, 1)], min_val=0, max_val=E - 1)
                    r_m = nc.sync.value_load(tab[0:1, 1, bass.ds(q * MQ + u, 1)], min_val=0, max_val=PADROW)
                    sp.wait_ge(s["m_free"], 1)
                    sp.sem_inc(s["m_free"], -1)
                    sp.dma_start(xs[u], xs_dram[bass.ds(r_m, P)]).then_inc(m_xs[u], 16)
                    sp.wait_ge(s["m_wfree"], 1)
                    sp.sem_inc(s["m_wfree"], -1)
                    sp.dma_start(wc[u], w_cols[bass.ds(e_m, 1)].rearrange("e (k p) n -> p (e k) n", p=P))\
                        .then_inc(m_wc[u], 16)
                    sp.dma_start(bc[:, u:u + 1], b_cols[bass.ds(e_m, 1)].rearrange("e n o -> (e n) o"))\
                        .then_inc(m_wc[u], 16)
                    sp.dma_start(pw[u], proj_w[bass.ds(e_m, 1)].rearrange("e n d -> (e n) d")).then_inc(m_wc[u], 16)

        @block.tensor
        def _(pe):
            def into(*use):
                pe.wait_ge(bank_free(*use), 1)
                pe.sem_inc(bank_free(*use), -1)
                return bank(*use)

            def project(name, j, hp):
                w = into(name, hp if name != "qk" else 2 * j + hp)
                for half in range(2):
                    hg = 2 * hp + half
                    for f in range(KD):
                        mm = pe.matmul(w[:, half * BT:(half + 1) * BT], w_sb[:, f, j * D + hg * P:j * D + (hg + 1) * P],
                                       xT[:, f, :], start=(f == 0), stop=(f == KD - 1))
                mm.then_inc(s[name + "_full"], 1)

            def squares_sum(n):
                pe.wait_ge(s["q_sq_ready"], 1)
                pe.sem_inc(s["q_sq_ready"], -1)
                w = into("ss", n)
                pe.matmul(w, blk1, qsq[n % 2][:], start=True, stop=True).then_inc(s["ss_full"], 1)

            def turn(name, src, n):
                w = into(name, n)
                for half in range(2):
                    f = 2 * n + half
                    for tb in range(TB):
                        mm = pe.transpose(w[:, half * BT + tb * P:half * BT + (tb + 1) * P], src[:, tb, f * P:(f + 1) * P], ident)
                mm.then_inc(s[name + "_full"], 1)

            def on_tiles(product):
                for g in range(G):
                    for h in range(HP):
                        mm = product(g, slice(DH * h, DH * h + DH), slice(DH * h, DH * h + CS))
                return mm

            def key_products(c):
                pe.wait_ge(s["kkq_free"], 1)
                pe.sem_inc(s["kkq_free"], -1)
                on_tiles(lambda g, q, q_half: pe.matmul(
                    kkq[q, g], kq[q, g, c, 0, :], kq[q, g, c].rearrange("p a t -> p (a t)"),
                    start=True, stop=True)).then_inc(s["kkq_full"], 1)

            def spread_pairs(c, j):
                for i, pack in enumerate(PACKS):
                    w = into("pair", c, j, i)
                    o = 0
                    for t0 in pack:
                        n = G * WID[t0]
                        mm = pe.matmul(w[:, o:o + n], sel[:, j * CS + t0, :], A[c][:, :, 0, j * CS + t0 + 1:(j + 1) * CS],
                                       start=(o == 0), stop=True, skip_group_check=True)
                        o += n
                    mm.then_inc(s["pair_full"], 1)

            def state_to_u(c):
                pe.wait_ge(s["kqd_ready"], 1)
                pe.sem_inc(s["kqd_ready"], -1)
                pe.wait_ge(s["S_ready"], 1)
                pe.sem_inc(s["S_ready"], -1)
                on_tiles(lambda g, q, q_half: pe.matmul(
                    uk[q, g], S[q, g, :], kqd[c][q, g, 0, :],
                    start=(g == 0), stop=True, skip_group_check=True)).then_inc(s["uk_full"], 1)

            def first_half_to_u(c):
                pe.wait_ge(s["delT_ready"], 1)
                pe.sem_inc(s["delT_ready"], -1)
                on_tiles(lambda g, q, q_half: pe.matmul(
                    uk[q, g, CS:C], delT[c][q_half, g, :], A[c][q_half, g, 0, CS:C],
                    start=False, stop=True, skip_group_check=True)).then_inc(s["corr_full"], 1)

            def state_to_outputs(c):
                pe.wait_ge(s["uq_free"], 1)
                pe.sem_inc(s["uq_free"], -1)
                on_tiles(lambda g, q, q_half: pe.matmul(
                    uq[q, g], S[q, g, :], kqd[c][q, g, 1, :], start=(g == 0), stop=True, skip_group_check=True))

            def chunk_to_outputs(c):
                on_tiles(lambda g, q, q_half: pe.matmul(
                    uq[q, g], delT[c][q, g, :], A[c][q, g, 1, :],
                    start=False, stop=True, skip_group_check=True)).then_inc(s["o_full"], 1)

            def change_state(c):
                pe.wait_ge(s["delT_ready"], 1)
                pe.sem_inc(s["delT_ready"], -1)
                pe.wait_ge(s["kd_ready"], 1)
                pe.sem_inc(s["kd_ready"], -1)
                on_tiles(lambda g, q, q_half: pe.matmul(
                    su[q, g, :], kd[c][q, g, :], delT[c][q, g, :], start=True, stop=True)).then_inc(s["su_full"], 1)

            def log_alpha():
                w = into("alpha")
                for tb in range(TB):
                    for f in range(KD):
                        mm = pe.matmul(w[:, tb * H:(tb + 1) * H], xT[:, f, tb * P:(tb + 1) * P], wa_sb[:, f, :],
                                       start=(f == 0), stop=(f == KD - 1))
                mm.then_inc(s["alpha_full"], 1)

            def decays(hp):
                w = into("G", hp)
                for half in range(2):
                    hg = 2 * hp + half
                    for tb in range(TB):
                        mm = pe.matmul(w[:, half * BT + tb * P:half * BT + (tb + 1) * P],
                                       lax[:, tb, hg * HP:(hg + 1) * HP, :].rearrange("p h e -> p (h e)"), ucum,
                                       start=True, stop=True)
                mm.then_inc(s["G_full"], 1)

            def outputs_squares_sum(hp):
                pe.wait_ge(s["o_sq_ready"], 1)
                pe.sem_inc(s["o_sq_ready"], -1)
                w = into("rms", hp)
                pe.matmul(w, blk1, qsq[hp][:], start=True, stop=True).then_inc(s["rms_full"], 1)

            def output_projection(tb):
                w = into("wo", tb)
                for hg in range(KD):
                    mm = pe.matmul(w, flat(ctxT[:, hg * B + tb * BL:hg * B + (tb + 1) * BL, :]), wo_sb[:, hg, :],
                                   start=(hg == 0), stop=(hg == KD - 1))
                mm.then_inc(s["wo_full"], 1)

            def gate_hidden():
                w = into("hid")
                for n in range(HID // P):
                    for f in range(KD):
                        mm = pe.matmul(w[:, n * BT:(n + 1) * BT], gw1_sb[:, f, n * P:(n + 1) * P], xfT[:, f, :],
                                       start=(f == 0), stop=(f == KD - 1))
                mm.then_inc(s["hid_full"], 1)

            def gate_logits():
                pe.wait_ge(s["h_ready"], 1)
                pe.sem_inc(s["h_ready"], -1)
                w = into("logits")
                for tb in range(TB):
                    tok = slice(tb * P, (tb + 1) * P)
                    for f in range(KD):
                        pe.matmul(w[:, tb * 2 * E:tb * 2 * E + E], xfT[:, f, tok], ceT[:, f, :],
                                  start=(f == 0), stop=(f == KD - 1))
                    for n in range(HID // P):
                        mm = pe.matmul(w[:, tb * 2 * E + E:(tb + 1) * 2 * E], hT[:, n, tok], gw2_sb[:, n, :],
                                       start=(n == 0), stop=(n == HID // P - 1))
                mm.then_inc(s["logits_full"], 1)

            def ranks():
                pe.wait_ge(s["oh_ready"], 1)
                pe.sem_inc(s["oh_ready"], -1)
                w = into("rank")
                pe.matmul(w[:, 0:TB * E], ustrict, oh[:].rearrange("p b e -> p (b e)"), start=True, stop=False,
                          skip_group_check=True)
                for n in range(1, TB):
                    pe.matmul(w[:, n * E:TB * E], ones, oh[:, 0:TB - n, :].rearrange("p b e -> p (b e)"),
                              start=False, stop=False, skip_group_check=True)
                for tb in range(TB):
                    mm = pe.matmul(w[:, TB * E:(TB + 1) * E], ones, oh[:, tb, :], start=False, stop=(tb == TB - 1),
                                   skip_group_check=True)
                mm.then_inc(s["rank_full"], 1)

            def step(p, chain, after, ahead):
                if chain:
                    spread_pairs(0, 1)
                    state_to_u(0)
                if after:
                    chunk_to_outputs(NC - 1)
                if ahead:
                    pe.wait_ge(s["xn_ready"], TB)
                    pe.sem_inc(s["xn_ready"], -TB)
                    turn("xT", xn, 0)
                    turn("xT", xn, 1)
                if chain:
                    key_products(1)
                if after:
                    outputs_squares_sum(0)
                    outputs_squares_sum(1)
                if ahead:
                    pe.wait_ge(s["xT_ready"], 2)
                    pe.sem_inc(s["xT_ready"], -2)
                    project("qk", 0, 0)
                    log_alpha()
                    project("qk", 0, 1)
                if chain:
                    first_half_to_u(0)
                if ahead:
                    squares_sum(0)
                if chain:
                    pe.wait_ge(s["A_ready"], 1)
                    pe.sem_inc(s["A_ready"], -1)
                    spread_pairs(1, 0)
                    state_to_outputs(0)
                if after:
                    pe.wait_ge(s["ctx_ready"], 2)
                    pe.sem_inc(s["ctx_ready"], -2)
                    output_projection(0)
                    output_projection(1)
                if ahead:
                    project("qk", 1, 0)
                    squares_sum(1)
                    pe.wait_ge(s["lax_ready"], 1)
                    pe.sem_inc(s["lax_ready"], -1)
                    decays(0)
                    decays(1)
                if chain:
                    change_state(0)
                if ahead:
                    project("qk", 1, 1)
                if chain:
                    state_to_u(1)
                    spread_pairs(1, 1)
                    chunk_to_outputs(0)
                if ahead:
                    squares_sum(2)
                    project("gate", 4, 0)
                    squares_sum(3)
                    project("gate", 4, 1)
                if chain:
                    first_half_to_u(1)
                if ahead:
                    project("beta", 3, 0)
                    pe.wait_ge(s["kq_ready_pe"], 4)
                    pe.sem_inc(s["kq_ready_pe"], -4)
                    key_products(0)
                if after:
                    pe.wait_ge(s["xf_ready"], TB)
                    pe.sem_inc(s["xf_ready"], -TB)
                    turn("xfT", xfw, 0)
                    turn("xfT", xfw, 1)
                if ahead:
                    project("beta", 3, 1)
                if chain:
                    state_to_outputs(1)
                if after:
                    pe.wait_ge(s["xfT_ready"], 2)
                    pe.sem_inc(s["xfT_ready"], -2)
                    gate_hidden()
                if ahead:
                    pe.wait_ge(s["A_ready"], 1)
                    pe.sem_inc(s["A_ready"], -1)
                    spread_pairs(0, 0)
                    project("v", 2, 0)
                if after:
                    gate_logits()
                if ahead:
                    project("v", 2, 1)
                if after:
                    ranks()
                if chain:
                    change_state(1)

            pe.wait_ge(loaded, ALL)
            pe.wait_ge(s["ce_n"], 1)
            pe.sem_inc(s["ce_n"], -1)
            for k in range(KD):
                mm = pe.transpose(work[0][:, k * E:(k + 1) * E], ce[:, k * P:(k + 1) * P], ident[0:E, 0:E])
            mm.then_inc(s["ce_T"], 1)
            step(1, False, False, True)
            step(0, True, False, True)
            with pe.Fori(0, NT // 2 - 1):
                step(1, True, True, True)
                step(0, True, True, True)
            step(1, True, True, False)
            step(0, False, True, False)
            with pe.Fori(0, NM // MQ):
                for pair in range(MQ // 2):
                    tiles = (2 * pair, 2 * pair + 1)
                    for u in tiles:
                        pe.wait_ge(m_xs[u], 16)
                        pe.sem_inc(m_xs[u], -16)
                        pe.sem_inc(s["m_xs_p"], 1)
                        pe.wait_ge(s["m_t_free"], 1)
                        pe.sem_inc(s["m_t_free"], -1)
                        for f in range(KD):
                            mm = pe.transpose(m_tp[u % 2][:, f * P:(f + 1) * P], xs[u][:, f * P:(f + 1) * P], ident)
                        mm.then_inc(s["m_t"], 1)
                    for u in tiles:
                        pe.wait_ge(m_wc[u], 48)
                        pe.sem_inc(m_wc[u], -48)
                        pe.wait_ge(s["m_xsT"], 1)
                        pe.sem_inc(s["m_xsT"], -1)
                        pe.wait_ge(s["m_h_free"], 1)
                        pe.sem_inc(s["m_h_free"], -1)
                        for f in range(KD):
                            mm = pe.matmul(m_hp[u % 2], wc[u][:, f, :], xsT[u % 2][:, f, :],
                                           start=(f == 0), stop=(f == KD - 1))
                        mm.then_inc(s["m_h"], 1)
                    for u in tiles:
                        pe.wait_ge(s["m_hm"], 1)
                        pe.sem_inc(s["m_hm"], -1)
                        pe.wait_ge(s["m_y_free"], 1)
                        pe.sem_inc(s["m_y_free"], -1)
                        pe.matmul(m_yp[u % 2], hm[u % 2], pw[u], start=True, stop=True).then_inc(s["m_y"], 1)

        @block.scalar
        def _(act):
            link = Chain(act, act_step)

            def load_ln_exp():
                nc.scalar.preload_act_table_set("natural_log_exp_and_others")

            def norm_tokens(dst, src, ready):
                act.wait_ge(s["norm_ready"], 1)
                act.sem_inc(s["norm_ready"], -1)
                for tb in range(TB):
                    link(nc.scalar.activation(dst[:, tb, 0:D], src[:, tb, :], ACT.Identity,
                                              scale=rstd[:, tb:tb + 1], bias=nmr[:, tb:tb + 1]))
                    act.sem_inc(ready, 1)

            def copy_pairs(c, j):
                act.wait_ge(s["pairs_free"], 1)
                act.sem_inc(s["pairs_free"], -1)
                for i, pack in enumerate(PACKS):
                    n = G * sum(WID[t0] for t0 in pack)
                    act.wait_ge(s["pair_full"], 1)
                    act.sem_inc(s["pair_full"], -1)
                    link(nc.scalar.activation(pairs[j][:, OFF[pack[0]]:OFF[pack[0]] + n], bank("pair", c, j, i)[:, 0:n], ACT.Copy))
                    act.sem_inc(bank_free("pair", c, j, i), 1)
                act.sem_inc(s["pr_copied"], 1)

            def copy_outputs(c):
                act.wait_ge(s["o_full"], 1)
                act.sem_inc(s["o_full"], -1)
                link(nc.scalar.activation(oT[:, :, c * C:(c + 1) * C], uq[:], ACT.Copy))
                act.sem_inc(s["uq_free"], 1)

            def copy_turned(name, dst, ready, n):
                act.wait_ge(s[name + "_full"], 1)
                act.sem_inc(s[name + "_full"], -1)
                link(nc.scalar.activation(dst[:, 2 * n:2 * n + 2, :].rearrange("p k t -> p (k t)"), bank(name, n), ACT.Copy))
                act.sem_inc(bank_free(name, n), 1)
                act.sem_inc(ready, 1)

            def copy_and_square(n):
                act.wait_ge(s["qraw_free"], 1)
                act.sem_inc(s["qraw_free"], -1)
                act.wait_ge(s["qk_full"], 1)
                act.sem_inc(s["qk_full"], -1)
                link(nc.scalar.activation(qraw[n % 2][:], bank("qk", n), ACT.Copy))
                link(nc.scalar.activation(qsq[n % 2][:], bank("qk", n), ACT.Square))
                act.sem_inc(bank_free("qk", n), 1)
                act.sem_inc(s["q_sq_ready"], 1)

            def inverse_norm(n):
                r = qr[n % 2][:]
                act.wait_ge(s["ss_full"], 1)
                act.sem_inc(s["ss_full"], -1)
                link(nc.scalar.activation(r, bank("ss", n), ACT.Ln))
                act.sem_inc(bank_free("ss", n), 1)
                nc.scalar.activation(r, r, ACT.Exp, scale=-0.5, **({"bias": lnq[:]} if n < 2 else {}))\
                    .then_inc(s["q_r_ready"], 1)

            def copy_decays(hp, p_next):
                act.wait_ge(s["G_full"], 1)
                act.sem_inc(s["G_full"], -1)
                w = bank("G", hp)
                link(nc.scalar.activation(gsb[hp], w, ACT.Copy))
                act.sem_inc(s["g_copied"], 1)
                nc.scalar.activation(unit(eg_end[p_next], hp), per_chunk(w)[:, :, :, C - 1], ACT.Exp)
                link(nc.scalar.activation(flat(unit(eg, hp)), w, ACT.Exp))
                act.sem_inc(bank_free("G", hp), 1)
                act.sem_inc(s["eg_ready"], 1)

            def pair_decays(hp):
                act.wait_ge(s["diff_ready"], 1)
                act.sem_inc(s["diff_ready"], -1)
                link(nc.scalar.activation(flat(unit(dec, hp)), flat(unit(dec, hp)), ACT.Exp))
                act.sem_inc(s["dec_ready"], 1)

            def square_outputs(hp):
                nc.scalar.activation(qsq[hp][:], flat(unit(oT, hp)), ACT.Square).then_inc(s["o_sq_ready"], 1)

            def inverse_rms(hp):
                r = qr[hp][:]
                act.wait_ge(s["rms_full"], 1)
                act.sem_inc(s["rms_full"], -1)
                link(nc.scalar.activation(r, bank("rms", hp), ACT.Ln, scale=1.0 / DH, bias=eps6[:]))
                act.sem_inc(bank_free("rms", hp), 1)
                nc.scalar.activation(r, r, ACT.Exp, scale=-0.5).then_inc(s["o_r_ready"], 1)

            def sigmoid(name, hp, dst):
                act.wait_ge(s[name + "_full"], 1)
                act.sem_inc(s[name + "_full"], -1)
                return nc.scalar.activation(dst, bank(name, hp), ACT.Sigmoid)

            def copy_values(hp):
                act.wait_ge(s["v_full"], 1)
                act.sem_inc(s["v_full"], -1)
                link(nc.scalar.activation(flat(unit(vT, hp)), bank("v", hp), ACT.Copy))
                act.sem_inc(bank_free("v", hp), 1)

            def step(p, chain, after, ahead):
                if chain:
                    copy_pairs(0, 1)
                if ahead:
                    norm_tokens(xn, xt, s["xn_ready"])
                if after:
                    copy_outputs(NC - 1)
                    square_outputs(0)
                    square_outputs(1)
                if ahead:
                    copy_turned("xT", xT, s["xT_ready"], 0)
                    copy_turned("xT", xT, s["xT_ready"], 1)
                if after:
                    inverse_rms(0)
                    inverse_rms(1)
                if ahead:
                    copy_and_square(0)
                    copy_and_square(1)
                    act.wait_ge(s["la_e_ready"], 1)
                    act.sem_inc(s["la_e_ready"], -1)
                    link(nc.scalar.activation(alog[:, 2, :], alog[:, 1, :], ACT.Exp, scale=-1.0))
                    nc.scalar.activation(alog[:, 3, :], alog[:, 2, :], ACT.Ln, bias=1.0).then_inc(s["la_l_ready"], 1)
                if after:
                    act.wait_ge(s["ctx_raw"], 2)
                    act.sem_inc(s["ctx_raw"], -2)
                if ahead:
                    inverse_norm(0)
                if chain:
                    copy_pairs(1, 0)
                if ahead:
                    copy_and_square(2)
                    inverse_norm(1)
                if after:
                    norm_tokens(y, y, s["zn_ready"])
                if ahead:
                    copy_decays(0, 1 - p)
                    copy_decays(1, 1 - p)
                    act.sem_inc(s["xt_free"], 1)
                    pair_decays(0)
                    pair_decays(1)
                    copy_and_square(3)
                if chain:
                    copy_pairs(1, 1)
                    copy_outputs(0)
                if ahead:
                    inverse_norm(2)
                    inverse_norm(3)
                def next_gate(hp):
                    act.wait_ge(s["sg_free"], 1)
                    act.sem_inc(s["sg_free"], -1)
                    link(sigmoid("gate", hp, sg[:]))
                    act.sem_inc(s["gate_ready"], 1)

                if ahead:
                    next_gate(0)
                if after:
                    norm_tokens(xfw, x1, s["xf_ready"])
                    act.sem_inc(s["x1_free"], 1)
                    for tb in range(TB):
                        link(nc.scalar.activation(junk[:, tb, :], xfw[:, tb, 0:D], ACT.Square, accum_out=ssq[:, tb:tb + 1]))
                    act.sem_inc(s["ss_ready"], 1)
                if ahead:
                    next_gate(1)

                def next_beta(hp):
                    link(sigmoid("beta", hp, flat(unit(beta, hp))))
                    act.sem_inc(bank_free("beta", hp), 1)
                    act.sem_inc(s["beta_ready"], 1)

                if ahead:
                    if chain:
                        act.wait_ge(s["vb_free"], 1)
                        act.sem_inc(s["vb_free"], -1)
                    next_beta(0)
                if after:
                    copy_turned("xfT", xfT, s["xfT_ready"], 0)
                    copy_turned("xfT", xfT, s["xfT_ready"], 1)
                if ahead:
                    next_beta(1)
                if after:
                    act.wait_ge(s["hid_full"], 1)
                    act.sem_inc(s["hid_full"], -1)
                    for n in range(HID // P):
                        link(nc.scalar.activation(hT[:, n, :], bank("hid")[:, n * BT:(n + 1) * BT], ACT.Gelu, bias=gb1_sb[:, n:n + 1]))
                    act.sem_inc(bank_free("hid"), 1)
                    act.sem_inc(s["h_ready"], 1)
                if ahead:
                    copy_pairs(0, 0)
                    copy_values(0)
                if after:
                    act.wait_ge(s["lg_ready"], 1)
                    act.sem_inc(s["lg_ready"], -1)
                    nc.scalar.activation(lt[:, 1], lt[:, 1], ACT.Tanh, scale=0.5).then_inc(s["sig_ready"], 1)
                load_ln_exp()
                if ahead:
                    copy_values(1)
                    act.sem_inc(s["vb_ready"], 1)
                if after:
                    act.wait_ge(s["d_ready"], 1)
                    act.sem_inc(s["d_ready"], -1)
                    nc.scalar.activation(lt[:, 3], lt[:, 2], ACT.Exp).then_inc(s["e_ready"], 1)
                link.restart()

            act.wait_ge(loaded, ALL)
            load_ln_exp()
            act.wait_ge(s["setup_v"], 1)
            act.sem_inc(s["setup_v"], -1)
            link(nc.scalar.activation(neg_a[:], neg_a[:], ACT.Exp))
            act.sem_inc(s["setup_a"], 1)
            link(nc.scalar.activation(junk[0:E, 0, :], ce, ACT.Square, accum_out=ce_s[:, 0:1]))
            act.sem_inc(s["ce_sq"], 1)
            link.restart()
            step(1, False, False, True)
            step(0, True, False, True)
            with act.Fori(0, NT // 2 - 1):
                step(1, True, True, True)
                step(0, True, True, True)
            step(1, True, True, False)
            step(0, False, True, False)
            with act.Fori(0, NM // MQ):
                for pair in range(MQ // 2):
                    tiles = (2 * pair, 2 * pair + 1)
                    for u in tiles:
                        act.wait_ge(s["m_t"], 1)
                        act.sem_inc(s["m_t"], -1)
                        link(nc.scalar.activation(xsT[u % 2].rearrange("p k t -> p (k t)"), m_tp[u % 2], ACT.Copy))
                        act.sem_inc(s["m_t_free"], 1)
                        act.sem_inc(s["m_xsT"], 1)
                    for u in tiles:
                        act.wait_ge(s["m_h"], 1)
                        act.sem_inc(s["m_h"], -1)
                        link(nc.scalar.activation(hm[u % 2], m_hp[u % 2], ACT.Gelu, bias=bc[:, u:u + 1]))
                        act.sem_inc(s["m_h_free"], 1)
                        act.sem_inc(s["m_hm"], 1)
                link.restart()

        @block.gpsimd
        def _(pool):
            link = Chain(pool, pool_step)

            def decay_state(p, c):
                pool.wait_ge(s["S_ready_p"], 1)
                pool.sem_inc(s["S_ready_p"], -1)
                nc.gpsimd.tensor_tensor(Sd[:], S[:], eg_end[p][:, :, c:c + 1].to_broadcast([P, G, DH]), ALU.mult)\
                    .then_inc(s["Sd_ready"], 1)

            def decay_k_and_q(c):
                link(nc.gpsimd.tensor_tensor(kqd[c][:], kq[:, :, c], eg[:, :, c * C:(c + 1) * C].unsqueeze(2).to_broadcast([P, G, 2, C]),
                                             ALU.mult))
                pool.sem_inc(s["kqd_ready"], 1)

            def pairs_times_beta(c, j):
                pool.wait_ge(s["pr_copied"], 1)
                pool.sem_inc(s["pr_copied"], -1)
                for t0 in range(CS - 1):
                    a = pairs[j][:, OFF[t0]:OFF[t0] + G * WID[t0]].rearrange("p (g t) -> p g t", g=G)
                    t = c * C + j * CS + t0 + 1
                    ins = nc.gpsimd.tensor_tensor(a, a, beta[:, :, t:t + WID[t0]], ALU.mult)
                ins.then_inc(s["pr_ready"], 1)

            def step(p, chain, after, ahead, added):
                if chain:
                    decay_state(p, 0)
                    decay_k_and_q(1)
                    pool.sem_inc(s["kq_free"], 1)
                    pairs_times_beta(0, 1)
                    pool.wait_ge(s["kt_ready"], 1)
                    pool.sem_inc(s["kt_ready"], -1)
                    for c in range(NC):
                        link(nc.gpsimd.tensor_tensor(kd[c][:], kd[c][:], dec[:, :, c * C + C - 1:c * C + C].to_broadcast([P, G, C]),
                                                     ALU.mult))
                        pool.sem_inc(s["kd_ready"], 1)
                if ahead:
                    pool.wait_ge(s["la_ready"], 1)
                    pool.sem_inc(s["la_ready"], -1)
                    nc.gpsimd.tensor_copy(lax, la[:].unsqueeze(3).to_broadcast([P, TB, H, DH])).then_inc(s["lax_ready"], 1)
                if after:
                    for hp in range(2):
                        pool.wait_ge(s["o_copied"], 1)
                        pool.sem_inc(s["o_copied"], -1)
                        nc.gpsimd.tensor_tensor(unit(ctxT, hp), unit(ctxT, hp), unit(silu[1 - p], hp), ALU.mult)\
                            .then_inc(s["ctx_ready"], 1)
                if chain:
                    pairs_times_beta(1, 0)
                if after:
                    pool.wait_ge(s["xres_loaded"], 16 * BL)
                    pool.sem_inc(s["xres_loaded"], -(16 * BL))
                    for tb in range(TB):
                        pool.wait_ge(s["zn_ready"], 1)
                        pool.sem_inc(s["zn_ready"], -1)
                        link(nc.gpsimd.tensor_tensor(x1[:, tb, :], x1[:, tb, :], y[:, tb, :], ALU.add))
                    pool.sem_inc(s["y_ready"], 1)
                    pool.sem_inc(s["x1_ready"], 1)
                if ahead:
                    for hp in range(2):
                        pool.wait_ge(s["gT_ready"], 1)
                        pool.sem_inc(s["gT_ready"], -1)
                        d = flat(unit(dec, hp))
                        link(nc.gpsimd.tensor_tensor(d, gsb[hp], gT[hp], ALU.subtract))
                        dt = d.rearrange("p (n t) -> p n t", t=C)
                        link(nc.gpsimd.tensor_tensor(dt, dt, mask[:].unsqueeze(1).to_broadcast([P, GU * NC, C]), ALU.add))
                        pool.sem_inc(s["diff_ready"], 1)
                if chain:
                    decay_state(p, 1)
                    pairs_times_beta(1, 1)
                if ahead:
                    pool.wait_ge(s["eg_ready"], 2)
                    pool.sem_inc(s["eg_ready"], -2)
                    pool.wait_ge(s["kq_ready_p"], 4)
                    pool.sem_inc(s["kq_ready_p"], -4)
                    decay_k_and_q(0)
                    pool.wait_ge(s["beta_ready"], 2)
                    pool.sem_inc(s["beta_ready"], -2)
                    pairs_times_beta(0, 0)
                if after:
                    pool.wait_ge(s["slot_ready"], 1)
                    pool.sem_inc(s["slot_ready"], -1)
                    for tb in range(TB):
                        nc.gpsimd.indirect_dma_start(
                            xs_dram, bass.IndirectOffsetOnAxis(ap=slot[:, tb:tb + 1].bitcast(U32), axis=0),
                            xfw[:, tb, :], None).then_inc(s["scat_done"], 16)
                    pool.wait_ge(s["scat_done"], added)
                link.restart()

            pool.wait_ge(loaded, ALL)
            link(nc.gpsimd.memset(S[:], 0.0))
            pool.sem_inc(s["S_ready"], 1)
            link(nc.gpsimd.memset(base[:], 0.0))
            pool.sem_inc(s["base_ready"], 1)
            for n in ("xt_free", "x1_free", "kkq_free", "uq_free", "sg_free", "S_ready_p"):
                pool.sem_inc(s[n], 1)
            for f in work_free:
                pool.sem_inc(f, 1)
            for n in ("pairs_free", "qraw_free"):
                pool.sem_inc(s[n], 2)
            link.restart()
            ROW = 16 * TB
            step(1, False, False, True, None)
            step(0, True, False, True, None)
            with pool.Fori(0, NT // 2 - 1) as i:
                step(1, True, True, True, i * (2 * ROW) + ROW)
                step(0, True, True, True, i * (2 * ROW) + 2 * ROW)
            step(1, True, True, False, (NT - 1) * ROW)
            step(0, False, True, False, NT * ROW)
            def add_bias(u):
                pool.wait_ge(s["m_xs_p"], 1)
                pool.sem_inc(s["m_xs_p"], -1)
                nc.gpsimd.tensor_tensor(xsb[u], xs[u][:, 0:D], pb_sb, ALU.add).then_inc(s["m_xsb"], 1)

            def four_tiles(q, last):
                for pair in range(MQ // 2):
                    tiles = (2 * pair, 2 * pair + 1)
                    if pair:
                        pool.wait_ge(s["m_add"], q * (16 * MQ) + 32)
                    if not (last and pair):
                        for u in tiles:
                            add_bias((u + 2) % MQ)
                    for u in tiles:
                        pool.wait_ge(s["m_n"], 1)
                        pool.sem_inc(s["m_n"], -1)
                        link(nc.gpsimd.tensor_scalar(z[u], ya[u], ms[:, 0, u, 0:1], ms[:, 1, u, 0:1], ALU.mult, ALU.add))
                        link(nc.gpsimd.tensor_copy(toki[:, u:u + 1], xs[u][:, D + 1:D + 2]))
                        pool.sem_inc(s["m_free"], 1)
                        nc.gpsimd.indirect_dma_start(
                            out_rows, bass.IndirectOffsetOnAxis(ap=toki[:, u:u + 1].bitcast(U32), axis=0), z[u], None,
                            bounds_check=ROWS - 1, oob_is_err=False, compute_op=ALU.add).then_inc(s["m_add"], 16)
                link.restart()

            for u in range(2):
                add_bias(u)
            with pool.Fori(0, NM // MQ - 1) as q:
                four_tiles(q, False)
            four_tiles(NM // MQ - 1, True)
            pool.wait_ge(s["m_add"], 16 * NM)

        @block.vector
        def _(dve):
            link = Chain(dve, dve_step)
            v = nc.vector
            turns = (slice(0, G // 2), slice(G // 2, G))

            def rsqrt(r, var, t):
                link(v.tensor_scalar(r.bitcast(I32), var.bitcast(I32), -0.5, RSQRT_GUESS, ALU.mult, ALU.add))
                for _ in range(3):
                    link(v.tensor_tensor(t, r, r, ALU.mult))
                    link(v.scalar_tensor_tensor(t, t, -0.5, var, ALU.mult, ALU.mult))
                    link(v.scalar_tensor_tensor(r, t, 1.5, r, ALU.add, ALU.mult))

            def token_stats(src, tb):
                link(v.bn_stats(stats[:, tb, :], src[:, tb, :]))
                link(v.bn_aggr(mv[:, tb, :], stats[:, tb, :]))

            def token_norm():
                link(v.tensor_scalar(ve[:], mv[:, :, 1], 1e-5, None, ALU.add))
                rsqrt(rstd[:], ve[:], nt1[:])
                link(v.scalar_tensor_tensor(nmr[:], mv[:, :, 0], -1.0, rstd[:], ALU.mult, ALU.mult))
                dve.sem_inc(s["norm_ready"], 1)

            def decay_products(c):
                dve.wait_ge(s["kkq_full"], 1)
                dve.sem_inc(s["kkq_full"], -1)
                link(v.tensor_tensor(A[c][:], kkq[:], dec[:, :, c * C:(c + 1) * C].unsqueeze(2).to_broadcast([P, G, 2, C]), ALU.mult))
                dve.sem_inc(s["kkq_free"], 1)
                dve.sem_inc(s["A_ready"], 1)

            def solve_half(c, j):
                h = slice(j * CS, (j + 1) * CS)
                th = slice(c * C + j * CS, c * C + (j + 1) * CS)
                for g in turns:
                    link(v.tensor_tensor(Ut[:, g], vT[:, g, th], uk[:, g, h], ALU.subtract), behind=1)
                for g in turns:
                    link(v.tensor_tensor(U[:, g, h], Ut[:, g], beta[:, g, th], ALU.mult), behind=1)
                dve.wait_ge(s["pr_ready"], 1)
                dve.sem_inc(s["pr_ready"], -1)
                if (c, j) == (NC - 1, 1):
                    dve.wait_ge(dve_step, link.n)
                    dve.sem_inc(s["vb_free"], 1)
                for t0 in range(CS - 1):
                    n, at = WID[t0], j * CS + t0
                    pr = pairs[j][:, OFF[t0]:OFF[t0] + G * n].rearrange("p (g t) -> p g t", g=G)
                    for g in turns:
                        link(v.tensor_tensor(Ut[:, g, 0:n], pr[:, g], U[:, g, at:at + 1].to_broadcast([P, G // 2, n]),
                                             ALU.mult), behind=1)
                    for g in turns:
                        link(v.tensor_tensor(U[:, g, at + 1:at + 1 + n], U[:, g, at + 1:at + 1 + n], Ut[:, g, 0:n],
                                             ALU.subtract), behind=1)
                dve.wait_ge(dve_step, link.n)
                dve.sem_inc(s["pairs_free"], 1)
                link(v.transpose(delT[c][:], U[:]))
                dve.sem_inc(s["delT_ready"], 1)

            def add_to_state():
                dve.wait_ge(s["su_full"], 1)
                dve.sem_inc(s["su_full"], -1)
                dve.wait_ge(s["Sd_ready"], 1)
                dve.sem_inc(s["Sd_ready"], -1)
                link(v.tensor_tensor(S[:], Sd[:], su[:], ALU.add))
                dve.sem_inc(s["S_ready"], 1)
                dve.sem_inc(s["S_ready_p"], 1)

            def scale(n):
                j, hp = divmod(n, 2)
                dve.wait_ge(s["q_r_ready"], 1)
                dve.sem_inc(s["q_r_ready"], -1)
                link(v.tensor_tensor(unit(kq, hp)[:, :, :, 1 - j, :], per_chunk(qraw[n % 2][:]), per_chunk(qr[n % 2][:]), ALU.mult))
                dve.sem_inc(s["qraw_free"], 1)
                dve.sem_inc(s["kq_ready_pe"], 1)
                dve.sem_inc(s["kq_ready_p"], 1)

            def alpha_argument():
                dve.wait_ge(s["alpha_full"], 1)
                dve.sem_inc(s["alpha_full"], -1)
                link(v.tensor_tensor(alog[:, 0, :].rearrange("p (b h) -> p b h", b=TB),
                                     bank("alpha")[:, 0:TB * H].rearrange("p (b h) -> p b h", b=TB),
                                     dtb[:].unsqueeze(1).to_broadcast([P, TB, H]), ALU.add))
                dve.sem_inc(bank_free("alpha"), 1)
                link(v.scalar_tensor_tensor(alog[:, 1, :], alog[:, 0, :], -1.0, alog[:, 0, :], ALU.mult, ALU.max))
                dve.sem_inc(s["la_e_ready"], 1)

            def log_alpha():
                dve.wait_ge(s["la_l_ready"], 1)
                dve.sem_inc(s["la_l_ready"], -1)
                link(v.scalar_tensor_tensor(alog[:, 1, :], alog[:, 0, :], 0.0, alog[:, 3, :], ALU.max, ALU.add))
                link(v.tensor_tensor(la[:], alog[:, 1, :].rearrange("p (b h) -> p b h", b=TB),
                                     neg_a[:].unsqueeze(1).to_broadcast([P, TB, H]), ALU.mult))
                dve.sem_inc(s["la_ready"], 1)

            def normed_outputs(hp):
                dve.wait_ge(s["o_r_ready"], 1)
                dve.sem_inc(s["o_r_ready"], -1)
                link(v.scalar_tensor_tensor(flat(unit(ctxT, hp)), flat(unit(oT, hp)), nw[:], qr[hp][:], ALU.mult, ALU.mult))
                dve.sem_inc(s["ctx_raw"], 1)
                dve.sem_inc(s["o_copied"], 1)

            def choose_columns():
                dve.wait_ge(s["logits_full"], 1)
                dve.sem_inc(s["logits_full"], -1)
                lw = bank("logits")[:, 0:2 * TB * E].rearrange("p (b a e) -> p b a e", b=TB, a=2)
                link(v.tensor_tensor(lt[:, 1], lw[:, :, 1, :], gb2_sb[:].unsqueeze(1).to_broadcast([P, TB, E]), ALU.add))
                dve.sem_inc(s["lg_ready"], 1)
                link(v.tensor_tensor(lt[:, 0], lw[:, :, 0, :], rstd[:].unsqueeze(2).to_broadcast([P, TB, E]), ALU.mult))
                dve.sem_inc(bank_free("logits"), 1)
                dve.wait_ge(s["sig_ready"], 1)
                dve.sem_inc(s["sig_ready"], -1)
                link(v.tensor_scalar(lt[:, 1], lt[:, 1], 0.5, 0.5, ALU.mult, ALU.add))
                link(v.tensor_tensor(lt[:, 0], lt[:, 0], lt[:, 1], ALU.add))
                link(v.tensor_reduce(l1[:, 0, :], lt[:, 0], AX.X, ALU.max))
                link(v.tensor_tensor(lt[:, 2], lt[:, 0], l1[:, 0, :].unsqueeze(2).to_broadcast([P, TB, E]), ALU.subtract))
                dve.sem_inc(s["d_ready"], 1)
                link(v.tensor_scalar(lt[:, 4], lt[:, 2], 0.0, -float(E), ALU.is_ge, ALU.mult))
                link(v.tensor_tensor(lt[:, 4], lt[:, 4], iota[:].unsqueeze(1).to_broadcast([P, TB, E]), ALU.add))
                link(v.tensor_reduce(l1[:, 1, :], lt[:, 4], AX.X, ALU.min))
                link(v.tensor_tensor(oh[:], lt[:, 4], l1[:, 1, :].unsqueeze(2).to_broadcast([P, TB, E]), ALU.is_equal))
                dve.sem_inc(s["oh_ready"], 1)
                dve.wait_ge(s["e_ready"], 1)
                dve.sem_inc(s["e_ready"], -1)
                link(v.tensor_reduce(l1[:, 2, :], lt[:, 3], AX.X, ALU.add))
                link(v.reciprocal(xfw[:, :, D], l1[:, 2, :]))
                link(v.tensor_copy(xfw[:, :, D + 1], tokf[:]))
                link(v.tensor_scalar(tokf[:], tokf[:], float(T), None, ALU.add))
                link(v.memset(xfw[:, :, D + 2:XSW], 0.0))

            def rows_of_tokens():
                dve.wait_ge(s["rank_full"], 1)
                dve.sem_inc(s["rank_full"], -1)
                w = bank("rank")
                link(v.tensor_tensor(lt[:, 5], w[:, 0:TB * E].rearrange("p (b e) -> p b e", b=TB),
                                     base[:].unsqueeze(1).to_broadcast([P, TB, E]), ALU.add))
                link(v.tensor_tensor(base[:], base[:], w[:, TB * E:(TB + 1) * E], ALU.add))
                dve.sem_inc(bank_free("rank"), 1)
                link(v.tensor_tensor(lt[:, 5], lt[:, 5], col[:, 1, :].unsqueeze(1).to_broadcast([P, TB, E]), ALU.mult))
                link(v.tensor_tensor(lt[:, 5], lt[:, 5], col[:, 0, :].unsqueeze(1).to_broadcast([P, TB, E]), ALU.add))
                link(v.tensor_tensor(lt[:, 5], lt[:, 5], oh[:], ALU.mult))
                link(v.tensor_reduce(slotf[:], lt[:, 5], AX.X, ALU.add))
                link(v.tensor_copy(slot[:], slotf[:]))
                dve.sem_inc(s["slot_ready"], 1)

            def step(p, chain, after, ahead):
                if ahead:
                    dve.wait_ge(s["x_loaded"], 16 * BL)
                    dve.sem_inc(s["x_loaded"], -(16 * BL))
                    for tb in range(TB):
                        token_stats(xt, tb)
                    token_norm()
                if chain:
                    dve.wait_ge(s["vb_ready"], 1)
                    dve.sem_inc(s["vb_ready"], -1)
                    dve.wait_ge(s["uk_full"], 1)
                    dve.sem_inc(s["uk_full"], -1)
                    solve_half(0, 0)
                    for c in range(NC):
                        link(v.transpose(kd[c][:], kq[:, :, c, 0, :]))
                    dve.sem_inc(s["kt_ready"], 1)
                    decay_products(1)
                if ahead:
                    alpha_argument()
                if after:
                    for hp in range(2):
                        normed_outputs(hp)
                if ahead:
                    log_alpha()
                if chain:
                    dve.wait_ge(s["corr_full"], 1)
                    dve.sem_inc(s["corr_full"], -1)
                    solve_half(0, 1)
                if ahead:
                    if chain:
                        dve.wait_ge(s["kq_free"], 1)
                        dve.sem_inc(s["kq_free"], -1)
                    scale(0)
                if after:
                    for tb in range(TB):
                        dve.wait_ge(s["wo_full"], 1)
                        dve.sem_inc(s["wo_full"], -1)
                        link(v.tensor_tensor(y[:, tb, :], bank("wo", tb), bo_sb[:], ALU.add))
                        dve.sem_inc(bank_free("wo", tb), 1)
                        token_stats(y, tb)
                    token_norm()
                if ahead:
                    scale(1)
                    for hp in range(2):
                        dve.wait_ge(s["g_copied"], 1)
                        dve.sem_inc(s["g_copied"], -1)
                        link(v.transpose(gT[hp], gsb[hp]))
                        dve.sem_inc(s["gT_ready"], 1)
                if chain:
                    add_to_state()
                    dve.wait_ge(s["uk_full"], 1)
                    dve.sem_inc(s["uk_full"], -1)
                    solve_half(1, 0)
                if after:
                    dve.wait_ge(s["y_ready"], 1)
                    dve.sem_inc(s["y_ready"], -1)
                    for tb in range(TB):
                        token_stats(x1, tb)
                    token_norm()
                if ahead:
                    scale(2)
                    scale(3)
                    for hp in range(2):
                        dve.wait_ge(s["gate_ready"], 1)
                        dve.sem_inc(s["gate_ready"], -1)
                        link(v.tensor_tensor(flat(unit(silu[1 - p], hp)), bank("gate", hp), sg[:], ALU.mult))
                        dve.sem_inc(bank_free("gate", hp), 1)
                        dve.sem_inc(s["sg_free"], 1)
                if chain:
                    dve.wait_ge(s["corr_full"], 1)
                    dve.sem_inc(s["corr_full"], -1)
                    solve_half(1, 1)
                if ahead:
                    dve.wait_ge(s["dec_ready"], 2)
                    dve.sem_inc(s["dec_ready"], -2)
                    decay_products(0)
                if after:
                    dve.wait_ge(s["ss_ready"], 1)
                    dve.sem_inc(s["ss_ready"], -1)
                    link(v.tensor_scalar(ve[:], ssq[:], 1e-24, None, ALU.max))
                    rsqrt(rstd[:], ve[:], nt1[:])
                    choose_columns()
                    rows_of_tokens()
                if chain:
                    add_to_state()
                link.restart()

            dve.wait_ge(loaded, ALL)
            link(v.memset(U[:], 0.0))
            link(v.memset(eps6[:], 1e-6))
            link(v.memset(lnq[:], -0.5 * math.log(DH)))
            dve.sem_inc(s["setup_v"], 1)
            dve.wait_ge(s["setup_a"], 1)
            dve.sem_inc(s["setup_a"], -1)
            link(v.tensor_scalar(neg_a[:], neg_a[:], -1.0, None, ALU.mult))
            dve.wait_ge(s["ce_sq"], 1)
            dve.sem_inc(s["ce_sq"], -1)
            link(v.tensor_scalar(ce_s[:, 1:2], ce_s[:, 0:1], 1e-24, None, ALU.max))
            rsqrt(ce_s[:, 2:3], ce_s[:, 1:2], ce_s[:, 3:4])
            link(v.tensor_scalar(ce, ce, ce_s[:, 2:3], None, ALU.mult))
            dve.sem_inc(s["ce_n"], 1)
            dve.wait_ge(s["ce_T"], 1)
            dve.sem_inc(s["ce_T"], -1)
            link(v.tensor_copy(ceT[:].rearrange("p k e -> p (k e)"), work[0][:, 0:KD * E]))
            dve.wait_ge(s["base_ready"], 1)
            dve.sem_inc(s["base_ready"], -1)
            link(v.tensor_copy(tokf[:], tok0[:]))
            link.restart()
            step(1, False, False, True)
            step(0, True, False, True)
            with dve.Fori(0, NT // 2 - 1):
                step(1, True, True, True)
                step(0, True, True, True)
            step(1, True, True, False)
            step(0, False, True, False)
            link(v.tensor_tensor(tb[:, 2, :], base[:], col[:, 1, :], ALU.mult))
            link(v.tensor_tensor(cnt[:], tb[:, 2, :], col[:, 2, :], ALU.add))
            link(v.tensor_scalar(tabf[:, 0, :], krow[:], float(P), None, ALU.mult))
            link(v.tensor_tensor(tb2[:], base[:].unsqueeze(2).to_broadcast([P, E, P]),
                                 tabf[:, 0, :].unsqueeze(1).to_broadcast([P, E, P]), ALU.is_gt))
            link(v.tensor_reduce(tb[:, 0, :], tb2[:], AX.X, ALU.add))
            link(v.tensor_copy(tb[:, 1, :], tb[:, 0, :]))
            for e in range(1, E):
                link(v.tensor_tensor(tb[:, 1, e:e + 1], tb[:, 1, e:e + 1], tb[:, 1, e - 1:e], ALU.add))
            link(v.tensor_tensor(tb2[:], tb[:, 1, :].unsqueeze(2).to_broadcast([P, E, P]),
                                 krow[:].unsqueeze(1).to_broadcast([P, E, P]), ALU.is_le))
            link(v.tensor_reduce(tabf[:, 1, :], tb2[:].rearrange("p e m -> p m e"), AX.X, ALU.add))
            for n, step in ((2, tb[:, 0, :]), (3, col[:, 3, :]), (4, col[:, 4, :])):
                link(v.tensor_tensor(tb3[:], tb2[:], step.unsqueeze(2).to_broadcast([P, E, P]), ALU.mult))
                link(v.tensor_reduce(tabf[:, n, :], tb3[:].rearrange("p e m -> p m e"), AX.X, ALU.add))
            link(v.tensor_tensor(tabf[:, 2, :], krow[:], tabf[:, 2, :], ALU.subtract))
            link(v.tensor_scalar(tabf[:, 4, :], tabf[:, 4, :], 1.0, float(P), ALU.add, ALU.mult))
            link(v.tensor_tensor(tabf[:, 4, :], tabf[:, 4, :], tabf[:, 2, :], ALU.mult))
            link(v.tensor_tensor(tab[:, 1, :], tabf[:, 3, :], tabf[:, 4, :], ALU.add))
            link(v.tensor_scalar(tab[:, 0, :], tabf[:, 1, :], float(E - 1), None, ALU.min))
            dve.sem_inc(s["table_ready"], 1)
            for n, free in (("m_free", MQ), ("m_wfree", MQ), ("m_t_free", 2), ("m_h_free", 2), ("m_y_free", 2)):
                dve.sem_inc(s[n], free)
            link.restart()
            with dve.Fori(0, NM // MQ):
                def row_stats(u):
                    link(v.bn_stats(mst[:, u % 2], ya[u]))
                    link(v.bn_aggr(mmv[:, u % 2], mst[:, u % 2]))

                def row_rsqrt(r):
                    link(v.tensor_scalar(mt[:, 0], mmv[:, :, 1], 1e-5, None, ALU.add))
                    rsqrt(r, mt[:, 0], mt[:, 1])

                for pair in range(MQ // 2):
                    tiles = (2 * pair, 2 * pair + 1)
                    for u in tiles:
                        dve.wait_ge(s["m_xsb"], 1)
                        dve.sem_inc(s["m_xsb"], -1)
                        dve.wait_ge(s["m_y"], 1)
                        dve.sem_inc(s["m_y"], -1)
                        dve.sem_inc(s["m_wfree"], 1)
                        link(v.scalar_tensor_tensor(ya[u], m_yp[u % 2], xs[u][:, D:D + 1], xsb[u], ALU.mult, ALU.add))
                        dve.sem_inc(s["m_y_free"], 1)
                        row_stats(u)
                    row_rsqrt(mt[:, 2])
                    for u in tiles:
                        link(v.scalar_tensor_tensor(ya[u], ya[u], mmv[:, u % 2, 0:1], lg_sb, ALU.subtract, ALU.mult))
                        link(v.scalar_tensor_tensor(ya[u], ya[u], mt[:, 2, u % 2:u % 2 + 1], lb_sb, ALU.mult, ALU.add))
                        row_stats(u)
                    r = ms[:, 0, 2 * pair:2 * pair + 2, 0]
                    row_rsqrt(r)
                    link(v.scalar_tensor_tensor(ms[:, 1, 2 * pair:2 * pair + 2, 0], mmv[:, :, 0], -1.0, r, ALU.mult, ALU.mult))
                    dve.sem_inc(s["m_n"], 2)
                link.restart()


def column_rows():
    import numpy as np
    e = np.arange(E)
    front, sign = e // 2 * SHARE, 1 - 2 * (e % 2)
    first = np.where(e % 2, front + SHARE - 1, front)
    behind = np.where(e % 2, first + 1 - P, first)
    return np.stack([first, sign, behind, np.diff(behind, append=PADROW), np.diff(sign, append=0)])


def constants():
    import numpy as np
    p = np.arange(P)
    same = (p[:, None] // DH) == (p[None, :] // DH)
    squares = np.stack([np.eye(P), same, same & (p[:, None] <= p[None, :]), p[:, None] < p[None, :],
                        np.ones((P, P))], axis=1)
    sel = same[:, None, :] & ((p % DH)[:, None] == np.arange(C)[None, :])[:, :, None]
    mask = np.where(np.arange(C)[None, :] >= (p % DH)[:, None], 0.0, NEG)
    iota = np.broadcast_to(np.arange(E), (P, E))
    pad = np.zeros((P, XSW))
    pad[:, D + 1] = 2 * ROWS
    tok = (np.arange(TB)[None, :] * BL + p[:, None] // T) * L + p[:, None] % T
    row = np.broadcast_to(p, (P, P))
    col = np.broadcast_to(column_rows(), (P, 5, E))
    return {n: np.ascontiguousarray(a, dtype=np.float32) for n, a in
            dict(c_sq=squares, c_sel=sel, c_mask=mask, c_iota=iota, c_pad=pad, c_tok=tok, c_row=row, c_col=col).items()}


def kernel(**inputs):
    import numpy as np
    import concourse.bacc as bacc
    from concourse.bass_utils import run_bass_kernel_spmd as run

    a = {n[3:]: np.asarray(v) for n, v in inputs.items()}
    laid = {
        "x": a["attn_x"],
        "w_in": np.concatenate([a[f"attn_W{n}"].T for n in "qkvbg"], axis=1),
        "wa": a["attn_Wa"].T, "dt_bias": a["attn_dt_bias"], "a_log": a["attn_A_log"], "norm_w": a["attn_norm_w"],
        "wo": a["attn_Wo"].T, "bo": a["attn_bo"], "col_emb": a["ffn_col_emb"],
        "gw1": a["ffn_gate_w1"], "gb1": a["ffn_gate_b1"].reshape(HID // P, P).T, "gw2": a["ffn_gate_w2"], "gb2": a["ffn_gate_b2"],
        "w_cols": a["ffn_W_cols"], "b_cols": a["ffn_b_cols"][:, :, None], "proj_w": a["ffn_proj_w"].reshape(E, N, D),
        "proj_b": a["ffn_proj_b"], "ln_g": a["ffn_ln_g"], "ln_b": a["ffn_ln_b"], **constants(),
    }
    nc = bacc.Bacc("TRN2", target_bir_lowering=False, num_devices=1)
    arrays, args = {}, {}
    for name, v in laid.items():
        arrays[f"in_{name}"] = v = np.ascontiguousarray(v)
        args[name] = nc.dram_tensor(f"in_{name}", v.shape, mybir.dt.from_np(v.dtype), kind="ExternalInput").ap()
    out = nc.dram_tensor("out", (B, L, D), F32, kind="ExternalOutput").ap()
    xs_dram = nc.dram_tensor("xs_rows", (PADROW + P, XSW), F32, kind="Internal").ap()
    sandwich_kernel(nc, out=out, xs_dram=xs_dram, **args)
    return run(nc, [arrays], core_ids=[0]).results[0]["out"]
```

```python
import math
from contextlib import ExitStack

import concourse.bass as bass
from concourse import mybir

F32 = mybir.dt.float32
I32 = mybir.dt.int32
U32 = mybir.dt.uint32
ALU = mybir.AluOpType
ACT = mybir.ActivationFunctionType
AX = mybir.AxisListType

B, L, D = 4, 2048, 512
H, DH = 16, 32
P = 128
KD = D // P
HP = P // DH
T = 64
NT = L // T
BL = P // T
TB = B // BL
BT = B * T
C = DH
NC = T // C
CS = C // 2
G = KD * B
NP = 5
E, N = 16, 128
HID = 256
ROWS = B * L
XSW = D + 4
SHARE = ROWS + 2 * P
PADROW = E // 2 * SHARE
MQ = 4
NM = -(-(ROWS // P + E - 1) // MQ) * MQ
RSQRT_GUESS = float(0x5f3759df)
NEG = -1.0e30

WID = [CS - 1 - s for s in range(CS - 1)]
PACKS = [(0, 1, 14), (2, 3, 10), (4, 5, 6), (7, 8, 9, 11, 12, 13)]
ORDER = [s for pack in PACKS for s in pack]
OFF = [G * sum(WID[s] for s in ORDER[:ORDER.index(t)]) for t in range(CS - 1)]
NPAIR = G * sum(WID)
GU = G // 2
NW = 3

TURNS = [("pair", 0, 1, i) for i in range(len(PACKS))] + [
    ("xT", 0), ("xT", 1), ("qk", 0), ("rms", 0), ("alpha",), ("qk", 1), ("rms", 1), ("ss", 0)] + [
    ("pair", 1, 0, i) for i in range(len(PACKS))] + [
    ("wo", 0), ("wo", 1), ("qk", 2), ("ss", 1), ("G", 0), ("G", 1), ("qk", 3)] + [
    ("pair", 1, 1, i) for i in range(len(PACKS))] + [
    ("ss", 2), ("gate", 0), ("ss", 3), ("gate", 1), ("beta", 0), ("xfT", 0), ("xfT", 1), ("beta", 1), ("hid",)] + [
    ("pair", 0, 0, i) for i in range(len(PACKS))] + [
    ("v", 0), ("logits",), ("v", 1), ("rank",)]
BANK = {use: n % NW for n, use in enumerate(TURNS)}


class Chain:

    def __init__(self, eng, sem):
        self.eng, self.sem, self.n = eng, sem, 0

    def __call__(self, ins, behind=0):
        self.n += 1
        ins.then_inc(self.sem, 1)
        self.eng.wait_ge(self.sem, self.n - behind)

    def restart(self):
        self.eng.sem_inc(self.sem, -self.n)
        self.n = 0


def sandwich_kernel(nc, x, w_in, wa, dt_bias, a_log, norm_w, wo, bo, col_emb, gw1, gb1, gw2, gb2,
                    w_cols, b_cols, proj_w, proj_b, ln_g, ln_b,
                    c_sq, c_sel, c_mask, c_iota, c_pad, c_tok, c_row, c_col, out, xs_dram):
    with ExitStack() as ctx:
        def sb(name, shape, dt=F32):
            return ctx.enter_context(nc.sbuf_tensor(name, shape, dt))

        def ps(name, shape):
            return ctx.enter_context(nc.psum_tensor(name, shape, F32))

        def sem(name):
            return ctx.enter_context(nc.semaphore(name))

        squares = sb("squares", [P, 5, P])
        ident, blk1, ucum, ustrict, ones = (squares[:, i, :] for i in range(5))
        sel = sb("sel", [P, C, P])
        mask = sb("mask", [P, C])
        iota = sb("iota", [P, E])
        w_sb = sb("w_sb", [P, KD, NP * D])
        wa_sb = sb("wa_sb", [P, KD, H])
        dtb = sb("dtb", [P, H])
        neg_a = sb("neg_a", [P, H])
        nw = sb("nw", [P, 1])
        wo_sb = sb("wo_sb", [P, KD, D])
        bo_sb = sb("bo_sb", [P, D])
        gw1_sb = sb("gw1_sb", [P, KD, HID])
        gb1_sb = sb("gb1_sb", [P, HID // P])
        gw2_sb = sb("gw2_sb", [P, HID // P, E])
        gb2_sb = sb("gb2_sb", [P, E])
        ceT = sb("ceT", [P, KD, E])
        ce_s = sb("ce_s", [E, 4])
        eps6 = sb("eps6", [P, 1])
        lnq = sb("lnq", [P, 1])
        minus_half = sb("minus_half", [P, 1])

        xt = sb("xt", [P, TB, D])
        xn = sb("xn", [P, TB, D])
        xT = sb("xT", [P, KD, BT])
        stats = sb("stats", [P, TB, 6])
        mv = sb("mv", [P, TB, 2])
        ve = sb("ve", [P, TB])
        rstd = sb("rstd", [P, TB])
        nt1 = sb("nt1", [P, TB])
        nmr = sb("nmr", [P, TB])
        x_rstd = sb("x_rstd", [P, TB])
        x_nmr = sb("x_nmr", [P, TB])
        alog = sb("alog", [P, 4, TB * H])
        la = sb("la", [P, TB, H])
        eg = sb("eg", [P, G, T])
        eg_end = [sb(f"eg_end{p}", [P, G, NC]) for p in range(2)]
        dec = sb("dec", [P, G, T])
        qraw = [sb(f"qraw{n}", [P, GU * T]) for n in range(2)]
        qsq = [sb(f"qsq{n}", [P, GU * T]) for n in range(2)]
        qr = [sb(f"qr{n}", [P, GU * T]) for n in range(2)]
        sg = sb("sg", [P, GU * T])
        kq = sb("kq", [P, G, NC, 2, C])
        vT = sb("vT", [P, G, T])
        beta = sb("beta", [P, G, T])
        silu = [sb(f"silu{p}", [P, G, T]) for p in range(2)]
        A = [sb(f"A{c}", [P, G, 2, C]) for c in range(NC)]
        kqd = [sb(f"kqd{c}", [P, G, 2, C]) for c in range(NC)]
        kd = [sb(f"kd{c}", [P, G, C]) for c in range(NC)]
        delT = [sb(f"delT{c}", [P, G, C]) for c in range(NC)]
        pairs = [sb(f"pairs{j}", [P, NPAIR]) for j in range(2)]
        S = sb("S", [P, G, DH])
        Sd = sb("Sd", [P, G, DH])
        U = sb("U", [P, G, C])
        Ut = sb("Ut", [P, G, CS])
        oT = sb("oT", [P, G, T])
        ctxT = sb("ctxT", [P, G, T])
        y = sb("y", [P, TB, D])
        x1 = sb("x1", [P, TB, D])
        xfw = sb("xfw", [P, TB, XSW])
        ssq = sb("ssq", [P, TB])
        lt = sb("lt", [P, 6, TB, E])
        l1 = sb("l1", [P, 4, TB])
        oh = sb("oh", [P, TB, E])
        base = sb("base", [P, E])
        slotf = sb("slotf", [P, TB])
        slot = sb("slot", [P, TB], I32)
        tok0 = sb("tok0", [P, TB])
        tokf = sb("tokf", [P, TB])
        ctx_flat = ctxT[:].rearrange("p g t -> p (g t)")
        gsb = qsq[1][:], ctx_flat[:, 0:GU * T]
        gT = qraw[1][:], ctx_flat[:, GU * T:2 * GU * T]
        lax = xt[:].rearrange("p b (h e) -> p b h e", h=H)
        xfT = xn[:].rearrange("p b d -> p (b d)").rearrange("p (k t) -> p k t", k=KD)
        hT = ctx_flat[:, 0:HID // P * BT].rearrange("p (n t) -> p n t", n=HID // P)
        junk = y
        osq = [y[:, hp, :] for hp in range(2)]
        ce = qsq[0][0:E, :]
        tabf = A[0][:].rearrange("p g a t -> p (g a t)")[:, 0:6 * P].rearrange("p (n m) -> p n m", n=6)
        vT_flat, beta_flat, eg_flat, dec_flat = (a[:].rearrange("p g t -> p (g t)") for a in (vT, beta, eg, dec))
        kq_flat = kq[:].rearrange("p g c a t -> p (g c a t)")
        sel_flat = sel[:].rearrange("p s l -> p (s l)")
        w_flat = w_sb[:].rearrange("p k n -> p (k n)")

        def side_by_side(flat, at, n, width):
            return [flat[:, at + i * width:at + (i + 1) * width] for i in range(n)]

        wc = [a.rearrange("p (k n) -> p k n", k=KD) for a in side_by_side(w_flat, 0, MQ, D)]
        pw = side_by_side(w_flat, MQ * D, MQ, D)
        pb_sb, lg_sb, lb_sb = side_by_side(w_flat, 2 * MQ * D, 3, D)
        xs = side_by_side(w_flat, (2 * MQ + 3) * D, MQ, XSW)
        pad = w_flat[:, (2 * MQ + 3) * D + MQ * XSW:(2 * MQ + 3) * D + (MQ + 1) * XSW]
        xsb = side_by_side(vT_flat, 0, 2, D)
        ya = [a[:, n * D:(n + 1) * D] for a in (eg_flat, dec_flat) for n in range(2)]
        z = side_by_side(sel_flat, 0, MQ, D)
        xsT = [a.rearrange("p (k t) -> p k t", k=KD) for a in side_by_side(kq_flat, 0, 2, D)]
        hm = side_by_side(kq_flat, 2 * D, 2, P)
        tb2, tb3 = (a.rearrange("p (e m) -> p e m", e=E) for a in side_by_side(sel_flat, 0, 2, E * P))
        krow = sb("krow", [P, P])
        col = sb("col", [P, 5, E])
        at = 0

        def in_qr(*shape, dt=F32):
            nonlocal at
            n = math.prod(shape)
            a, at = qr[0][:, at:at + n], at + n
            dims = {f"d{i}": d for i, d in enumerate(shape)}
            names = " ".join(dims)
            return a.bitcast(dt).rearrange(f"p ({names}) -> p {names}", **dims)

        tb = in_qr(3, E)
        tab = in_qr(2, P, dt=I32)
        cnt = in_qr(E, dt=I32)
        toki = in_qr(MQ, dt=I32)
        bc = in_qr(MQ)
        wtok = in_qr(MQ, 2)
        token = in_qr(MQ)
        mst = in_qr(2, 6)
        ymv = in_qr(MQ, 2)
        yr = in_qr(MQ)
        zmv = in_qr(MQ, 2)
        zr = in_qr(MQ)
        znm = in_qr(MQ)

        work = [ps(f"work{i}", [P, 512]) for i in range(NW)]
        kkq = ps("kkq", [P, G, 2, C])
        uk = ps("uk", [P, G, C])
        uq = ps("uq", [P, G, C])
        su = ps("su", [P, G, DH])
        kkq_flat = kkq[:].rearrange("p g a t -> p (g a t)")
        m_tp = [w[:] for w in work[0:2]]
        m_hp = [a[:].rearrange("p g t -> p (g t)")[:, 0:P] for a in (uk, uq)]
        m_yp = [kkq_flat[:, n * D:(n + 1) * D] for n in range(2)]

        loaded = sem("loaded")
        dve_step, act_step, pool_step = sem("dve_step"), sem("act_step"), sem("pool_step")
        names = """x_loaded xt_free xres_loaded x1_free x1_ready store_done
            x_norm_ready norm_ready xn_ready xT_full xT_ready alpha_full la_e_ready la_l_ready la_ready lax_ready
            G_full g_copied gT_ready diff_ready dec_ready eg_ready
            qk_full q_sq_ready ss_full q_r_ready qraw_free kq_free kq_ready_pe kq_ready_p
            v_full beta_full gate_full vb_ready beta_ready vb_free gate_ready sg_free
            pair_full pr_copied pr_ready pairs_free kkq_full kkq_free A_ready kt_ready kd_ready kqd_ready
            uk_full uq_free corr_full delT_ready S_ready S_ready_p su_full Sd_ready o_full
            o_sq_ready rms_full o_r_ready ctx_raw o_copied ctx_ready wo_full zn_ready y_ready
            xf_ready xfT_full xfT_ready ss_ready hid_full h_ready logits_full lg_ready sig_ready d_ready e_ready
            oh_ready rank_full slot_ready scat_done
            ce_sq ce_n ce_T base_ready setup_v setup_a cnt_ready table_ready
            m_xs_p m_xsb m_t m_t_free m_xsT m_h m_h_free m_hm m_y m_y_free m_v m_r m_n m_ya_free m_free m_t_done m_wfree m_pad
            """.split()
        s = {n: sem(n) for n in names}
        m_add = [sem(f"m_add{pair}") for pair in range(MQ // 2)]
        m_xs, m_wc = ([sem(f"{n}{u}") for u in range(MQ)] for n in ("m_xs", "m_wc"))
        work_free = [sem(f"work{i}_free") for i in range(NW)]

        def bank(*use):
            return work[BANK[use]][:]

        def bank_free(*use):
            return work_free[BANK[use]]

        def unit(a, hp):
            return a[:, hp * GU:(hp + 1) * GU]

        def flat(a):
            return a.rearrange("p g t -> p (g t)")

        def per_chunk(a):
            return a.rearrange("p (g c t) -> p g c t", g=GU, c=NC)

        block = ctx.enter_context(nc.Block())
        x_v = x.rearrange("(bh bl) (i t) d -> bl i t bh d", bl=BL, t=T)
        out_v = out.rearrange("(bh bl) (i t) d -> bl i t bh d", bl=BL, t=T)
        out_rows = out.rearrange("b l d -> (b l) d")

        loads = [
            (squares[:], c_sq), (sel[:], c_sel), (mask[:], c_mask), (iota[:], c_iota), (tok0[:], c_tok), (krow[:], c_row), (col[:], c_col),
            (w_sb[:], w_in.rearrange("(k p) n -> p k n", p=P)),
            (wa_sb[:], wa.rearrange("(k p) n -> p k n", p=P)),
            (dtb[:], dt_bias.partition_broadcast(P)), (neg_a[:], a_log.partition_broadcast(P)),
            (wo_sb[:], wo.rearrange("(k p) n -> p k n", p=P)), (bo_sb[:], bo.partition_broadcast(P)),
            (gw1_sb[:], gw1.rearrange("(k p) n -> p k n", p=P)),
            (gb1_sb[:], gb1),
            (gw2_sb[:], gw2.rearrange("(k p) n -> p k n", p=P)), (gb2_sb[:], gb2.partition_broadcast(P)),
            (ce, col_emb),
        ] + [(nw[DH * h:DH * h + DH, :], norm_w.rearrange("(p o) -> p o", o=1)) for h in range(HP)]
        ALL = 16 * len(loads)

        @block.sync
        def _(sp):
            for dst, src in loads:
                sp.dma_start(dst, src).then_inc(loaded, 16)
            def load_tokens(i):
                sp.wait_ge(s["xt_free"], 1)
                sp.sem_inc(s["xt_free"], -1)
                for bl in range(BL):
                    sp.dma_start(xt[bl * T:(bl + 1) * T], x_v[bl, bass.ds(i, 1)].rearrange("i t b d -> (i t) b d"))\
                        .then_inc(s["x_loaded"], 16)

            def add_and_store(i):
                sp.wait_ge(s["x1_free"], 1)
                sp.sem_inc(s["x1_free"], -1)
                for bl in range(BL):
                    sp.dma_start(x1[bl * T:(bl + 1) * T], x_v[bl, bass.ds(i, 1)].rearrange("i t b d -> (i t) b d"))\
                        .then_inc(s["xres_loaded"], 16)
                sp.wait_ge(s["x1_ready"], 1)
                sp.sem_inc(s["x1_ready"], -1)
                for bl in range(BL):
                    sp.dma_start(out_v[bl, bass.ds(i, 1)].rearrange("i t b d -> (i t) b d"), x1[bl * T:(bl + 1) * T])\
                        .then_inc(s["store_done"], 16)
                sp.wait_ge(s["store_done"], 16 * BL)
                sp.sem_inc(s["store_done"], -(16 * BL))

            load_tokens(0)
            load_tokens(1)
            with sp.Fori(0, NT - 2) as i:
                load_tokens(i + 2)
                add_and_store(i)
            load_tokens(NT - 1)
            add_and_store(NT - 2)
            add_and_store(NT - 1)
            for dst, src in ((pad, c_pad), (pb_sb, proj_b.partition_broadcast(P)), (lg_sb, ln_g.partition_broadcast(P)),
                             (lb_sb, ln_b.partition_broadcast(P))):
                sp.dma_start(dst, src).then_inc(s["m_pad"], 16)
            sp.wait_ge(s["m_pad"], 64)
            sp.sem_inc(s["m_pad"], -64)
            sp.wait_ge(s["cnt_ready"], 1)
            sp.sem_inc(s["cnt_ready"], -1)
            for e in range(E):
                behind = nc.sync.value_load(cnt[0:1, e:e + 1], min_val=0, max_val=PADROW)
                sp.dma_start(xs_dram[bass.ds(behind, P)], pad).then_inc(s["m_pad"], 16)
            sp.dma_start(xs_dram[PADROW:PADROW + P], pad).then_inc(s["m_pad"], 16)
            sp.wait_ge(s["m_pad"], 16 * (E + 1))
            sp.sem_inc(s["m_pad"], -(16 * (E + 1)))
            sp.wait_ge(s["table_ready"], 1)
            sp.sem_inc(s["table_ready"], -1)
            sp.wait_ge(s["scat_done"], 16 * TB * NT)
            with sp.Fori(0, NM // MQ) as q:
                for u in range(MQ):
                    e_m = nc.sync.value_load(tab[0:1, 0, bass.ds(q * MQ + u, 1)], min_val=0, max_val=E - 1)
                    r_m = nc.sync.value_load(tab[0:1, 1, bass.ds(q * MQ + u, 1)], min_val=0, max_val=PADROW)
                    sp.wait_ge(s["m_free"], 1)
                    sp.sem_inc(s["m_free"], -1)
                    sp.wait_ge(s["m_t_done"], 1)
                    sp.sem_inc(s["m_t_done"], -1)
                    sp.dma_start(xs[u], xs_dram[bass.ds(r_m, P)]).then_inc(m_xs[u], 16)
                    sp.wait_ge(s["m_wfree"], 1)
                    sp.sem_inc(s["m_wfree"], -1)
                    sp.dma_start(wc[u], w_cols[bass.ds(e_m, 1)].rearrange("e (k p) n -> p (e k) n", p=P))\
                        .then_inc(m_wc[u], 16)
                    sp.dma_start(bc[:, u:u + 1], b_cols[bass.ds(e_m, 1)].rearrange("e n o -> (e n) o"))\
                        .then_inc(m_wc[u], 16)
                    sp.dma_start(pw[u], proj_w[bass.ds(e_m, 1)].rearrange("e n d -> (e n) d")).then_inc(m_wc[u], 16)

        @block.tensor
        def _(pe):
            def into(*use):
                pe.wait_ge(bank_free(*use), 1)
                pe.sem_inc(bank_free(*use), -1)
                return bank(*use)

            def project(name, j, hp, half):
                use = (name, hp if name != "qk" else 2 * j + hp)
                w = bank(*use) if half else into(*use)
                hg = 2 * hp + half
                for f in range(KD):
                    mm = pe.matmul(w[:, half * BT:(half + 1) * BT], w_sb[:, f, j * D + hg * P:j * D + (hg + 1) * P],
                                   xT[:, f, :], start=(f == 0), stop=(f == KD - 1))
                if half:
                    mm.then_inc(s[name + "_full"], 1)

            def squares_sum(n):
                pe.wait_ge(s["q_sq_ready"], 1)
                pe.sem_inc(s["q_sq_ready"], -1)
                w = into("ss", n)
                pe.matmul(w, blk1, qsq[n % 2][:], start=True, stop=True).then_inc(s["ss_full"], 1)

            def turn(name, src, n):
                w = into(name, n)
                for half in range(2):
                    f = 2 * n + half
                    for tb in range(TB):
                        mm = pe.transpose(w[:, half * BT + tb * P:half * BT + (tb + 1) * P], src[:, tb, f * P:(f + 1) * P], ident)
                mm.then_inc(s[name + "_full"], 1)

            def on_tiles(half, full, product):
                for g in range(half * GU, (half + 1) * GU):
                    for h in range(HP):
                        mm = product(g, slice(DH * h, DH * h + DH), slice(DH * h, DH * h + CS))
                if half and full:
                    mm.then_inc(s[full], 1)

            def key_products(c, half):
                if not half:
                    pe.wait_ge(s["kkq_free"], 1)
                    pe.sem_inc(s["kkq_free"], -1)
                on_tiles(half, "kkq_full", lambda g, q, q_half: pe.matmul(
                    kkq[q, g], kq[q, g, c, 0, :], kq[q, g, c].rearrange("p a t -> p (a t)"), start=True, stop=True))

            def spread_pairs(c, j, i):
                w = into("pair", c, j, i)
                o = 0
                for t0 in PACKS[i]:
                    n = G * WID[t0]
                    mm = pe.matmul(w[:, o:o + n], sel[:, j * CS + t0, :], A[c][:, :, 0, j * CS + t0 + 1:(j + 1) * CS],
                                   start=(o == 0), stop=True, skip_group_check=True)
                    o += n
                mm.then_inc(s["pair_full"], 1)

            def state_to_u(c, half):
                if not half:
                    pe.wait_ge(s["kqd_ready"], 1)
                    pe.sem_inc(s["kqd_ready"], -1)
                    pe.wait_ge(s["S_ready"], 1)
                    pe.sem_inc(s["S_ready"], -1)
                on_tiles(half, "uk_full", lambda g, q, q_half: pe.matmul(
                    uk[q, g], S[q, g, :], kqd[c][q, g, 0, :], start=(g == 0), stop=True, skip_group_check=True))

            def first_half_to_u(c, half):
                if not half:
                    pe.wait_ge(s["delT_ready"], 1)
                    pe.sem_inc(s["delT_ready"], -1)
                on_tiles(half, "corr_full", lambda g, q, q_half: pe.matmul(
                    uk[q, g, CS:C], delT[c][q_half, g, :], A[c][q_half, g, 0, CS:C],
                    start=False, stop=True, skip_group_check=True))

            def state_to_outputs(c, half):
                if not half:
                    pe.wait_ge(s["uq_free"], 1)
                    pe.sem_inc(s["uq_free"], -1)
                on_tiles(half, None, lambda g, q, q_half: pe.matmul(
                    uq[q, g], S[q, g, :], kqd[c][q, g, 1, :], start=(g == 0), stop=True, skip_group_check=True))

            def chunk_to_outputs(c, half):
                on_tiles(half, "o_full", lambda g, q, q_half: pe.matmul(
                    uq[q, g], delT[c][q, g, :], A[c][q, g, 1, :], start=False, stop=True, skip_group_check=True))

            def change_state(c, half):
                if not half:
                    pe.wait_ge(s["delT_ready"], 1)
                    pe.sem_inc(s["delT_ready"], -1)
                    pe.wait_ge(s["kd_ready"], 1)
                    pe.sem_inc(s["kd_ready"], -1)
                on_tiles(half, "su_full", lambda g, q, q_half: pe.matmul(
                    su[q, g, :], kd[c][q, g, :], delT[c][q, g, :], start=True, stop=True))

            def log_alpha(tb):
                w = bank("alpha") if tb else into("alpha")
                for f in range(KD):
                    mm = pe.matmul(w[:, tb * H:(tb + 1) * H], xT[:, f, tb * P:(tb + 1) * P], wa_sb[:, f, :],
                                   start=(f == 0), stop=(f == KD - 1))
                if tb == TB - 1:
                    mm.then_inc(s["alpha_full"], 1)

            def decays(hp):
                w = into("G", hp)
                for half in range(2):
                    hg = 2 * hp + half
                    for tb in range(TB):
                        mm = pe.matmul(w[:, half * BT + tb * P:half * BT + (tb + 1) * P],
                                       lax[:, tb, hg * HP:(hg + 1) * HP, :].rearrange("p h e -> p (h e)"), ucum,
                                       start=True, stop=True)
                mm.then_inc(s["G_full"], 1)

            def outputs_squares_sum(hp):
                pe.wait_ge(s["o_sq_ready"], 1)
                pe.sem_inc(s["o_sq_ready"], -1)
                w = into("rms", hp)
                pe.matmul(w, blk1, osq[hp], start=True, stop=True).then_inc(s["rms_full"], 1)

            def output_projection(tb):
                w = into("wo", tb)
                for hg in range(KD):
                    mm = pe.matmul(w, flat(ctxT[:, hg * B + tb * BL:hg * B + (tb + 1) * BL, :]), wo_sb[:, hg, :],
                                   start=(hg == 0), stop=(hg == KD - 1))
                mm.then_inc(s["wo_full"], 1)

            def gate_hidden():
                w = into("hid")
                for n in range(HID // P):
                    for f in range(KD):
                        mm = pe.matmul(w[:, n * BT:(n + 1) * BT], gw1_sb[:, f, n * P:(n + 1) * P], xfT[:, f, :],
                                       start=(f == 0), stop=(f == KD - 1))
                mm.then_inc(s["hid_full"], 1)

            def gate_logits(tb):
                if tb == 0:
                    pe.wait_ge(s["h_ready"], 1)
                    pe.sem_inc(s["h_ready"], -1)
                w = bank("logits") if tb else into("logits")
                tok = slice(tb * P, (tb + 1) * P)
                for f in range(KD):
                    pe.matmul(w[:, tb * 2 * E:tb * 2 * E + E], xfT[:, f, tok], ceT[:, f, :],
                              start=(f == 0), stop=(f == KD - 1))
                for n in range(HID // P):
                    mm = pe.matmul(w[:, tb * 2 * E + E:(tb + 1) * 2 * E], hT[:, n, tok], gw2_sb[:, n, :],
                                   start=(n == 0), stop=(n == HID // P - 1))
                if tb == TB - 1:
                    mm.then_inc(s["logits_full"], 1)

            def ranks():
                pe.wait_ge(s["oh_ready"], 1)
                pe.sem_inc(s["oh_ready"], -1)
                w = into("rank")
                pe.matmul(w[:, 0:TB * E], ustrict, oh[:].rearrange("p b e -> p (b e)"), start=True, stop=False,
                          skip_group_check=True)
                for n in range(1, TB):
                    pe.matmul(w[:, n * E:TB * E], ones, oh[:, 0:TB - n, :].rearrange("p b e -> p (b e)"),
                              start=False, stop=False, skip_group_check=True)
                for tb in range(TB):
                    mm = pe.matmul(w[:, TB * E:(TB + 1) * E], ones, oh[:, tb, :], start=False, stop=(tb == TB - 1),
                                   skip_group_check=True)
                mm.then_inc(s["rank_full"], 1)

            def step(p, chain, after, ahead):
                if chain:
                    spread_pairs(0, 1, 0)
                    spread_pairs(0, 1, 1)
                    spread_pairs(0, 1, 2)
                    state_to_u(0, 0)
                    spread_pairs(0, 1, 3)
                    state_to_u(0, 1)
                if ahead:
                    pe.wait_ge(s["xn_ready"], TB)
                    pe.sem_inc(s["xn_ready"], -TB)
                    turn("xT", xn, 0)
                if after:
                    chunk_to_outputs(NC - 1, 0)
                if ahead:
                    turn("xT", xn, 1)
                if after:
                    chunk_to_outputs(NC - 1, 1)
                if ahead:
                    pe.wait_ge(s["xT_ready"], 2)
                    pe.sem_inc(s["xT_ready"], -2)
                    project("qk", 0, 0, 0)
                if chain:
                    key_products(1, 0)
                if ahead:
                    project("qk", 0, 0, 1)
                if chain:
                    key_products(1, 1)
                if after:
                    outputs_squares_sum(0)
                if ahead:
                    log_alpha(0)
                    project("qk", 0, 1, 0)
                    log_alpha(1)
                if after:
                    outputs_squares_sum(1)
                if ahead:
                    squares_sum(0)
                if chain:
                    first_half_to_u(0, 0)
                if ahead:
                    project("qk", 0, 1, 1)
                if chain:
                    first_half_to_u(0, 1)
                if chain:
                    pe.wait_ge(s["A_ready"], 1)
                    pe.sem_inc(s["A_ready"], -1)
                    spread_pairs(1, 0, 0)
                    state_to_outputs(0, 0)
                    spread_pairs(1, 0, 1)
                    spread_pairs(1, 0, 2)
                    state_to_outputs(0, 1)
                    spread_pairs(1, 0, 3)
                if after:
                    pe.wait_ge(s["ctx_ready"], 2)
                    pe.sem_inc(s["ctx_ready"], -2)
                    output_projection(0)
                    output_projection(1)
                if ahead:
                    project("qk", 1, 0, 0)
                    project("qk", 1, 0, 1)
                    squares_sum(1)
                    pe.wait_ge(s["lax_ready"], 1)
                    pe.sem_inc(s["lax_ready"], -1)
                    decays(0)
                if chain:
                    change_state(0, 0)
                if ahead:
                    decays(1)
                if chain:
                    change_state(0, 1)
                if ahead:
                    project("qk", 1, 1, 0)
                if chain:
                    state_to_u(1, 0)
                if ahead:
                    project("qk", 1, 1, 1)
                if chain:
                    state_to_u(1, 1)
                    spread_pairs(1, 1, 0)
                    chunk_to_outputs(0, 0)
                    spread_pairs(1, 1, 1)
                    spread_pairs(1, 1, 2)
                    chunk_to_outputs(0, 1)
                    spread_pairs(1, 1, 3)
                if ahead:
                    squares_sum(2)
                    project("gate", 4, 0, 0)
                    project("gate", 4, 0, 1)
                    squares_sum(3)
                    project("gate", 4, 1, 0)
                if chain:
                    first_half_to_u(1, 0)
                if ahead:
                    project("gate", 4, 1, 1)
                if chain:
                    first_half_to_u(1, 1)
                if ahead:
                    project("beta", 3, 0, 0)
                    pe.wait_ge(s["kq_ready_pe"], 4)
                    pe.sem_inc(s["kq_ready_pe"], -4)
                    key_products(0, 0)
                    project("beta", 3, 0, 1)
                    key_products(0, 1)
                if after:
                    pe.wait_ge(s["xf_ready"], TB)
                    pe.sem_inc(s["xf_ready"], -TB)
                    turn("xfT", xfw, 0)
                    turn("xfT", xfw, 1)
                if ahead:
                    project("beta", 3, 1, 0)
                if chain:
                    state_to_outputs(1, 0)
                if ahead:
                    project("beta", 3, 1, 1)
                if chain:
                    state_to_outputs(1, 1)
                if after:
                    pe.wait_ge(s["xfT_ready"], 2)
                    pe.sem_inc(s["xfT_ready"], -2)
                    gate_hidden()
                if ahead:
                    pe.wait_ge(s["A_ready"], 1)
                    pe.sem_inc(s["A_ready"], -1)
                    spread_pairs(0, 0, 0)
                    spread_pairs(0, 0, 1)
                    spread_pairs(0, 0, 2)
                    spread_pairs(0, 0, 3)
                    project("v", 2, 0, 0)
                if after:
                    gate_logits(0)
                if ahead:
                    project("v", 2, 0, 1)
                if after:
                    gate_logits(1)
                if ahead:
                    project("v", 2, 1, 0)
                if chain:
                    change_state(1, 0)
                if ahead:
                    project("v", 2, 1, 1)
                if after:
                    ranks()
                if chain:
                    change_state(1, 1)

            pe.wait_ge(loaded, ALL)
            pe.wait_ge(s["ce_n"], 1)
            pe.sem_inc(s["ce_n"], -1)
            for k in range(KD):
                mm = pe.transpose(work[0][:, k * E:(k + 1) * E], ce[:, k * P:(k + 1) * P], ident[0:E, 0:E])
            mm.then_inc(s["ce_T"], 1)
            step(1, False, False, True)
            step(0, True, False, True)
            with pe.Fori(0, NT // 2 - 1):
                step(1, True, True, True)
                step(0, True, True, True)
            step(1, True, True, False)
            step(0, False, True, False)
            with pe.Fori(0, NM // MQ):
                def turn_rows(u):
                    pe.wait_ge(m_xs[u], 16)
                    pe.sem_inc(m_xs[u], -16)
                    pe.sem_inc(s["m_xs_p"], 1)
                    pe.wait_ge(s["m_t_free"], 1)
                    pe.sem_inc(s["m_t_free"], -1)
                    for f in range(KD):
                        mm = pe.transpose(m_tp[u % 2][:, f * P:(f + 1) * P], xs[u][:, f * P:(f + 1) * P], ident)
                    mm.then_inc(s["m_t"], 1)

                def neurons(u):
                    pe.wait_ge(m_wc[u], 48)
                    pe.sem_inc(m_wc[u], -48)
                    pe.wait_ge(s["m_xsT"], 1)
                    pe.sem_inc(s["m_xsT"], -1)
                    pe.wait_ge(s["m_h_free"], 1)
                    pe.sem_inc(s["m_h_free"], -1)
                    for f in range(KD):
                        mm = pe.matmul(m_hp[u % 2], wc[u][:, f, :], xsT[u % 2][:, f, :],
                                       start=(f == 0), stop=(f == KD - 1))
                    mm.then_inc(s["m_h"], 1)

                def columns_result(u):
                    pe.wait_ge(s["m_hm"], 1)
                    pe.sem_inc(s["m_hm"], -1)
                    pe.wait_ge(s["m_y_free"], 1)
                    pe.sem_inc(s["m_y_free"], -1)
                    pe.matmul(m_yp[u % 2], hm[u % 2], pw[u], start=True, stop=True).then_inc(s["m_y"], 1)

                for stage, u in ((turn_rows, 0), (turn_rows, 1), (neurons, 0), (neurons, 1), (turn_rows, 2), (columns_result, 0),
                                 (turn_rows, 3), (columns_result, 1), (neurons, 2), (neurons, 3), (columns_result, 2),
                                 (columns_result, 3)):
                    stage(u)

        @block.scalar
        def _(act):
            link = Chain(act, act_step)

            def load_ln_exp():
                nc.scalar.preload_act_table_set("natural_log_exp_and_others")

            def norm_tokens(dst, src, r, nm, ready):
                for tb in range(TB):
                    link(nc.scalar.activation(dst[:, tb, 0:D], src[:, tb, :], ACT.Identity,
                                              scale=r[:, tb:tb + 1], bias=nm[:, tb:tb + 1]))
                    act.sem_inc(ready, 1)

            def copy_pairs(c, j):
                act.wait_ge(s["pairs_free"], 1)
                act.sem_inc(s["pairs_free"], -1)
                for i, pack in enumerate(PACKS):
                    n = G * sum(WID[t0] for t0 in pack)
                    act.wait_ge(s["pair_full"], 1)
                    act.sem_inc(s["pair_full"], -1)
                    link(nc.scalar.activation(pairs[j][:, OFF[pack[0]]:OFF[pack[0]] + n], bank("pair", c, j, i)[:, 0:n], ACT.Copy))
                    act.sem_inc(bank_free("pair", c, j, i), 1)
                act.sem_inc(s["pr_copied"], 1)

            def copy_outputs(c):
                act.wait_ge(s["o_full"], 1)
                act.sem_inc(s["o_full"], -1)
                link(nc.scalar.activation(oT[:, :, c * C:(c + 1) * C], uq[:], ACT.Copy))
                act.sem_inc(s["uq_free"], 1)

            def copy_turned(name, dst, ready, n):
                act.wait_ge(s[name + "_full"], 1)
                act.sem_inc(s[name + "_full"], -1)
                link(nc.scalar.activation(dst[:, 2 * n:2 * n + 2, :].rearrange("p k t -> p (k t)"), bank(name, n), ACT.Copy))
                act.sem_inc(bank_free(name, n), 1)
                act.sem_inc(ready, 1)

            def copy_and_square(n):
                act.wait_ge(s["qraw_free"], 1)
                act.sem_inc(s["qraw_free"], -1)
                act.wait_ge(s["qk_full"], 1)
                act.sem_inc(s["qk_full"], -1)
                link(nc.scalar.activation(qraw[n % 2][:], bank("qk", n), ACT.Copy))
                link(nc.scalar.activation(qsq[n % 2][:], bank("qk", n), ACT.Square))
                act.sem_inc(bank_free("qk", n), 1)
                act.sem_inc(s["q_sq_ready"], 1)

            def inverse_norm(n):
                r = qr[n % 2][:]
                act.wait_ge(s["ss_full"], 1)
                act.sem_inc(s["ss_full"], -1)
                link(nc.scalar.activation(r, bank("ss", n), ACT.Ln))
                act.sem_inc(bank_free("ss", n), 1)
                nc.scalar.activation(r, r, ACT.Exp, scale=-0.5, **({"bias": lnq[:]} if n < 2 else {}))\
                    .then_inc(s["q_r_ready"], 1)

            def copy_decays(hp, p_next):
                act.wait_ge(s["G_full"], 1)
                act.sem_inc(s["G_full"], -1)
                w = bank("G", hp)
                link(nc.scalar.activation(gsb[hp], w, ACT.Copy))
                act.sem_inc(s["g_copied"], 1)
                nc.scalar.activation(unit(eg_end[p_next], hp), per_chunk(w)[:, :, :, C - 1], ACT.Exp)
                link(nc.scalar.activation(flat(unit(eg, hp)), w, ACT.Exp))
                act.sem_inc(bank_free("G", hp), 1)
                act.sem_inc(s["eg_ready"], 1)

            def pair_decays(hp):
                act.wait_ge(s["diff_ready"], 1)
                act.sem_inc(s["diff_ready"], -1)
                link(nc.scalar.activation(flat(unit(dec, hp)), flat(unit(dec, hp)), ACT.Exp))
                act.sem_inc(s["dec_ready"], 1)

            def square_outputs(hp):
                nc.scalar.activation(osq[hp], flat(unit(oT, hp)), ACT.Square).then_inc(s["o_sq_ready"], 1)

            def inverse_rms(hp):
                r = qr[hp][:]
                act.wait_ge(s["rms_full"], 1)
                act.sem_inc(s["rms_full"], -1)
                link(nc.scalar.activation(r, bank("rms", hp), ACT.Ln, scale=1.0 / DH, bias=eps6[:]))
                act.sem_inc(bank_free("rms", hp), 1)
                nc.scalar.activation(r, r, ACT.Exp, scale=-0.5).then_inc(s["o_r_ready"], 1)

            def sigmoid(name, hp, dst):
                act.wait_ge(s[name + "_full"], 1)
                act.sem_inc(s[name + "_full"], -1)
                return nc.scalar.activation(dst, bank(name, hp), ACT.Sigmoid)

            def copy_values(hp):
                act.wait_ge(s["v_full"], 1)
                act.sem_inc(s["v_full"], -1)
                link(nc.scalar.activation(flat(unit(vT, hp)), bank("v", hp), ACT.Copy))
                act.sem_inc(bank_free("v", hp), 1)

            def step(p, chain, after, ahead):
                if ahead:
                    act.wait_ge(s["x_norm_ready"], 1)
                    act.sem_inc(s["x_norm_ready"], -1)
                    norm_tokens(xn, xt, x_rstd, x_nmr, s["xn_ready"])
                if chain:
                    copy_pairs(0, 1)
                if ahead:
                    copy_turned("xT", xT, s["xT_ready"], 0)
                    copy_turned("xT", xT, s["xT_ready"], 1)
                if after:
                    copy_outputs(NC - 1)
                    square_outputs(0)
                    square_outputs(1)
                if ahead:
                    copy_and_square(0)
                if after:
                    inverse_rms(0)
                    inverse_rms(1)
                if ahead:
                    act.wait_ge(s["la_e_ready"], 1)
                    act.sem_inc(s["la_e_ready"], -1)
                    link(nc.scalar.activation(alog[:, 2, :], alog[:, 1, :], ACT.Exp, scale=-1.0))
                    nc.scalar.activation(alog[:, 3, :], alog[:, 2, :], ACT.Ln, bias=1.0).then_inc(s["la_l_ready"], 1)
                if after:
                    act.wait_ge(s["ctx_raw"], 2)
                    act.sem_inc(s["ctx_raw"], -2)
                if ahead:
                    inverse_norm(0)
                    copy_and_square(1)
                if chain:
                    copy_pairs(1, 0)
                if ahead:
                    copy_and_square(2)
                    inverse_norm(1)
                if after:
                    act.wait_ge(s["norm_ready"], 1)
                    act.sem_inc(s["norm_ready"], -1)
                    norm_tokens(y, y, rstd, nmr, s["zn_ready"])
                if ahead:
                    copy_decays(0, 1 - p)
                    copy_decays(1, 1 - p)
                    act.sem_inc(s["xt_free"], 1)
                    pair_decays(0)
                    copy_and_square(3)
                if chain:
                    copy_pairs(1, 1)
                    copy_outputs(0)
                if ahead:
                    pair_decays(1)
                    inverse_norm(2)
                    inverse_norm(3)
                def next_gate(hp):
                    act.wait_ge(s["sg_free"], 1)
                    act.sem_inc(s["sg_free"], -1)
                    link(sigmoid("gate", hp, sg[:]))
                    act.sem_inc(s["gate_ready"], 1)

                if ahead:
                    next_gate(0)
                if after:
                    act.wait_ge(s["norm_ready"], 1)
                    act.sem_inc(s["norm_ready"], -1)
                    norm_tokens(xfw, x1, rstd, nmr, s["xf_ready"])
                    act.sem_inc(s["x1_free"], 1)
                    for tb in range(TB):
                        link(nc.scalar.activation(junk[:, tb, :], xfw[:, tb, 0:D], ACT.Square, accum_out=ssq[:, tb:tb + 1]))
                    act.sem_inc(s["ss_ready"], 1)
                if ahead:
                    next_gate(1)

                def next_beta(hp):
                    link(sigmoid("beta", hp, flat(unit(beta, hp))))
                    act.sem_inc(bank_free("beta", hp), 1)
                    act.sem_inc(s["beta_ready"], 1)

                if ahead:
                    if chain:
                        act.wait_ge(s["vb_free"], 1)
                        act.sem_inc(s["vb_free"], -1)
                    next_beta(0)
                if after:
                    copy_turned("xfT", xfT, s["xfT_ready"], 0)
                    copy_turned("xfT", xfT, s["xfT_ready"], 1)
                if ahead:
                    next_beta(1)
                if after:
                    act.wait_ge(s["hid_full"], 1)
                    act.sem_inc(s["hid_full"], -1)
                    for n in range(HID // P):
                        link(nc.scalar.activation(hT[:, n, :], bank("hid")[:, n * BT:(n + 1) * BT], ACT.Gelu, bias=gb1_sb[:, n:n + 1]))
                    act.sem_inc(bank_free("hid"), 1)
                    act.sem_inc(s["h_ready"], 1)
                if ahead:
                    copy_pairs(0, 0)
                    copy_values(0)
                if after:
                    act.wait_ge(s["lg_ready"], 1)
                    act.sem_inc(s["lg_ready"], -1)
                    nc.scalar.activation(lt[:, 1], lt[:, 1], ACT.Tanh, scale=0.5).then_inc(s["sig_ready"], 1)
                load_ln_exp()
                if ahead:
                    copy_values(1)
                    act.sem_inc(s["vb_ready"], 1)
                if after:
                    act.wait_ge(s["d_ready"], 1)
                    act.sem_inc(s["d_ready"], -1)
                    nc.scalar.activation(lt[:, 3], lt[:, 2], ACT.Exp).then_inc(s["e_ready"], 1)
                link.restart()

            act.wait_ge(loaded, ALL)
            load_ln_exp()
            act.wait_ge(s["setup_v"], 1)
            act.sem_inc(s["setup_v"], -1)
            link(nc.scalar.activation(neg_a[:], neg_a[:], ACT.Exp))
            act.sem_inc(s["setup_a"], 1)
            link(nc.scalar.activation(junk[0:E, 0, :], ce, ACT.Square, accum_out=ce_s[:, 0:1]))
            act.sem_inc(s["ce_sq"], 1)
            link.restart()
            step(1, False, False, True)
            step(0, True, False, True)
            with act.Fori(0, NT // 2 - 1):
                step(1, True, True, True)
                step(0, True, True, True)
            step(1, True, True, False)
            step(0, False, True, False)
            nc.scalar.preload_act_table_set("gelu_and_others")
            with act.Fori(0, NM // MQ):
                def copy_turned_rows(u):
                    act.wait_ge(s["m_t"], 1)
                    act.sem_inc(s["m_t"], -1)
                    act.sem_inc(s["m_t_done"], 1)
                    link(nc.scalar.activation(xsT[u % 2].rearrange("p k t -> p (k t)"), m_tp[u % 2], ACT.Copy))
                    act.sem_inc(s["m_t_free"], 1)
                    act.sem_inc(s["m_xsT"], 1)

                def activate(u):
                    act.wait_ge(s["m_h"], 1)
                    act.sem_inc(s["m_h"], -1)
                    link(nc.scalar.activation(hm[u % 2], m_hp[u % 2], ACT.Gelu, bias=bc[:, u:u + 1]))
                    act.sem_inc(s["m_h_free"], 1)
                    act.sem_inc(s["m_hm"], 1)

                for stage, u in ((copy_turned_rows, 0), (copy_turned_rows, 1), (activate, 0), (activate, 1),
                                 (copy_turned_rows, 2), (copy_turned_rows, 3), (activate, 2), (activate, 3)):
                    stage(u)
                link.restart()

        @block.gpsimd
        def _(pool):
            link = Chain(pool, pool_step)

            def decay_state(p, c):
                pool.wait_ge(s["S_ready_p"], 1)
                pool.sem_inc(s["S_ready_p"], -1)
                nc.gpsimd.tensor_tensor(Sd[:], S[:], eg_end[p][:, :, c:c + 1].to_broadcast([P, G, DH]), ALU.mult)\
                    .then_inc(s["Sd_ready"], 1)

            def decay_k_and_q(c):
                link(nc.gpsimd.tensor_tensor(kqd[c][:], kq[:, :, c], eg[:, :, c * C:(c + 1) * C].unsqueeze(2).to_broadcast([P, G, 2, C]),
                                             ALU.mult))
                pool.sem_inc(s["kqd_ready"], 1)

            def pairs_times_beta(c, j):
                pool.wait_ge(s["pr_copied"], 1)
                pool.sem_inc(s["pr_copied"], -1)
                for t0 in range(CS - 1):
                    a = pairs[j][:, OFF[t0]:OFF[t0] + G * WID[t0]].rearrange("p (g t) -> p g t", g=G)
                    t = c * C + j * CS + t0 + 1
                    ins = nc.gpsimd.tensor_tensor(a, a, beta[:, :, t:t + WID[t0]], ALU.mult)
                ins.then_inc(s["pr_ready"], 1)

            def step(p, chain, after, ahead, added):
                if chain:
                    decay_state(p, 0)
                    decay_k_and_q(1)
                    pool.sem_inc(s["kq_free"], 1)
                    pairs_times_beta(0, 1)
                    pool.wait_ge(s["kt_ready"], 1)
                    pool.sem_inc(s["kt_ready"], -1)
                    for c in range(NC):
                        link(nc.gpsimd.tensor_tensor(kd[c][:], kd[c][:], dec[:, :, c * C + C - 1:c * C + C].to_broadcast([P, G, C]),
                                                     ALU.mult))
                        pool.sem_inc(s["kd_ready"], 1)
                if ahead:
                    pool.wait_ge(s["la_ready"], 1)
                    pool.sem_inc(s["la_ready"], -1)
                    nc.gpsimd.tensor_copy(lax, la[:].unsqueeze(3).to_broadcast([P, TB, H, DH])).then_inc(s["lax_ready"], 1)
                if after:
                    for hp in range(2):
                        pool.wait_ge(s["o_copied"], 1)
                        pool.sem_inc(s["o_copied"], -1)
                        nc.gpsimd.tensor_tensor(unit(ctxT, hp), unit(ctxT, hp), unit(silu[1 - p], hp), ALU.mult)\
                            .then_inc(s["ctx_ready"], 1)
                if chain:
                    pairs_times_beta(1, 0)
                if after:
                    pool.wait_ge(s["xres_loaded"], 16 * BL)
                    pool.sem_inc(s["xres_loaded"], -(16 * BL))
                    for tb in range(TB):
                        pool.wait_ge(s["zn_ready"], 1)
                        pool.sem_inc(s["zn_ready"], -1)
                        link(nc.gpsimd.tensor_tensor(x1[:, tb, :], x1[:, tb, :], y[:, tb, :], ALU.add))
                    pool.sem_inc(s["y_ready"], 1)
                    pool.sem_inc(s["x1_ready"], 1)
                if ahead:
                    for hp in range(2):
                        pool.wait_ge(s["gT_ready"], 1)
                        pool.sem_inc(s["gT_ready"], -1)
                        d = flat(unit(dec, hp))
                        link(nc.gpsimd.tensor_tensor(d, gsb[hp], gT[hp], ALU.subtract))
                        dt = d.rearrange("p (n t) -> p n t", t=C)
                        link(nc.gpsimd.tensor_tensor(dt, dt, mask[:].unsqueeze(1).to_broadcast([P, GU * NC, C]), ALU.add))
                        pool.sem_inc(s["diff_ready"], 1)
                if chain:
                    decay_state(p, 1)
                    pairs_times_beta(1, 1)
                if ahead:
                    pool.wait_ge(s["eg_ready"], 2)
                    pool.sem_inc(s["eg_ready"], -2)
                    pool.wait_ge(s["kq_ready_p"], 4)
                    pool.sem_inc(s["kq_ready_p"], -4)
                    decay_k_and_q(0)
                    pool.wait_ge(s["beta_ready"], 2)
                    pool.sem_inc(s["beta_ready"], -2)
                    pairs_times_beta(0, 0)
                if after:
                    pool.wait_ge(s["slot_ready"], 1)
                    pool.sem_inc(s["slot_ready"], -1)
                    for tb in range(TB):
                        nc.gpsimd.indirect_dma_start(
                            xs_dram, bass.IndirectOffsetOnAxis(ap=slot[:, tb:tb + 1].bitcast(U32), axis=0),
                            xfw[:, tb, :], None).then_inc(s["scat_done"], 16)
                    pool.wait_ge(s["scat_done"], added)
                link.restart()

            pool.wait_ge(loaded, ALL)
            link(nc.gpsimd.memset(minus_half[:], -0.5))
            link(nc.gpsimd.memset(S[:], 0.0))
            pool.sem_inc(s["S_ready"], 1)
            link(nc.gpsimd.memset(base[:], 0.0))
            pool.sem_inc(s["base_ready"], 1)
            for n in ("xt_free", "x1_free", "kkq_free", "uq_free", "sg_free", "S_ready_p"):
                pool.sem_inc(s[n], 1)
            for f in work_free:
                pool.sem_inc(f, 1)
            for n in ("pairs_free", "qraw_free"):
                pool.sem_inc(s[n], 2)
            link.restart()
            ROW = 16 * TB
            step(1, False, False, True, None)
            step(0, True, False, True, None)
            with pool.Fori(0, NT // 2 - 1) as i:
                step(1, True, True, True, i * (2 * ROW) + ROW)
                step(0, True, True, True, i * (2 * ROW) + 2 * ROW)
            step(1, True, True, False, (NT - 1) * ROW)
            step(0, False, True, False, NT * ROW)
            def add_bias(u):
                pool.wait_ge(s["m_xs_p"], 1)
                pool.sem_inc(s["m_xs_p"], -1)
                link(nc.gpsimd.tensor_copy(wtok[:, u, :], xs[u][:, D:D + 2]))
                if u < 2:
                    link(nc.gpsimd.tensor_tensor(xsb[u], xs[u][:, 0:D], pb_sb, ALU.add))
                    pool.sem_inc(s["m_free"], 1)
                pool.sem_inc(s["m_xsb"], 1)

            def inverse_std(r, mv, pair, added=None):
                two = slice(2 * pair, 2 * pair + 2)
                link(nc.gpsimd.tensor_scalar(r[:, two], mv[:, two, 1], 1e-5, None, ALU.add))
                if added is not None:
                    pool.wait_ge(m_add[pair], added)
                link(nc.gpsimd.tensor_tensor(r[:, two], r[:, two], minus_half[:].to_broadcast([P, 2]), ALU.pow))

            def four_tiles(last, added):
                for pair in range(MQ // 2):
                    pool.wait_ge(s["m_v"], 1)
                    pool.sem_inc(s["m_v"], -1)
                    inverse_std(yr, ymv, pair)
                    pool.sem_inc(s["m_r"], 1)
                link(nc.gpsimd.tensor_copy(token[:], wtok[:, :, 1]))
                if not last:
                    for u in range(MQ):
                        add_bias(u)
                for pair in range(MQ // 2):
                    tiles = (2 * pair, 2 * pair + 1)
                    pool.wait_ge(s["m_n"], 1)
                    pool.sem_inc(s["m_n"], -1)
                    inverse_std(zr, zmv, pair, added)
                    two = slice(2 * pair, 2 * pair + 2)
                    link(nc.gpsimd.tensor_scalar(znm[:, two], zmv[:, two, 0], -1.0, None, ALU.mult))
                    link(nc.gpsimd.tensor_tensor(znm[:, two], znm[:, two], zr[:, two], ALU.mult))
                    link(nc.gpsimd.tensor_copy(toki[:, tiles[0]:tiles[1] + 1], token[:, tiles[0]:tiles[1] + 1]))
                    for u in tiles:
                        link(nc.gpsimd.tensor_scalar(z[u], ya[u], zr[:, u:u + 1], znm[:, u:u + 1], ALU.mult, ALU.add))
                        pool.sem_inc(s["m_ya_free"], 1)
                        nc.gpsimd.indirect_dma_start(
                            out_rows, bass.IndirectOffsetOnAxis(ap=toki[:, u:u + 1].bitcast(U32), axis=0), z[u], None,
                            bounds_check=ROWS - 1, oob_is_err=False, compute_op=ALU.add).then_inc(m_add[pair], 16)
                link.restart()

            for u in range(MQ):
                add_bias(u)
            four_tiles(False, None)
            with pool.Fori(0, NM // MQ - 2) as q:
                four_tiles(False, q * 32 + 32)
            four_tiles(True, (NM // MQ - 1) * 32)
            for pair in range(MQ // 2):
                pool.wait_ge(m_add[pair], NM // MQ * 32)

        @block.vector
        def _(dve):
            link = Chain(dve, dve_step)
            v = nc.vector
            turns = (slice(0, G // 2), slice(G // 2, G))

            def rsqrt(r, var, t):
                link(v.tensor_scalar(r.bitcast(I32), var.bitcast(I32), -0.5, RSQRT_GUESS, ALU.mult, ALU.add))
                for _ in range(3):
                    link(v.tensor_tensor(t, r, r, ALU.mult))
                    link(v.scalar_tensor_tensor(t, t, -0.5, var, ALU.mult, ALU.mult))
                    link(v.scalar_tensor_tensor(r, t, 1.5, r, ALU.add, ALU.mult))

            def token_stats(src, tb):
                link(v.bn_stats(stats[:, tb, :], src[:, tb, :]))
                link(v.bn_aggr(mv[:, tb, :], stats[:, tb, :]))

            def token_norm(r, nm, ready):
                link(v.tensor_scalar(ve[:], mv[:, :, 1], 1e-5, None, ALU.add))
                rsqrt(r[:], ve[:], nt1[:])
                link(v.scalar_tensor_tensor(nm[:], mv[:, :, 0], -1.0, r[:], ALU.mult, ALU.mult))
                dve.sem_inc(ready, 1)

            def next_tokens_norm():
                dve.wait_ge(s["x_loaded"], 16 * BL)
                dve.sem_inc(s["x_loaded"], -(16 * BL))
                for tb in range(TB):
                    token_stats(xt, tb)
                token_norm(x_rstd, x_nmr, s["x_norm_ready"])

            def decay_products(c):
                dve.wait_ge(s["kkq_full"], 1)
                dve.sem_inc(s["kkq_full"], -1)
                link(v.tensor_tensor(A[c][:], kkq[:], dec[:, :, c * C:(c + 1) * C].unsqueeze(2).to_broadcast([P, G, 2, C]), ALU.mult))
                dve.sem_inc(s["kkq_free"], 1)
                dve.sem_inc(s["A_ready"], 1)

            def solve_half(c, j):
                h = slice(j * CS, (j + 1) * CS)
                th = slice(c * C + j * CS, c * C + (j + 1) * CS)
                for g in turns:
                    link(v.tensor_tensor(Ut[:, g], vT[:, g, th], uk[:, g, h], ALU.subtract), behind=1)
                for g in turns:
                    link(v.tensor_tensor(U[:, g, h], Ut[:, g], beta[:, g, th], ALU.mult), behind=1)
                dve.wait_ge(s["pr_ready"], 1)
                dve.sem_inc(s["pr_ready"], -1)
                if (c, j) == (NC - 1, 1):
                    dve.wait_ge(dve_step, link.n)
                    dve.sem_inc(s["vb_free"], 1)
                for t0 in range(CS - 1):
                    n, at = WID[t0], j * CS + t0
                    pr = pairs[j][:, OFF[t0]:OFF[t0] + G * n].rearrange("p (g t) -> p g t", g=G)
                    for g in turns:
                        link(v.tensor_tensor(Ut[:, g, 0:n], pr[:, g], U[:, g, at:at + 1].to_broadcast([P, G // 2, n]),
                                             ALU.mult), behind=1)
                    for g in turns:
                        link(v.tensor_tensor(U[:, g, at + 1:at + 1 + n], U[:, g, at + 1:at + 1 + n], Ut[:, g, 0:n],
                                             ALU.subtract), behind=1)
                dve.wait_ge(dve_step, link.n)
                dve.sem_inc(s["pairs_free"], 1)
                link(v.transpose(delT[c][:], U[:]))
                dve.sem_inc(s["delT_ready"], 1)

            def add_to_state():
                dve.wait_ge(s["su_full"], 1)
                dve.sem_inc(s["su_full"], -1)
                dve.wait_ge(s["Sd_ready"], 1)
                dve.sem_inc(s["Sd_ready"], -1)
                link(v.tensor_tensor(S[:], Sd[:], su[:], ALU.add))
                dve.sem_inc(s["S_ready"], 1)
                dve.sem_inc(s["S_ready_p"], 1)

            def scale(n):
                j, hp = divmod(n, 2)
                dve.wait_ge(s["q_r_ready"], 1)
                dve.sem_inc(s["q_r_ready"], -1)
                link(v.tensor_tensor(unit(kq, hp)[:, :, :, 1 - j, :], per_chunk(qraw[n % 2][:]), per_chunk(qr[n % 2][:]), ALU.mult))
                dve.sem_inc(s["qraw_free"], 1)
                dve.sem_inc(s["kq_ready_pe"], 1)
                dve.sem_inc(s["kq_ready_p"], 1)

            def alpha_argument():
                dve.wait_ge(s["alpha_full"], 1)
                dve.sem_inc(s["alpha_full"], -1)
                link(v.tensor_tensor(alog[:, 0, :].rearrange("p (b h) -> p b h", b=TB),
                                     bank("alpha")[:, 0:TB * H].rearrange("p (b h) -> p b h", b=TB),
                                     dtb[:].unsqueeze(1).to_broadcast([P, TB, H]), ALU.add))
                dve.sem_inc(bank_free("alpha"), 1)
                link(v.scalar_tensor_tensor(alog[:, 1, :], alog[:, 0, :], -1.0, alog[:, 0, :], ALU.mult, ALU.max))
                dve.sem_inc(s["la_e_ready"], 1)

            def log_alpha():
                dve.wait_ge(s["la_l_ready"], 1)
                dve.sem_inc(s["la_l_ready"], -1)
                link(v.scalar_tensor_tensor(alog[:, 1, :], alog[:, 0, :], 0.0, alog[:, 3, :], ALU.max, ALU.add))
                link(v.tensor_tensor(la[:], alog[:, 1, :].rearrange("p (b h) -> p b h", b=TB),
                                     neg_a[:].unsqueeze(1).to_broadcast([P, TB, H]), ALU.mult))
                dve.sem_inc(s["la_ready"], 1)

            def normed_outputs(hp):
                dve.wait_ge(s["o_r_ready"], 1)
                dve.sem_inc(s["o_r_ready"], -1)
                link(v.scalar_tensor_tensor(flat(unit(ctxT, hp)), flat(unit(oT, hp)), nw[:], qr[hp][:], ALU.mult, ALU.mult))
                dve.sem_inc(s["ctx_raw"], 1)
                dve.sem_inc(s["o_copied"], 1)

            def choose_columns():
                dve.wait_ge(s["logits_full"], 1)
                dve.sem_inc(s["logits_full"], -1)
                lw = bank("logits")[:, 0:2 * TB * E].rearrange("p (b a e) -> p b a e", b=TB, a=2)
                link(v.tensor_tensor(lt[:, 1], lw[:, :, 1, :], gb2_sb[:].unsqueeze(1).to_broadcast([P, TB, E]), ALU.add))
                dve.sem_inc(s["lg_ready"], 1)
                link(v.tensor_tensor(lt[:, 0], lw[:, :, 0, :], rstd[:].unsqueeze(2).to_broadcast([P, TB, E]), ALU.mult))
                dve.sem_inc(bank_free("logits"), 1)
                dve.wait_ge(s["sig_ready"], 1)
                dve.sem_inc(s["sig_ready"], -1)
                link(v.tensor_scalar(lt[:, 1], lt[:, 1], 0.5, 0.5, ALU.mult, ALU.add))
                link(v.tensor_tensor(lt[:, 0], lt[:, 0], lt[:, 1], ALU.add))
                link(v.tensor_reduce(l1[:, 0, :], lt[:, 0], AX.X, ALU.max))
                link(v.tensor_tensor(lt[:, 2], lt[:, 0], l1[:, 0, :].unsqueeze(2).to_broadcast([P, TB, E]), ALU.subtract))
                dve.sem_inc(s["d_ready"], 1)
                link(v.tensor_scalar(lt[:, 4], lt[:, 2], 0.0, -float(E), ALU.is_ge, ALU.mult))
                link(v.tensor_tensor(lt[:, 4], lt[:, 4], iota[:].unsqueeze(1).to_broadcast([P, TB, E]), ALU.add))
                link(v.tensor_reduce(l1[:, 1, :], lt[:, 4], AX.X, ALU.min))
                link(v.tensor_tensor(oh[:], lt[:, 4], l1[:, 1, :].unsqueeze(2).to_broadcast([P, TB, E]), ALU.is_equal))
                dve.sem_inc(s["oh_ready"], 1)
                dve.wait_ge(s["e_ready"], 1)
                dve.sem_inc(s["e_ready"], -1)
                link(v.tensor_reduce(l1[:, 2, :], lt[:, 3], AX.X, ALU.add))
                link(v.reciprocal(xfw[:, :, D], l1[:, 2, :]))
                link(v.tensor_copy(xfw[:, :, D + 1], tokf[:]))
                link(v.tensor_scalar(tokf[:], tokf[:], float(T), None, ALU.add))
                link(v.memset(xfw[:, :, D + 2:XSW], 0.0))

            def rows_of_tokens():
                dve.wait_ge(s["rank_full"], 1)
                dve.sem_inc(s["rank_full"], -1)
                w = bank("rank")
                link(v.tensor_tensor(lt[:, 5], w[:, 0:TB * E].rearrange("p (b e) -> p b e", b=TB),
                                     base[:].unsqueeze(1).to_broadcast([P, TB, E]), ALU.add))
                link(v.tensor_tensor(base[:], base[:], w[:, TB * E:(TB + 1) * E], ALU.add))
                dve.sem_inc(bank_free("rank"), 1)
                link(v.tensor_tensor(lt[:, 5], lt[:, 5], col[:, 1, :].unsqueeze(1).to_broadcast([P, TB, E]), ALU.mult))
                link(v.tensor_tensor(lt[:, 5], lt[:, 5], col[:, 0, :].unsqueeze(1).to_broadcast([P, TB, E]), ALU.add))
                link(v.tensor_tensor(lt[:, 5], lt[:, 5], oh[:], ALU.mult))
                link(v.tensor_reduce(slotf[:], lt[:, 5], AX.X, ALU.add))
                link(v.tensor_copy(slot[:], slotf[:]))
                dve.sem_inc(s["slot_ready"], 1)

            def step(p, chain, after, ahead):
                if chain:
                    dve.wait_ge(s["vb_ready"], 1)
                    dve.sem_inc(s["vb_ready"], -1)
                    dve.wait_ge(s["uk_full"], 1)
                    dve.sem_inc(s["uk_full"], -1)
                    solve_half(0, 0)
                    for c in range(NC):
                        link(v.transpose(kd[c][:], kq[:, :, c, 0, :]))
                    dve.sem_inc(s["kt_ready"], 1)
                    decay_products(1)
                if ahead:
                    alpha_argument()
                if after:
                    for hp in range(2):
                        normed_outputs(hp)
                if ahead:
                    log_alpha()
                if chain:
                    dve.wait_ge(s["corr_full"], 1)
                    dve.sem_inc(s["corr_full"], -1)
                    solve_half(0, 1)
                if ahead:
                    if chain:
                        dve.wait_ge(s["kq_free"], 1)
                        dve.sem_inc(s["kq_free"], -1)
                    scale(0)
                if after:
                    for tb in range(TB):
                        dve.wait_ge(s["wo_full"], 1)
                        dve.sem_inc(s["wo_full"], -1)
                        link(v.tensor_tensor(y[:, tb, :], bank("wo", tb), bo_sb[:], ALU.add))
                        dve.sem_inc(bank_free("wo", tb), 1)
                        token_stats(y, tb)
                    token_norm(rstd, nmr, s["norm_ready"])
                if ahead:
                    scale(1)
                if chain:
                    add_to_state()
                if ahead:
                    for hp in range(2):
                        dve.wait_ge(s["g_copied"], 1)
                        dve.sem_inc(s["g_copied"], -1)
                        link(v.transpose(gT[hp], gsb[hp]))
                        dve.sem_inc(s["gT_ready"], 1)
                if chain:
                    dve.wait_ge(s["uk_full"], 1)
                    dve.sem_inc(s["uk_full"], -1)
                    solve_half(1, 0)
                if after:
                    dve.wait_ge(s["y_ready"], 1)
                    dve.sem_inc(s["y_ready"], -1)
                    for tb in range(TB):
                        token_stats(x1, tb)
                    token_norm(rstd, nmr, s["norm_ready"])
                if ahead:
                    scale(2)
                    scale(3)
                    for hp in range(2):
                        dve.wait_ge(s["gate_ready"], 1)
                        dve.sem_inc(s["gate_ready"], -1)
                        link(v.tensor_tensor(flat(unit(silu[1 - p], hp)), bank("gate", hp), sg[:], ALU.mult))
                        dve.sem_inc(bank_free("gate", hp), 1)
                        dve.sem_inc(s["sg_free"], 1)
                if chain:
                    dve.wait_ge(s["corr_full"], 1)
                    dve.sem_inc(s["corr_full"], -1)
                    solve_half(1, 1)
                if ahead:
                    dve.wait_ge(s["dec_ready"], 2)
                    dve.sem_inc(s["dec_ready"], -2)
                    decay_products(0)
                    next_tokens_norm()
                if after:
                    dve.wait_ge(s["ss_ready"], 1)
                    dve.sem_inc(s["ss_ready"], -1)
                    link(v.tensor_scalar(ve[:], ssq[:], 1e-24, None, ALU.max))
                    rsqrt(rstd[:], ve[:], nt1[:])
                    choose_columns()
                    rows_of_tokens()
                if chain:
                    add_to_state()
                link.restart()

            dve.wait_ge(loaded, ALL)
            link(v.memset(U[:], 0.0))
            link(v.memset(eps6[:], 1e-6))
            link(v.memset(lnq[:], -0.5 * math.log(DH)))
            dve.sem_inc(s["setup_v"], 1)
            dve.wait_ge(s["setup_a"], 1)
            dve.sem_inc(s["setup_a"], -1)
            link(v.tensor_scalar(neg_a[:], neg_a[:], -1.0, None, ALU.mult))
            dve.wait_ge(s["ce_sq"], 1)
            dve.sem_inc(s["ce_sq"], -1)
            link(v.tensor_scalar(ce_s[:, 1:2], ce_s[:, 0:1], 1e-24, None, ALU.max))
            rsqrt(ce_s[:, 2:3], ce_s[:, 1:2], ce_s[:, 3:4])
            link(v.tensor_scalar(ce, ce, ce_s[:, 2:3], None, ALU.mult))
            dve.sem_inc(s["ce_n"], 1)
            dve.wait_ge(s["ce_T"], 1)
            dve.sem_inc(s["ce_T"], -1)
            link(v.tensor_copy(ceT[:].rearrange("p k e -> p (k e)"), work[0][:, 0:KD * E]))
            dve.wait_ge(s["base_ready"], 1)
            dve.sem_inc(s["base_ready"], -1)
            link(v.tensor_copy(tokf[:], tok0[:]))
            next_tokens_norm()
            link.restart()
            step(1, False, False, True)
            step(0, True, False, True)
            with dve.Fori(0, NT // 2 - 1):
                step(1, True, True, True)
                step(0, True, True, True)
            step(1, True, True, False)
            step(0, False, True, False)
            link(v.tensor_tensor(tb[:, 2, :], base[:], col[:, 1, :], ALU.mult))
            link(v.tensor_tensor(cnt, tb[:, 2, :], col[:, 2, :], ALU.add))
            dve.sem_inc(s["cnt_ready"], 1)
            full = ROWS // P
            link(v.tensor_scalar(tabf[:, 0, :], krow[:], float(P), None, ALU.mult))
            link(v.tensor_tensor(tb2[:, :, 0:full], base[:].unsqueeze(2).to_broadcast([P, E, full]),
                                 tabf[:, 0, 0:full].unsqueeze(1).to_broadcast([P, E, full]), ALU.is_gt))
            link(v.tensor_reduce(tb[:, 0, :], tb2[:, :, 0:full], AX.X, ALU.add))
            link(v.tensor_copy(tb[:, 1, :], tb[:, 0, :]))
            for e in range(1, E):
                link(v.tensor_tensor(tb[:, 1, e:e + 1], tb[:, 1, e:e + 1], tb[:, 1, e - 1:e], ALU.add))
            link(v.tensor_tensor(tb2[:, :, 0:NM], tb[:, 1, :].unsqueeze(2).to_broadcast([P, E, NM]),
                                 krow[:, 0:NM].unsqueeze(1).to_broadcast([P, E, NM]), ALU.is_le))
            link(v.tensor_reduce(tabf[:, 1, 0:NM], tb2[:, :, 0:NM].rearrange("p e m -> p m e"), AX.X, ALU.add))
            for n, step in ((2, tb[:, 0, :]), (3, col[:, 3, :]), (4, col[:, 4, :])):
                link(v.tensor_tensor(tb3[:, :, 0:NM], tb2[:, :, 0:NM], step.unsqueeze(2).to_broadcast([P, E, NM]), ALU.mult))
                link(v.tensor_reduce(tabf[:, n, 0:NM], tb3[:, :, 0:NM].rearrange("p e m -> p m e"), AX.X, ALU.add))
            link(v.tensor_tensor(tabf[:, 2, 0:NM], krow[:, 0:NM], tabf[:, 2, 0:NM], ALU.subtract))
            link(v.tensor_scalar(tabf[:, 4, 0:NM], tabf[:, 4, 0:NM], 1.0, float(P), ALU.add, ALU.mult))
            link(v.tensor_tensor(tabf[:, 4, 0:NM], tabf[:, 4, 0:NM], tabf[:, 2, 0:NM], ALU.mult))
            link(v.tensor_tensor(tab[:, 1, 0:NM], tabf[:, 3, 0:NM], tabf[:, 4, 0:NM], ALU.add))
            link(v.tensor_scalar(tab[:, 0, 0:NM], tabf[:, 1, 0:NM], float(E - 1), None, ALU.min))
            dve.sem_inc(s["table_ready"], 1)
            for n, free in (("m_free", MQ), ("m_t_done", MQ), ("m_ya_free", MQ), ("m_wfree", MQ), ("m_t_free", 2), ("m_h_free", 2), ("m_y_free", 2)):
                dve.sem_inc(s[n], free)
            link.restart()
            with dve.Fori(0, NM // MQ):
                def row_stats(mv, tiles):
                    for u in tiles:
                        link(v.bn_stats(mst[:, u % 2], ya[u]), behind=1)
                    for u in tiles:
                        link(v.bn_aggr(mv[:, u], mst[:, u % 2]), behind=1)

                for pair in range(MQ // 2):
                    tiles = (2 * pair, 2 * pair + 1)
                    for u in tiles:
                        dve.wait_ge(s["m_xsb"], 1)
                        dve.sem_inc(s["m_xsb"], -1)
                        dve.wait_ge(s["m_y"], 1)
                        dve.sem_inc(s["m_y"], -1)
                        dve.sem_inc(s["m_wfree"], 1)
                        dve.wait_ge(s["m_ya_free"], 1)
                        dve.sem_inc(s["m_ya_free"], -1)
                        link(v.scalar_tensor_tensor(ya[u], m_yp[u % 2], wtok[:, u, 0:1], xs[u][:, 0:D] if pair else xsb[u],
                                                    ALU.mult, ALU.add))
                        dve.sem_inc(s["m_y_free"], 1)
                        if pair:
                            dve.sem_inc(s["m_free"], 1)
                    if pair:
                        for u in tiles:
                            link(v.tensor_tensor(ya[u], ya[u], pb_sb, ALU.add), behind=1)
                    row_stats(ymv, tiles)
                    dve.wait_ge(dve_step, link.n)
                    dve.sem_inc(s["m_v"], 1)
                for pair in range(MQ // 2):
                    tiles = (2 * pair, 2 * pair + 1)
                    dve.wait_ge(s["m_r"], 1)
                    dve.sem_inc(s["m_r"], -1)
                    for u in tiles:
                        link(v.scalar_tensor_tensor(ya[u], ya[u], ymv[:, u, 0:1], lg_sb, ALU.subtract, ALU.mult), behind=1)
                    for u in tiles:
                        link(v.scalar_tensor_tensor(ya[u], ya[u], yr[:, u:u + 1], lb_sb, ALU.mult, ALU.add), behind=1)
                    row_stats(zmv, tiles)
                    dve.wait_ge(dve_step, link.n)
                    dve.sem_inc(s["m_n"], 1)
                link.restart()


def column_rows():
    import numpy as np
    e = np.arange(E)
    front, sign = e // 2 * SHARE, 1 - 2 * (e % 2)
    first = np.where(e % 2, front + SHARE - 1, front)
    behind = np.where(e % 2, first + 1 - P, first)
    return np.stack([first, sign, behind, np.diff(behind, append=PADROW), np.diff(sign, append=0)])


def constants():
    import numpy as np
    p = np.arange(P)
    same = (p[:, None] // DH) == (p[None, :] // DH)
    squares = np.stack([np.eye(P), same, same & (p[:, None] <= p[None, :]), p[:, None] < p[None, :],
                        np.ones((P, P))], axis=1)
    sel = same[:, None, :] & ((p % DH)[:, None] == np.arange(C)[None, :])[:, :, None]
    mask = np.where(np.arange(C)[None, :] >= (p % DH)[:, None], 0.0, NEG)
    iota = np.broadcast_to(np.arange(E), (P, E))
    pad = np.zeros((P, XSW))
    pad[:, D + 1] = 2 * ROWS
    tok = (np.arange(TB)[None, :] * BL + p[:, None] // T) * L + p[:, None] % T
    row = np.broadcast_to(p, (P, P))
    col = np.broadcast_to(column_rows(), (P, 5, E))
    return {n: np.ascontiguousarray(a, dtype=np.float32) for n, a in
            dict(c_sq=squares, c_sel=sel, c_mask=mask, c_iota=iota, c_pad=pad, c_tok=tok, c_row=row, c_col=col).items()}


def kernel(**inputs):
    import numpy as np
    import concourse.bacc as bacc
    from concourse.bass_utils import run_bass_kernel_spmd as run

    a = {n[3:]: np.asarray(v) for n, v in inputs.items()}
    laid = {
        "x": a["attn_x"],
        "w_in": np.concatenate([a[f"attn_W{n}"].T for n in "qkvbg"], axis=1),
        "wa": a["attn_Wa"].T, "dt_bias": a["attn_dt_bias"], "a_log": a["attn_A_log"], "norm_w": a["attn_norm_w"],
        "wo": a["attn_Wo"].T, "bo": a["attn_bo"], "col_emb": a["ffn_col_emb"],
        "gw1": a["ffn_gate_w1"], "gb1": a["ffn_gate_b1"].reshape(HID // P, P).T, "gw2": a["ffn_gate_w2"], "gb2": a["ffn_gate_b2"],
        "w_cols": a["ffn_W_cols"], "b_cols": a["ffn_b_cols"][:, :, None], "proj_w": a["ffn_proj_w"].reshape(E, N, D),
        "proj_b": a["ffn_proj_b"], "ln_g": a["ffn_ln_g"], "ln_b": a["ffn_ln_b"], **constants(),
    }
    nc = bacc.Bacc("TRN2", target_bir_lowering=False, num_devices=1)
    arrays, args = {}, {}
    for name, v in laid.items():
        arrays[f"in_{name}"] = v = np.ascontiguousarray(v)
        args[name] = nc.dram_tensor(f"in_{name}", v.shape, mybir.dt.from_np(v.dtype), kind="ExternalInput").ap()
    out = nc.dram_tensor("out", (B, L, D), F32, kind="ExternalOutput").ap()
    xs_dram = nc.dram_tensor("xs_rows", (PADROW + P, XSW), F32, kind="Internal").ap()
    sandwich_kernel(nc, out=out, xs_dram=xs_dram, **args)
    return run(nc, [arrays], core_ids=[0]).results[0]["out"]
```
